# Optimizing a Trainium2 kernel written in Bass

```python
import numpy as np
import jax
import jax.numpy as jnp

def _softmax(x, axis=-1):
    return jax.nn.softmax(x, axis=axis)

def _gelu(x):
    return jax.nn.gelu(x, approximate=True)

def _silu(x):
    return jax.nn.silu(x)

def _sigmoid(x):
    return jax.nn.sigmoid(x)

def _layernorm(x, axis=-1, eps=1e-05):
    m = jnp.mean(x, axis=axis, keepdims=True)
    v = jnp.var(x, axis=axis, keepdims=True)
    return (x - m) / jnp.sqrt(v + eps)

def _scatter_add(tgt, idx, src, axis=0):
    return tgt.at[idx].add(src)

def _segment_sum(src, seg, n):
    return jax.ops.segment_sum(src, seg, n)
kernel_name = 'mk_gnn_resnorm_d4_gnn_r32_be42ed'

def setup_inputs(seed: int=0):
    np.random.seed(seed)
    _w = jnp.asarray

    def _rec_inputs():
        import jax
        import jax.numpy as jnp
        _gk = jax.random.key(seed)
        x = -0.000202 + 1 * jax.random.normal(jax.random.fold_in(_gk, 1), (50000, 128), jnp.float32)
        src = jax.random.randint(jax.random.fold_in(_gk, 2), (25000,), 0, 50000, jnp.int32)
        dst = jnp.minimum((50000 * jax.random.uniform(jax.random.fold_in(_gk, 3), (25000,)) ** 2.0).astype(jnp.int32), 49999)
        _o = jnp.argsort(dst, stable=True)
        src = src[_o]
        dst = dst[_o]
        edge_attr_128 = -5.16925e-05 + 1.00005 * jax.random.normal(jax.random.fold_in(_gk, 12), (25000, 128), jnp.float32)
        edge_type_8 = jax.random.randint(jax.random.fold_in(_gk, 14), (25000,), 0, 8, jnp.int32)
        edge_weight = -0.00126848 + 0.999356 * jax.random.normal(jax.random.fold_in(_gk, 15), (25000,), jnp.float32)
        return (x, src, dst, edge_attr_128, edge_type_8, edge_weight)
    x, src, dst, edge_attr_128, edge_type_8, edge_weight = _rec_inputs()

    def _L0_gnn_setup():
        import jax, jax.numpy as jnp
        import numpy as np
        N_NODES = 50000

        def _gin_conv(x, src, dst, wa, ba, wb, bb):
            agg = jax.ops.segment_sum(x[src], dst, num_segments=N_NODES)
            h = x + agg
            h = jnp.maximum(h @ wa + ba, 0.0)
            return h @ wb + bb
        key = jax.random.key(seed)
        ks = jax.random.split(key, 8)
        E = 15625
        d_in, d_h, d_out, d_lat = (128, 64, 256, 128)
        x = jax.random.normal(ks[0], (N_NODES, d_in), dtype=jnp.float32)
        edge_index = jax.random.randint(ks[1], (2, E), 0, N_NODES, dtype=jnp.int64)
        edge_attr = jax.random.normal(ks[2], (E,), dtype=jnp.float32)

        def glorot(k, shape):
            fan_in, fan_out = shape
            lim = (6.0 / (fan_in + fan_out)) ** 0.5
            return jax.random.uniform(k, shape, jnp.float32, -lim, lim)
        return {'x': x, 'edge_index': edge_index, 'edge_attr': edge_attr, 'w1a': glorot(ks[3], (d_in, d_h)), 'b1a': jnp.zeros((d_h,), jnp.float32), 'w1b': glorot(ks[4], (d_h, d_h)), 'b1b': jnp.zeros((d_h,), jnp.float32), 'w2a': glorot(ks[5], (d_h, d_out)), 'b2a': jnp.zeros((d_out,), jnp.float32), 'w2b': glorot(ks[6], (d_out, d_out)), 'b2b': jnp.zeros((d_out,), jnp.float32), 'wl': glorot(ks[7], (d_out, d_lat)), 'bl': jnp.zeros((d_lat,), jnp.float32)}
    _L0_gnn_all = _L0_gnn_setup()
    _L0_gnn_in = {k: v for k, v in _L0_gnn_all.items() if k in ('w1a', 'b1a', 'w1b', 'b1b', 'w2a', 'b2a', 'w2b', 'b2b', 'wl', 'bl')}
    del _L0_gnn_all

    def _L1_gnn_setup():
        import jax, jax.numpy as jnp
        import numpy as np
        N_NODES = 50000
        N_EDGES = 25000
        N_RELS = 8
        N_BASES = 4
        IN_FEAT = 128
        OUT_FEAT = 128
        key = jax.random.key(seed)
        k = jax.random.split(key, 7)
        x = jax.random.normal(k[0], (N_NODES, IN_FEAT), dtype=jnp.float32)
        edge_norm = jax.random.uniform(k[1], (N_EDGES,), dtype=jnp.float32)
        bases = jax.random.normal(k[2], (N_BASES, IN_FEAT, OUT_FEAT), dtype=jnp.float32) * 0.05
        w_comp = jax.random.normal(k[3], (N_RELS, N_BASES), dtype=jnp.float32)
        edge_src = jax.random.randint(k[4], (N_EDGES,), 0, N_NODES, dtype=jnp.int32)
        edge_dst = jax.random.randint(k[5], (N_EDGES,), 0, N_NODES, dtype=jnp.int32)
        edge_type = jax.random.randint(k[6], (N_EDGES,), 0, N_RELS, dtype=jnp.int32)
        return {'x': x, 'edge_norm': edge_norm, 'bases': bases, 'w_comp': w_comp, 'edge_src': edge_src, 'edge_dst': edge_dst, 'edge_type': edge_type}
    _L1_gnn_all = _L1_gnn_setup()
    _L1_gnn_in = {k: v for k, v in _L1_gnn_all.items() if k in ('bases', 'w_comp')}
    del _L1_gnn_all

    def _L2_gnn_setup():
        import jax, jax.numpy as jnp
        import numpy as np
        N_NODES = 10000
        N_EDGES = 20000
        D_IN = 128
        D_OUT = 128
        key = jax.random.key(seed)
        k1, k2, k3 = jax.random.split(key, 3)
        x = jax.random.normal(k1, (N_NODES, D_IN), dtype=jnp.float32)
        W = jax.random.normal(k2, (D_OUT, D_IN), dtype=jnp.float32) * (1.0 / np.sqrt(D_IN))
        bias = jnp.zeros((D_OUT,), dtype=jnp.float32)
        edge_index = jax.random.randint(k3, (2, N_EDGES), 0, N_NODES, dtype=jnp.int64)
        return {'x': x, 'W': W, 'bias': bias, 'edge_index': edge_index}
    _L2_gnn_all = _L2_gnn_setup()
    _L2_gnn_in = {k: v for k, v in _L2_gnn_all.items() if k in ('W', 'bias')}
    del _L2_gnn_all

    def _L3_gnn_setup():
        import jax, jax.numpy as jnp
        import numpy as np
        N = 50000
        E = 25000
        D = 128
        DE = 128
        L = 3
        key = jax.random.key(seed)
        ks = jax.random.split(key, 10)
        s = 0.05
        return dict(x=jax.random.normal(ks[0], (N, D), jnp.float32), edge_index=jax.random.randint(ks[1], (2, E), 0, N, jnp.int32), edge_attr=jax.random.normal(ks[2], (E, DE), jnp.float32), W=jax.random.normal(ks[3], (L, D, D), jnp.float32) * s, att_src=jax.random.normal(ks[4], (L, D), jnp.float32) * s, att_dst=jax.random.normal(ks[5], (L, D), jnp.float32) * s, W_e=jax.random.normal(ks[6], (L, DE, D), jnp.float32) * s, att_edge=jax.random.normal(ks[7], (L, D), jnp.float32) * s, bias=jnp.zeros((L, D), jnp.float32), ln_gamma=jnp.ones((L, D), jnp.float32), ln_beta=jnp.zeros((L, D), jnp.float32))
    _L3_gnn_all = _L3_gnn_setup()
    _L3_gnn_in = {k: v for k, v in _L3_gnn_all.items() if k in ('W', 'att_src', 'att_dst', 'W_e', 'att_edge', 'bias', 'ln_gamma', 'ln_beta')}
    del _L3_gnn_all
    return {'x': x, 'src': src, 'dst': dst, 'edge_attr_128': edge_attr_128, 'edge_type_8': edge_type_8, 'edge_weight': edge_weight, 'L0_gnn_w1a': _L0_gnn_in['w1a'], 'L0_gnn_b1a': _L0_gnn_in['b1a'], 'L0_gnn_w1b': _L0_gnn_in['w1b'], 'L0_gnn_b1b': _L0_gnn_in['b1b'], 'L0_gnn_w2a': _L0_gnn_in['w2a'], 'L0_gnn_b2a': _L0_gnn_in['b2a'], 'L0_gnn_w2b': _L0_gnn_in['w2b'], 'L0_gnn_b2b': _L0_gnn_in['b2b'], 'L0_gnn_wl': _L0_gnn_in['wl'], 'L0_gnn_bl': _L0_gnn_in['bl'], 'L1_gnn_bases': _L1_gnn_in['bases'], 'L1_gnn_w_comp': _L1_gnn_in['w_comp'], 'L2_gnn_W': _L2_gnn_in['W'], 'L2_gnn_bias': _L2_gnn_in['bias'], 'L3_gnn_W': _L3_gnn_in['W'], 'L3_gnn_att_src': _L3_gnn_in['att_src'], 'L3_gnn_att_dst': _L3_gnn_in['att_dst'], 'L3_gnn_W_e': _L3_gnn_in['W_e'], 'L3_gnn_att_edge': _L3_gnn_in['att_edge'], 'L3_gnn_bias': _L3_gnn_in['bias'], 'L3_gnn_ln_gamma': _L3_gnn_in['ln_gamma'], 'L3_gnn_ln_beta': _L3_gnn_in['ln_beta']}

def reference(x, src, dst, edge_attr_128, edge_type_8, edge_weight, L0_gnn_w1a, L0_gnn_b1a, L0_gnn_w1b, L0_gnn_b1b, L0_gnn_w2a, L0_gnn_b2a, L0_gnn_w2b, L0_gnn_b2b, L0_gnn_wl, L0_gnn_bl, L1_gnn_bases, L1_gnn_w_comp, L2_gnn_W, L2_gnn_bias, L3_gnn_W, L3_gnn_att_src, L3_gnn_att_dst, L3_gnn_W_e, L3_gnn_att_edge, L3_gnn_bias, L3_gnn_ln_gamma, L3_gnn_ln_beta):
    import jax
    import jax.numpy as jnp

    def _L0_gnn_ref(x, edge_index, edge_attr, w1a, b1a, w1b, b1b, w2a, b2a, w2b, b2b, wl, bl):
        import jax, jax.numpy as jnp
        import numpy as np
        N_NODES = 50000

        def _gin_conv(x, src, dst, wa, ba, wb, bb):
            agg = jax.ops.segment_sum(x[src], dst, num_segments=N_NODES)
            h = x + agg
            h = jnp.maximum(h @ wa + ba, 0.0)
            return h @ wb + bb
        src, dst = (edge_index[0], edge_index[1])
        h = _gin_conv(x, src, dst, w1a, b1a, w1b, b1b)
        h = jnp.maximum(h, 0.0)
        h = _gin_conv(h, src, dst, w2a, b2a, w2b, b2b)
        return h @ wl + bl

    def _L1_gnn_ref(x, edge_norm, bases, w_comp, edge_src, edge_dst, edge_type):
        import jax, jax.numpy as jnp
        import numpy as np
        N_NODES = 50000
        N_EDGES = 25000
        N_RELS = 8
        N_BASES = 4
        IN_FEAT = 128
        OUT_FEAT = 128
        N = x.shape[0]
        R = w_comp.shape[0]
        W = jnp.einsum('rb,bio->rio', w_comp, bases)
        msg = x[edge_src] * edge_norm[:, None]
        seg = edge_type * N + edge_dst
        agg = jax.ops.segment_sum(msg, seg, num_segments=R * N)
        agg = agg.reshape(R, N, -1)
        out = jnp.einsum('rni,rio->no', agg, W)
        return out

    def _L2_gnn_ref(x, W, bias, edge_index):
        import jax, jax.numpy as jnp
        import numpy as np
        N_NODES = 10000
        N_EDGES = 20000
        D_IN = 128
        D_OUT = 128
        y = x @ W.T
        row, col = (edge_index[0], edge_index[1])
        n = x.shape[0]
        deg = jax.ops.segment_sum(jnp.ones_like(col, dtype=y.dtype), col, num_segments=n)
        deg_inv_sqrt = jnp.where(deg > 0, jax.lax.rsqrt(deg), 0.0)
        norm = deg_inv_sqrt[row] * deg_inv_sqrt[col]
        msg = norm[:, None] * y[row]
        out = jax.ops.segment_sum(msg, col, num_segments=n)
        return out + bias

    def _L3_gnn_ref(x, edge_index, edge_attr, W, att_src, att_dst, W_e, att_edge, bias, ln_gamma, ln_beta):
        import jax, jax.numpy as jnp
        import numpy as np
        N = 50000
        E = 25000
        D = 128
        DE = 128
        L = 3
        n = x.shape[0]
        src, dst = (edge_index[0], edge_index[1])
        ones = jnp.ones((src.shape[0],), x.dtype)
        deg = jax.ops.segment_sum(ones, dst, num_segments=n)
        loop_attr = jax.ops.segment_sum(edge_attr, dst, num_segments=n) / jnp.maximum(deg, 1.0)[:, None]
        loop = jnp.arange(n, dtype=src.dtype)
        src_f = jnp.concatenate([src, loop])
        dst_f = jnp.concatenate([dst, loop])
        ea_f = jnp.concatenate([edge_attr, loop_attr], axis=0)

        def layer(h_in, p):
            Wl, asl, adl, Wel, ael, bl, gl, bel = p
            h = h_in @ Wl
            a = (h @ asl)[src_f] + (h @ adl)[dst_f] + ea_f @ (Wel @ ael)
            a = jnp.where(a > 0, a, 0.2 * a)
            m = jax.ops.segment_max(a, dst_f, num_segments=n)
            ea = jnp.exp(a - m[dst_f])
            denom = jax.ops.segment_sum(ea, dst_f, num_segments=n)
            alpha = ea / denom[dst_f]
            out = jax.ops.segment_sum(h[src_f] * alpha[:, None], dst_f, num_segments=n) + bl
            mu = jnp.mean(out, axis=-1, keepdims=True)
            var = jnp.var(out, axis=-1, keepdims=True)
            out = (out - mu) * jax.lax.rsqrt(var + 1e-05) * gl + bel
            return (out, None)
        h, _ = jax.lax.scan(layer, x, (W, att_src, att_dst, W_e, att_edge, bias, ln_gamma, ln_beta))
        return h
    edge_index = jnp.stack([src, dst])
    x = _layernorm(x + _L0_gnn_ref(x, edge_index, edge_weight, L0_gnn_w1a, L0_gnn_b1a, L0_gnn_w1b, L0_gnn_b1b, L0_gnn_w2a, L0_gnn_b2a, L0_gnn_w2b, L0_gnn_b2b, L0_gnn_wl, L0_gnn_bl), axis=-1)
    x = _layernorm(x + _L1_gnn_ref(x, edge_weight, L1_gnn_bases, L1_gnn_w_comp, src, dst, edge_type_8), axis=-1)
    x = _layernorm(x + _L2_gnn_ref(x, L2_gnn_W, L2_gnn_bias, edge_index), axis=-1)
    x = _layernorm(x + _L3_gnn_ref(x, edge_index, edge_attr_128, L3_gnn_W, L3_gnn_att_src, L3_gnn_att_dst, L3_gnn_W_e, L3_gnn_att_edge, L3_gnn_bias, L3_gnn_ln_gamma, L3_gnn_ln_beta), axis=-1)
    return x

_drawn_inputs = setup_inputs


def setup_inputs(seed=0):
    import zlib

    import numpy as np

    out = dict(_drawn_inputs(seed))
    spreads = {'L0_gnn_b1a': (0.0, 0.334),
     'L0_gnn_b1b': (0.0, 0.1),
     'L0_gnn_b2a': (0.0, 0.1),
     'L0_gnn_b2b': (0.0, 0.1),
     'L0_gnn_bl': (0.0, 0.1),
     'L2_gnn_bias': (0.0, 0.1),
     'L3_gnn_bias': (0.0, 0.1),
     'L3_gnn_ln_gamma': (1.0, 0.2),
     'L3_gnn_ln_beta': (0.0, 0.1)}
    factors = {'edge_attr_128': 3.391,
     'L3_gnn_att_dst': 18.517,
     'L3_gnn_W_e': 3.203,
     'L3_gnn_att_edge': 3.432}
    for name, (base, spread) in spreads.items():
        noise = np.random.default_rng([zlib.crc32(name.encode()), seed]).standard_normal(out[name].shape)
        drawn = base * np.exp(spread * noise) if base else spread * noise
        out[name] = jnp.asarray(drawn.astype(out[name].dtype))
    for name, factor in factors.items():
        out[name] = (out[name] * factor).astype(out[name].dtype)
    return out
```

```python
from contextlib import ExitStack

import numpy as np
import concourse.bass as bass
from concourse import mybir

F32 = mybir.dt.float32
I32 = mybir.dt.int32
ALU = mybir.AluOpType
ACT = mybir.ActivationFunctionType
AXX = mybir.AxisListType.X

N = 50000
E = 25000
D = 128
H = 64
CE = 127
G4 = 4
ROWP = 100
CHUNKS = 2 * ROWP
AG = CHUNKS // G4
SLOTS = 128 * CHUNKS
GN = 128 * G4
DG = -(-N // GN)
NPAD = DG * GN
XW = D + 4
RE = 2 * CE
EPS = 1e-5
FAR = 65535
BIG = 1e30
UN = 4


def steps(eng, count, lag, step):
    full = (count - 1) // UN
    for u in range(UN):
        step(0, u)
    with eng.Fori(1, full) as k:
        for u in range(UN):
            step(k, u)
    for i in range(full * UN, count + lag):
        step(i // UN, i % UN)


def live(k, u, lag, count):
    return not isinstance(k, int) or 0 <= UN * k + u - lag < count


def wait(eng, sem, value):
    if not isinstance(value, int) or value > 0:
        eng.wait_ge(sem, value)


class Chain:

    def __init__(self, eng, sem, per):
        self.eng, self.sem, self.per, self.j = eng, sem, per, per

    def group(self, n):
        assert self.j == self.per
        self.n, self.j = n, 0

    def __call__(self, ins, hold=None):
        self.j += 1
        assert self.j <= self.per
        ins.then_inc(self.sem, 1)
        if hold:
            hold(self.eng, (self.sem, self.n * self.per + self.j))
        else:
            self.eng.wait_ge(self.sem, self.n * self.per + self.j)


class Net:

    def __init__(self, nc, a, out):
        self.nc, self.a, self.out = nc, a, out
        self.n_sems = 0

    def scope(self, phase):
        ctx = ExitStack()
        nc = self.nc

        def sb(name, shape, dt=F32):
            return ctx.enter_context(nc.sbuf_tensor(f"{phase}_{name}", shape, dt))

        def ps(name, shape=(128, 512)):
            return ctx.enter_context(nc.psum_tensor(f"{phase}_{name}", list(shape), F32))

        sems = []

        def sem(name):
            sems.append(nc.alloc_semaphore(name=f"{phase}_{name}"))
            return sems[-1]

        def finish():
            nc.clear_and_free_semaphores(sems)
            nc.all_engine_barrier()

        ctx.callback(finish)
        return ctx, sb, ps, sem

    def allocate(self, ctx):
        nc = self.nc
        self.begun = ctx.enter_context(nc.semaphore("begun"))

        def sb(name, shape, dt=F32):
            return ctx.enter_context(nc.sbuf_tensor(name, shape, dt))

        def dram(name, rows, width, dt=F32):
            return nc.dram_tensor(name, (rows, width), dt, kind="Internal").ap()

        self.ident = sb("ident", [128, 128])
        self.iota = sb("iota", [128, 128])
        self.msgs = sb("msgs", [128, CHUNKS, XW])
        self.slot_id = sb("slot_id", [128, CHUNKS], I32)
        self.q = sb("q", [128, CHUNKS])
        self.src_i = sb("src_i", [128, CHUNKS], I32)
        self.dst_i = sb("dst_i", [128, CHUNKS], I32)
        self.own_i = sb("own_i", [128, CHUNKS], I32)
        self.row_i = sb("row_i", [128, CHUNKS], I32)
        self.row4_i = sb("row4_i", [128, CHUNKS], I32)
        self.coef = sb("coef", [128, 4, CHUNKS])
        self.deg = sb("deg", [128, CHUNKS, 4])
        self.dis = sb("dis", [128, CHUNKS])
        self.att_s = sb("att_s", [128, CHUNKS, 3])
        self.w_edge = sb("w_edge", [128, CHUNKS])
        self.w_self = sb("w_self", [128, CHUNKS])
        self.end = sb("end", [ROWP, 256])
        self.notend = sb("notend", [ROWP, 256])
        self.startneg = sb("startneg", [ROWP, 256])
        self.preneg = sb("preneg", [ROWP, 256])
        self.open = sb("open", [ROWP, 256])
        self.edge_t = sb("edge_t", [ROWP, 3, 256])
        self.flag_rows = sb("flag_rows", [1, 2, ROWP])
        self.w1a = sb("w1a", [D, H]); self.w1b = sb("w1b", [H, H])
        self.b1a = sb("b1a", [H, 1]); self.b1b = sb("b1b", [H, 1])
        self.w2a = sb("w2a", [H, 2 * D]); self.b2a = sb("b2a", [D, 2])
        self.wc = sb("wc", [D, 2, D])
        self.bc = sb("bc", [128, D])
        self.bases = sb("bases", [D, 4, D])
        self.wg = sb("wg", [D, D])
        self.bg = sb("bg", [128, D])
        self.wx = sb("wx", [D, 3, XW])
        self.cx = sb("cx", [128, 3, XW])
        self.bl = sb("bl", [128, 3, D])
        self.gam = sb("gam", [128, D]); self.bet = sb("bet", [128, D])
        self.eps = sb("eps", [128, 1])
        self.ve = sb("ve", [D, 3])
        self.t2 = dram("t_h1", SLOTS + NPAD, H)
        self.t3 = dram("t_x1", SLOTS + NPAD, D)
        self.t4 = dram("t_x2", SLOTS + 128, D)
        self.th = [dram(f"t_gat{l}", SLOTS + NPAD, XW) for l in range(3)]
        self.x3 = dram("t_x3", SLOTS + NPAD, D)
        self.xd = dram("t_xd", SLOTS, D)
        self.x2 = dram("t_x2s", SLOTS, D)
        self.where = dram("t_where", NPAD, 1, I32)
        self.terms = dram("t_terms", 3, E)

    def hold(self, eng, *waits):
        waits = [(sem, v if isinstance(v, int) else eng.to_reg(v)) for sem, v in waits]
        eng.wait_ge(self.begun, 1)
        for sem, value in waits:
            wait(eng, sem, value)

    def slots(self, t, k, u, lag=0):
        v = t[0:SLOTS, :].rearrange("(p c) f -> p c f", p=128)
        return v[:, bass.ds((UN * k + u - lag) * G4, G4), :]

    def nodes(self, t, k, u, lag=0, base=SLOTS):
        v = t[base:base + NPAD, :].rearrange("(g p j) f -> g p j f", p=128, j=G4)
        return v[bass.ds(UN * k + u - lag, 1), :, :, :].rearrange("g p j f -> p (g j) f")

    def phase_weights(self):
        nc, a = self.nc, self.a
        ctx, sb, ps, sem = self.scope("wt")
        with ctx:
            w2b = sb("w2b", [D, 2, 2 * D]); wl = sb("wl", [D, 2, D]); b2b = sb("b2b", [D, 2])
            w2bt = sb("w2bt", [D, 4, D]); wgr = sb("wgr", [D, D])
            asr = sb("asr", [128, 3, D]); adr = sb("adr", [128, 3, D]); aer = sb("aer", [128, 3, D])
            we = sb("we", [D, 3, D]); prod = sb("prod", [D, 3, 3, D]); wraw = sb("wraw", [D, 3, D])
            begin = sb("begin", [1, 1]); gcol = sb("gcol", [D, 2]); bcol = sb("bcol", [D, 2]); spread = sb("spread", [D, 4, D])
            ones = sb("ones", [128, 128])
            p_t = ps("p_t"); p_w = ps("p_w"); p_b = ps("p_b"); p_c = ps("p_c")
            loaded, ready, folded, turned, kept, made = (
                sem("loaded"), sem("ready"), sem("folded"), sem("turned"), sem("kept"), sem("made"))
            zeroed, stored = sem("zeroed"), sem("stored")
            row = lambda v: v.rearrange("(o n) -> o n", o=1).to_broadcast([128, v.shape[0]])
            rows3 = lambda v: v.rearrange("(o l) n -> o l n", o=1).to_broadcast([128, 3, D])
            cols = lambda v: v.rearrange("(t p) -> p t", p=128)
            loads = [
                (self.w1a[:], a["L0_gnn_w1a"]), (self.w1b[:], a["L0_gnn_w1b"]),
                (self.b1a[:], a["L0_gnn_b1a"].rearrange("(h o) -> h o", o=1)),
                (self.b1b[:], a["L0_gnn_b1b"].rearrange("(h o) -> h o", o=1)),
                (self.w2a[:], a["L0_gnn_w2a"]), (self.b2a[:], cols(a["L0_gnn_b2a"])),
                (w2b[:], a["L0_gnn_w2b"].rearrange("(t p) n -> p t n", p=128)),
                (wl[:], a["L0_gnn_wl"].rearrange("(t p) n -> p t n", p=128)),
                (b2b[:], cols(a["L0_gnn_b2b"])), (self.bc[:], row(a["L0_gnn_bl"])),
                (self.bases[:], a["L1_gnn_bases"].rearrange("b i o -> i b o")),
                (wgr[:], a["L2_gnn_W"]), (self.bg[:], row(a["L2_gnn_bias"])),
                (wraw[:], a["L3_gnn_W"].rearrange("l i o -> i l o")),
                (we[:], a["L3_gnn_W_e"].rearrange("l i o -> i l o")),
                (asr[:], rows3(a["L3_gnn_att_src"])), (adr[:], rows3(a["L3_gnn_att_dst"])),
                (aer[:], rows3(a["L3_gnn_att_edge"])), (self.bl[:], rows3(a["L3_gnn_bias"])),
                (gcol[:], a["L3_gnn_ln_gamma"][0:2, :].rearrange("l i -> i l")),
                (bcol[:], a["L3_gnn_ln_beta"][0:2, :].rearrange("l i -> i l")),
                (self.gam[:], row(a["L3_gnn_ln_gamma"][2, :])),
                (self.bet[:], row(a["L3_gnn_ln_beta"][2, :])),
            ]
            block = ctx.enter_context(nc.Block())

            @block.sync
            def _(sp):
                with nc.allow_non_contiguous_dma(reason="columns of biases, once"):
                    for dst, src in loads:
                        sp.dma_start(dst, src).then_inc(loaded, 16)
                sp.wait_ge(zeroed, 1)
                sp.dma_start(self.t4[SLOTS:SLOTS + 128, :], spread[:, 3, :]).then_inc(stored, 16)
                sp.wait_ge(loaded, 16 * len(loads))
                sp.wait_ge(stored, 16)

            @block.gpsimd
            def _(pool):
                nc.gpsimd.memset(self.ident[:], 0.0).then_inc(ready, 1)
                nc.gpsimd.memset(ones[:], 1.0).then_inc(ready, 1)
                nc.gpsimd.memset(self.eps[:], EPS).then_inc(ready, 1)
                nc.gpsimd.memset(spread[:, 3, :], 0.0).then_inc(zeroed, 1)
                nc.gpsimd.memset(begin[:], 0.0).then_inc(self.begun, 1)
                pool.wait_ge(ready, 3)
                nc.gpsimd.affine_select(out=self.ident[:], in_=self.ident[:], compare_op=ALU.not_equal,
                                        fill=1.0, base=0, pattern=[[-1, 128]],
                                        channel_multiplier=1).then_inc(ready, 1)
                nc.gpsimd.iota(self.iota[:], pattern=[[1, 128]], base=0, channel_multiplier=0,
                               allow_small_or_imprecise_dtypes=True).then_inc(ready, 1)

            @block.vector
            def _(dve):
                dve.wait_ge(loaded, 16 * len(loads))
                dve.wait_ge(ready, 5)
                for n, (w, v) in enumerate(((wraw, asr), (wraw, adr), (we, aer))):
                    nc.vector.tensor_tensor(prod[:, n], w[:], v[:], ALU.mult).then_inc(folded, 1)
                nc.vector.memset(self.wx[:], 0.0).then_inc(folded, 1)
                nc.vector.memset(self.cx[:], 0.0).then_inc(folded, 1)
                dve.wait_ge(folded, 5)
                nc.vector.tensor_copy(self.wx[:, :, 0:D], wraw[:]).then_inc(folded, 1)
                nc.vector.tensor_reduce(self.wx[:, :, D], prod[:, 0], AXX, ALU.add).then_inc(folded, 1)
                nc.vector.tensor_reduce(self.wx[:, :, D + 2], prod[:, 1], AXX, ALU.add).then_inc(folded, 1)
                nc.vector.tensor_reduce(self.ve[:], prod[:, 2], AXX, ALU.add).then_inc(folded, 1)
                for n, c in enumerate((b2b[:, 0:1], b2b[:, 1:2], bcol[:, 0:1], bcol[:, 1:2])):
                    if n == 3:
                        dve.wait_ge(stored, 16)
                    nc.vector.tensor_scalar(spread[:, n], ones[:], c, None, ALU.mult).then_inc(folded, 1)
                dve.wait_ge(turned, 1)
                nc.vector.tensor_copy(w2bt[:].rearrange("p a b -> p (a b)"), p_t[:]).then_inc(kept, 1)
                nc.vector.tensor_copy(self.wg[:], p_b[:, 0:D]).then_inc(kept, 1)
                dve.wait_ge(made, 1)
                nc.vector.tensor_copy(self.wc[:].rearrange("p a b -> p (a b)"), p_w[:, 0:2 * D]).then_inc(kept, 1)
                nc.vector.tensor_tensor(self.bc[:], p_w[:, 2 * D:3 * D], self.bc[:], ALU.add).then_inc(kept, 1)
                nc.vector.tensor_copy(self.cx[:, 1:3, :], p_c[:, 0:2 * XW].rearrange("p (a b) -> p a b", a=2)).then_inc(kept, 1)
                for l in (1, 2):
                    nc.vector.tensor_scalar(self.wx[:, l, :], self.wx[:, l, :], gcol[:, l - 1:l], None,
                                            ALU.mult).then_inc(kept, 1)
                dve.wait_ge(kept, 7)
                nc.vector.memset(self.cx[:, :, D + 1], 1.0).then_inc(kept, 1)

            @block.tensor
            def _(pe):
                pe.wait_ge(loaded, 16 * len(loads))
                pe.wait_ge(ready, 5)
                for t in range(2):
                    for k in range(2):
                        n = 2 * t + k
                        nc.tensor.transpose(p_t[:, n * D:(n + 1) * D], w2b[:, t, k * D:(k + 1) * D], self.ident[:])
                nc.tensor.transpose(p_b[:, 0:D], wgr[:], self.ident[:]).then_inc(turned, 1)
                pe.wait_ge(kept, 1)
                pe.wait_ge(folded, 13)
                for t in range(2):
                    for k in range(2):
                        nc.tensor.matmul(p_w[:, t * D:(t + 1) * D], w2bt[:, 2 * t + k, :], wl[:, k, :],
                                         start=(k == 0), stop=(k == 1))
                for k in range(2):
                    nc.tensor.matmul(p_w[:, 2 * D:3 * D], spread[:, k, :], wl[:, k, :], start=(k == 0), stop=(k == 1))
                for l in (1, 2):
                    last = nc.tensor.matmul(p_c[:, (l - 1) * XW:l * XW], spread[:, 1 + l, :], self.wx[:, l, :],
                                            start=True, stop=True)
                last.then_inc(made, 1)

    def phase_terms(self):
        nc, a = self.nc, self.a
        ctx, sb, ps, sem = self.scope("et")
        full, rest = E // GN, E % GN // G4
        with ctx:
            rows = sb("rows", [128, UN, G4, D]); turned = sb("turned", [D, 2, GN]); res = sb("res", [3, 2, GN])
            p_t = [ps(f"p_t{i}") for i in range(2)]; p_r = [ps(f"p_r{i}") for i in range(2)]
            arrived = [sem(f"arrived{i}") for i in range(UN)]
            stored = [sem(f"stored{i}") for i in range(2)]
            cleared, pe_t, act_t, pe_r, dve_r = sem("cleared"), sem("pe_t"), sem("act_t"), sem("pe_r"), sem("dve_r")
            attr = a["edge_attr_128"]
            groups = full + 1
            block = ctx.enter_context(nc.Block())

            @block.sync
            def _(sp):
                sp.wait_ge(cleared, 1)

                def step(k, u):
                    if live(k, u, 0, groups):
                        i = UN * k + u
                        wait(sp, pe_t, i - UN + 1)
                        if isinstance(i, int) and i == full:
                            sp.dma_start(rows[0:rest, u], attr[full * GN:E, :].rearrange("(p j) f -> p j f", j=G4)).then_inc(arrived[u], 16)
                        else:
                            v = attr[0:full * GN, :].rearrange("(g p j) f -> g p j f", p=128, j=G4)
                            sp.dma_start(rows[:, u], v[bass.ds(i, 1)].rearrange("g p j f -> p (g j) f")).then_inc(arrived[u], 16)
                    if live(k, u, 1, groups):
                        i = UN * k + u - 1
                        sp.wait_ge(dve_r, i + 1)
                        n = rest * G4 if isinstance(i, int) and i == full else GN
                        sp.dma_start(self.terms[:, bass.ds(i * GN, n)], res[:, (u - 1) % 2, 0:n]).then_inc(stored[(u - 1) % 2], 16)

                steps(sp, groups, 1, step)
                for i in range(2):
                    sp.wait_ge(stored[i], 16 * ((groups + 1 - i) // 2))

            @block.gpsimd
            def _(pool):
                nc.gpsimd.memset(rows[:].rearrange("p a b c -> p (a b c)"), 0.0).then_inc(cleared, 1)

            @block.tensor
            def _(pe):
                def step(k, u):
                    if live(k, u, 0, groups):
                        i = UN * k + u
                        pe.wait_ge(arrived[u], 16 * (k + 1))
                        wait(pe, act_t, i - 1)
                        for j in range(G4):
                            last = nc.tensor.transpose(p_t[u % 2][:, j * D:(j + 1) * D], rows[:, u, j, :], self.ident[:])
                        last.then_inc(pe_t, 1)
                    if live(k, u, 1, groups):
                        i = UN * k + u - 1
                        pe.wait_ge(act_t, i + 1)
                        wait(pe, dve_r, i - 1)
                        nc.tensor.matmul(p_r[(u - 1) % 2][0:3, :], self.ve[:], turned[:, (u - 1) % 2, :],
                                         start=True, stop=True).then_inc(pe_r, 1)

                steps(pe, groups, 1, step)

            @block.scalar
            def _(act):
                def step(k, u):
                    i = UN * k + u
                    act.wait_ge(pe_t, i + 1)
                    wait(act, pe_r, i - 1)
                    nc.scalar.activation(turned[:, u % 2, :], p_t[u % 2][:], ACT.Copy).then_inc(act_t, 1)

                steps(act, groups, 0, step)

            @block.vector
            def _(dve):
                def step(k, u):
                    i = UN * k + u
                    dve.wait_ge(pe_r, i + 1)
                    if not isinstance(i, int) or i >= 2:
                        dve.wait_ge(stored[u % 2], 16 * (2 * k + u // 2))
                    nc.vector.tensor_copy(res[:, u % 2, :].rearrange("r (p j) -> r j p", j=G4),
                                          p_r[u % 2][0:3, :].rearrange("r (j p) -> r j p", j=G4)).then_inc(dve_r, 1)

                steps(dve, groups, 0, step)

    def phase_segments(self):
        nc, a = self.nc, self.a
        ctx, sb, ps, sem = self.scope("sg")
        whole = E // RE
        rest = E - whole * RE
        with ctx:
            dst_raw = sb("dst_raw", [ROWP, RE + 2], I32)
            raw = sb("raw", [ROWP, 2, RE], I32)
            wr = sb("wr", [ROWP, RE])
            dstf = sb("dstf", [ROWP, RE + 2])
            row = sb("row", [ROWP, 6, 256])
            start = sb("start", [ROWP, 256]); pos = sb("pos", [ROWP, 256]); tmp = sb("tmp", [ROWP, 256])
            ty = sb("ty", [128, CHUNKS]); wcol = sb("wcol", [128, CHUNKS]); pick = sb("pick", [128, 8, CHUNKS])
            wcomp = sb("wcomp", [128, 8, 4])
            deg_tmp = sb("nodes", [128, NPAD // 128], I32)
            p = [ps(f"p{i}") for i in range(7)]
            loaded, cleared, told, v, turned, rows_done, gone = (
                sem("loaded"), sem("cleared"), sem("told"), sem("v"), sem("turned"), sem("rows_done"), sem("gone"))
            halves = lambda x: x.rearrange("p (j k) -> p j k", j=2)

            dst_loads = [
                (dst_raw[0:1, 1:RE + 2], bass.AP(tensor=a["dst"].tensor, offset=0, ap=[[RE, 1], [1, RE + 1]])),
                (dst_raw[1:whole, :], bass.AP(tensor=a["dst"].tensor, offset=RE - 1, ap=[[RE, whole - 1], [1, RE + 2]])),
                (dst_raw[whole:whole + 1, 0:rest + 1],
                 bass.AP(tensor=a["dst"].tensor, offset=whole * RE - 1, ap=[[RE, 1], [1, rest + 1]])),
            ]
            other_loads = []
            for t, name in ((raw[:, 0], "src"), (raw[:, 1], "edge_type_8"), (wr[:], "edge_weight")):
                other_loads.append((t[0:whole, :], a[name][0:whole * RE].rearrange("(p k) -> p k", k=RE)))
                other_loads.append((t[whole:whole + 1, 0:rest],
                                    a[name][whole * RE:E].rearrange("(o k) -> o k", o=1)))
            for l in range(3):
                t = halves(self.edge_t[:, l, :])[:, :, 1:128]
                r = self.terms[l, :]
                other_loads.append((t[0:whole], r[0:whole * RE].rearrange("(p j k) -> p j k", j=2, k=CE)))
                assert rest <= CE
                other_loads.append((t[whole:whole + 1, 0, 0:rest], r[whole * RE:E].rearrange("(o k) -> o k", o=1)))
            n_loads = len(dst_loads) + len(other_loads) + 1
            block = ctx.enter_context(nc.Block())

            @block.sync
            def _(sp):
                sp.wait_ge(cleared, 5)
                for dst, src in dst_loads + other_loads:
                    sp.dma_start(dst, src).then_inc(loaded, 16)
                sp.dma_start(wcomp[:], a["L1_gnn_w_comp"].rearrange("(o r) b -> o r b", o=1).to_broadcast([128, 8, 4])).then_inc(loaded, 16)
                sp.wait_ge(told, 2)
                sp.dma_start(self.where.rearrange("(p t) o -> p (t o)", p=128), deg_tmp[:]).then_inc(gone, 16)
                sp.wait_ge(gone, 16)
                sp.wait_ge(loaded, 16 * n_loads)

            @block.gpsimd
            def _(pool):
                nc.gpsimd.memset(dst_raw[:], FAR).then_inc(cleared, 1)
                nc.gpsimd.memset(raw[:].rearrange("p a b -> p (a b)"), 0).then_inc(cleared, 1)
                nc.gpsimd.memset(wr[:], 0.0).then_inc(cleared, 1)
                nc.gpsimd.memset(self.edge_t[:].rearrange("p a b -> p (a b)"), 0.0).then_inc(cleared, 1)
                nc.gpsimd.memset(row[:].rearrange("p a b -> p (a b)"), 0.0).then_inc(cleared, 1)
                nc.gpsimd.iota(halves(pos[:]), pattern=[[0, 2], [1, 128]], base=0, channel_multiplier=0,
                               allow_small_or_imprecise_dtypes=True).then_inc(told, 1)
                nc.gpsimd.iota(deg_tmp[:], pattern=[[1, NPAD // 128]], base=SLOTS,
                               channel_multiplier=NPAD // 128).then_inc(told, 1)
                nc.gpsimd.iota(self.slot_id[:], pattern=[[1, CHUNKS]], base=0,
                               channel_multiplier=CHUNKS).then_inc(told, 1)
                nc.gpsimd.memset(self.end[:], 0.0).then_inc(told, 1)
                nc.gpsimd.memset(start[:], 0.0).then_inc(told, 1)
                nc.gpsimd.memset(self.startneg[:], 0.0).then_inc(told, 1)

            @block.vector
            def _(dve):
                count = [0]

                def after(ins):
                    count[0] += 1
                    ins.then_inc(v, 1)
                    dve.wait_ge(v, count[0])

                dve.wait_ge(loaded, 16 * n_loads)
                dve.wait_ge(told, 6)
                after(nc.vector.tensor_copy(dstf[:], dst_raw[:]))
                after(nc.vector.memset(dstf[0:1, 0:1], -1.0))
                cur = halves(dstf[:, 1:RE + 1])
                at = lambda t: halves(t[:])[:, :, 1:128]
                nc.vector.tensor_tensor(at(start), cur, halves(dstf[:, 0:RE]), ALU.not_equal).then_inc(v, 1)
                nc.vector.tensor_tensor(at(self.end), cur, halves(dstf[:, 2:RE + 2]), ALU.not_equal).then_inc(v, 1)
                nc.vector.tensor_copy(halves(row[:, 0])[:, :, 1:128], halves(raw[:, 0])).then_inc(v, 1)
                nc.vector.tensor_scalar(halves(row[:, 1])[:, :, 1:128], cur, float(N - 1), None, ALU.min).then_inc(v, 1)
                nc.vector.tensor_copy(halves(row[:, 3])[:, :, 1:128], halves(wr[:])).then_inc(v, 1)
                nc.vector.tensor_copy(halves(row[:, 4])[:, :, 1:128], halves(raw[:, 1])).then_inc(v, 1)
                count[0] += 6
                dve.wait_ge(v, count[0])
                nc.vector.tensor_scalar(self.notend[:], self.end[:], -1.0, 1.0, ALU.mult, ALU.add).then_inc(v, 1)
                nc.vector.tensor_scalar(self.startneg[:], start[:], -BIG, None, ALU.mult).then_inc(v, 1)
                nc.vector.tensor_scalar(halves(row[:, 2])[:, :, 1:128], cur, float(-FAR), None, ALU.add).then_inc(v, 1)
                nc.vector.tensor_tensor(tmp[:], self.end[:], pos[:], ALU.mult).then_inc(v, 1)
                count[0] += 4
                dve.wait_ge(v, count[0])
                after(nc.vector.tensor_tensor(row[:, 2], row[:, 2], self.end[:], ALU.mult))
                after(nc.vector.tensor_scalar(row[:, 2], row[:, 2], float(FAR), None, ALU.add))
                for j in range(2):
                    lo, hi = j * 128, (j + 1) * 128
                    back = slice(hi - 1, lo - 1 if lo else None, -1)
                    after(nc.vector.tensor_tensor_scan(row[:, 5, back], self.notend[:, back], tmp[:, back], 0.0,
                                                       ALU.mult, ALU.add))
                q0, q1, s1 = (halves(t)[:, :, k] for t, k in ((row[:, 5], 0), (row[:, 5], 1), (start[:], 1)))
                after(nc.vector.tensor_scalar(q0, q1, 1.0, None, ALU.add))
                after(nc.vector.tensor_tensor(q0, q0, s1, ALU.mult))
                after(nc.vector.tensor_tensor(q0, q1, q0, ALU.subtract))
                after(nc.vector.tensor_tensor_scan(self.preneg[:], self.startneg[:], self.startneg[:], 0.0,
                                                   ALU.min, ALU.min))
                after(nc.vector.tensor_tensor_scan(self.open[:, ::-1], self.notend[:, ::-1], self.notend[:, ::-1], 1.0,
                                                   ALU.mult, ALU.mult))
                nc.vector.tensor_copy(tmp[:, 0:2], self.open[:, 0:2]).then_inc(rows_done, 1)
                dve.wait_ge(turned, 1)
                both = lambda t: t.rearrange("q (p j) -> q j p", j=2)
                of = lambda n: p[n][:, 0:CHUNKS].rearrange("q (j p) -> q j p", j=2)
                nc.vector.tensor_copy(both(self.src_i[:]), of(0)).then_inc(v, 1)
                nc.vector.tensor_copy(both(self.dst_i[:]), of(1)).then_inc(v, 1)
                nc.vector.tensor_copy(both(self.own_i[:]), of(2)).then_inc(v, 1)
                nc.vector.tensor_copy(both(wcol[:]), of(3)).then_inc(v, 1)
                nc.vector.tensor_copy(both(ty[:]), of(4)).then_inc(v, 1)
                nc.vector.tensor_copy(both(self.q[:]), of(5)).then_inc(v, 1)
                nc.vector.tensor_copy(self.flag_rows[:].rearrange("o a b -> o (a b)"), p[6][0:1, 0:2 * ROWP]).then_inc(v, 1)
                count[0] += 7
                dve.wait_ge(v, count[0])
                after(nc.vector.memset(self.msgs[:, :, D], 1.0))
                for l in range(3):
                    nc.vector.tensor_copy(self.msgs[:, :, D + 1 + l].rearrange("q (p j) -> q j p", j=2),
                                          p[l][:, 256:256 + CHUNKS].rearrange("q (j p) -> q j p", j=2)).then_inc(v, 1)
                    nc.vector.memset(halves(self.edge_t[:, l, :])[:, :, 0], -BIG).then_inc(v, 1)
                    count[0] += 2
                for r in range(8):
                    nc.vector.tensor_scalar(pick[:, r], ty[:], float(r), None, ALU.is_equal).then_inc(v, 1)
                count[0] += 8
                dve.wait_ge(v, count[0])
                for b in range(4):
                    after(nc.vector.tensor_scalar(self.coef[:, b], pick[:, 0], wcomp[:, 0, b:b + 1], None, ALU.mult))
                    for r in range(1, 8):
                        after(nc.vector.scalar_tensor_tensor(out=self.coef[:, b], in0=pick[:, r], scalar=wcomp[:, r, b:b + 1],
                                                             in1=self.coef[:, b], op0=ALU.mult, op1=ALU.add))
                    after(nc.vector.tensor_tensor(self.coef[:, b], self.coef[:, b], wcol[:], ALU.mult))

            @block.tensor
            def _(pe):
                pe.wait_ge(rows_done, 1)
                idp = self.ident[0:ROWP, 0:ROWP]
                for n in range(6):
                    for j in range(2):
                        nc.tensor.transpose(p[n][:, j * ROWP:(j + 1) * ROWP], row[:, n, j * 128:(j + 1) * 128], idp)
                for l in range(3):
                    for j in range(2):
                        nc.tensor.transpose(p[l][:, 256 + j * ROWP:256 + (j + 1) * ROWP],
                                            self.edge_t[:, l, j * 128:(j + 1) * 128], idp)
                nc.tensor.transpose(p[6][0:1, 0:ROWP], self.preneg[:, 255:256], idp)
                nc.tensor.transpose(p[6][0:1, ROWP:2 * ROWP], self.open[:, 0:1], idp).then_inc(turned, 1)

    def gather_group(self, pool, k, u, count, idx, stage, staged, table, ring, width, arrived, freed):
        nc = self.nc

        def put(k, u):
            if not isinstance(k, int) or k > 0:
                pool.wait_ge(arrived[u], 16 * G4 * k)
            i = UN * k + u
            nc.gpsimd.tensor_copy(stage[:, u, :], idx[:, bass.ds(i * G4, G4)]).then_inc(staged, 1)

        i = UN * k + u
        if isinstance(i, int) and i == 0:
            put(k, u)
        if not isinstance(i, int) or i + 1 < count:
            put(k + (u + 1) // UN, (u + 1) % UN)
        self.hold(pool, (staged, i + 1), *freed(k, u))
        for j in range(G4):
            nc.gpsimd.indirect_dma_start(
                out=ring[:, u, j, 0:width], out_offset=None, in_=table,
                in_offset=bass.IndirectOffsetOnAxis(ap=stage[:, u, j:j + 1], axis=0)).then_inc(arrived[u], 16)

    def resident_gather(self, idx, table, width, arrived):
        for c in range(CHUNKS):
            self.nc.gpsimd.indirect_dma_start(
                out=self.msgs[:, c, 0:width], out_offset=None, in_=table,
                in_offset=bass.IndirectOffsetOnAxis(ap=idx[:, c:c + 1], axis=0)).then_inc(arrived, 16)

    def slot_gathers(self, pool, sb, sem):
        nc, a = self.nc, self.a
        ring = sb("g_ring", [128, UN, G4, D]); rows = sb("g_rows", [128, UN, G4, 1], I32)
        stages = [sb(f"g_stage{n}", [128, UN, G4], I32) for n in range(5)]
        arrived = [[sem(f"g_arrived{n}_{u}") for u in range(UN)] for n in range(4)]
        staged = [sem(f"g_staged{n}") for n in range(4)]
        taken = sem("g_taken")
        copied = sem("g_copied")
        lag = UN - 1

        self.resident_gather(self.src_i, a["x"], D, arrived[0][0])

        def second(k, u):
            def freed(k, u):
                return ((stored[u], 16 * k),)
            if live(k, u, 0, AG):
                self.gather_group(pool, k, u, AG, self.dst_i, stages[1], staged[1], a["x"], ring, D, arrived[1], freed)
            if live(k, u, lag, AG):
                v = (u - lag) % UN
                kk = k - (1 if u < lag else 0)
                pool.wait_ge(arrived[1][v], 16 * G4 * (kk + 1))
                pool.dma_start(self.slots(self.xd, kk, v), ring[:, v]).then_inc(stored[v], 16)

        stored = [sem(f"g_stored{u}") for u in range(UN)]
        steps(pool, AG, lag, second)

        def third(k, u):
            i = UN * k + u
            if not isinstance(k, int) or k > 0:
                pool.wait_ge(arrived[2][u], 16 * G4 * k)
            nc.gpsimd.tensor_copy(stages[2][:, u, :], self.own_i[:, bass.ds(i * G4, G4)]).then_inc(staged[2], 1)
            nc.gpsimd.tensor_copy(stages[3][:, u, :], self.slot_id[:, bass.ds(i * G4, G4)]).then_inc(staged[2], 1)
            self.hold(pool, (staged[2], 2 * i + 2))
            for j in range(G4):
                nc.gpsimd.indirect_dma_start(
                    out=self.where, out_offset=bass.IndirectOffsetOnAxis(ap=stages[2][:, u, j:j + 1], axis=0),
                    in_=stages[3][:, u, j:j + 1], in_offset=None, bounds_check=N - 1,
                    oob_is_err=False).then_inc(arrived[2][u], 16)

        steps(pool, AG, 0, third)
        for u in range(UN):
            groups = (AG - u + UN - 1) // UN
            pool.wait_ge(arrived[2][u], 16 * G4 * groups)
            pool.wait_ge(stored[u], 16 * groups)

        def fourth(k, u):
            def freed(k, u):
                return ((taken, UN * k + u - UN + 1),)
            if live(k, u, 0, AG):
                self.gather_group(pool, k, u, AG, self.src_i, stages[4], staged[3], self.where, rows, 1, arrived[3], freed)
            if live(k, u, lag, AG):
                v = (u - lag) % UN
                kk = k - (1 if u < lag else 0)
                pool.wait_ge(arrived[3][v], 16 * G4 * (kk + 1))
                nc.gpsimd.tensor_copy(self.row_i[:, bass.ds((UN * kk + v) * G4, G4)],
                                      rows[:, v].rearrange("p j o -> p (j o)")).then_inc(taken, 1)

        steps(pool, AG, lag, fourth)
        pool.wait_ge(taken, AG)
        pool.wait_ge(arrived[0][0], 16 * CHUNKS)
        nc.gpsimd.tensor_scalar(self.row4_i[:], self.row_i[:], SLOTS, None, ALU.min).then_inc(copied, 1)

    def norm_stats(self, rows, st, mv, chain):
        nc = self.nc
        for j in range(G4):
            last = nc.vector.bn_stats(out=st[:, j, :], in_=rows(j))
        chain(last, self.hold)
        for j in range(G4):
            last = nc.vector.bn_aggr(out=mv[:, j, :], in_=st[:, j, :])
        chain(last)

    def norm_inverse(self, mv, inv, chain):
        nc = self.nc
        chain(nc.vector.tensor_scalar(inv, mv[:, :, 1], EPS, None, ALU.add))
        return nc.vector.reciprocal(inv, inv)

    def norm_shift(self, mv, rs, nb):
        return self.nc.vector.scalar_tensor_tensor(out=nb, in0=mv[:, :, 0], scalar=-1.0, in1=rs,
                                                   op0=ALU.mult, op1=ALU.mult)

    def norm_apply(self, out, rows, rs, nb):
        for j in range(G4):
            last = self.nc.scalar.activation(out[:, j, :], rows[:, j, :], ACT.Identity,
                                             bias=nb[:, j:j + 1], scale=rs[:, j:j + 1])
        return last

    def each(self, row):
        return row.rearrange("p (o f) -> p o f", o=1).to_broadcast([128, G4, row.shape[1]])

    def phase_dense(self):
        nc, a = self.nc, self.a
        ctx, sb, ps, sem = self.scope("de")
        with ctx:
            x = sb("x", [128, UN, G4, D])
            xt = sb("xt", [D, GN]); ha = sb("ha", [H, GN]); ht = sb("ht", [H, GN]); hh = sb("hh", [D, 2, GN])
            h1 = sb("h1", [128, 2, G4, H])
            r = sb("r", [128, 2, G4, D]); x1 = sb("x1", [128, 2, G4, D]); v = sb("v", [128, 2, G4, D])
            x3 = sb("x3", [128, 2, G4, D]); x3t = sb("x3t", [D, GN]); h0 = sb("h0", [128, 2, G4, XW])
            st = sb("st", [128, G4, 6]); st2 = sb("st2", [128, G4, 6])
            mv = sb("mv", [128, 2, G4, 2]); mv2 = sb("mv2", [128, 2, G4, 2])
            inv = sb("inv", [128, 2, 2, G4]); rs = sb("rs", [128, 2, 2, G4]); nb = sb("nb", [128, 2, G4])
            inv2 = sb("inv2", [128, 2, G4]); rs2 = sb("rs2", [128, 2, G4]); nb2 = sb("nb2", [128, 2, G4])
            p_x, p_a, p_b, p_c0, p_c1, p_o = (ps(n) for n in ("p_x", "p_a", "p_b", "p_c0", "p_c1", "p_o"))
            p_h = ps("p_h", (128, 2, 512))
            arrived = [sem(f"arrived{u}") for u in range(UN)]
            out2, out3, outx, outh = ([sem(f"{n}{u}") for u in range(2)] for n in ("out2_", "out3_", "outx_", "outh_"))
            names = ("pe_xt", "act_xt", "pe_a", "act_a", "pe_b", "act_b", "pe_h1", "dve_h1", "pe_c", "act_c",
                     "pe_o", "dve_r", "dve_inv", "act_rs", "dve_nb", "act_x1", "dve_v", "dve_inv2", "act_rs2",
                     "dve_nb2", "act_x3", "pe_x3t", "act_x3t", "pe_h0", "dve_h0", "link1", "link2", "cleared")
            s = {n: sem(n) for n in names}
            last_rows = (N - (DG - 1) * GN) // G4
            block = ctx.enter_context(nc.Block())

            def stored(eng, sems, k, u, lag):
                n = UN * k + u - lag
                if not isinstance(n, int):
                    eng.wait_ge(sems[(u - lag) % 2], 16 * (2 * k + (u - lag) // 2))
                elif n >= 2:
                    eng.wait_ge(sems[n % 2], 16 * (n // 2))

            @block.sync
            def _(sp):
                sp.wait_ge(s["cleared"], 1)

                def step(k, u):
                    i = UN * k + u
                    if live(k, u, 0, DG):
                        wait(sp, s["dve_r"], i - UN + 1)
                        if isinstance(i, int) and i == DG - 1:
                            sp.dma_start(x[0:last_rows, u], a["x"][(DG - 1) * GN:N, :].rearrange("(p j) f -> p j f", j=G4)).then_inc(arrived[u], 16)
                        else:
                            t = a["x"][0:(DG - 1) * GN, :].rearrange("(g p j) f -> g p j f", p=128, j=G4)
                            sp.dma_start(x[:, u], t[bass.ds(i, 1)].rearrange("g p j f -> p (g j) f")).then_inc(arrived[u], 16)
                    if live(k, u, 1, DG):
                        w = (u - 1) % 2
                        sp.wait_ge(s["dve_h1"], i)
                        sp.dma_start(self.nodes(self.t2, k, u, 1), h1[:, w]).then_inc(out2[w], 16)
                    if live(k, u, 3, DG):
                        w = (u - 3) % 2
                        sp.wait_ge(s["act_x1"], i - 2)
                        sp.dma_start(self.nodes(self.t3, k, u, 3), x1[:, w]).then_inc(out3[w], 16)
                    if live(k, u, 4, DG):
                        w = u % 2
                        sp.wait_ge(s["act_x3"], i - 3)
                        sp.dma_start(self.nodes(self.x3, k, u, 4), x3[:, w]).then_inc(outx[w], 16)
                        sp.wait_ge(s["dve_h0"], i - 3)
                        sp.dma_start(self.nodes(self.th[0], k, u, 4), h0[:, w]).then_inc(outh[w], 16)

                steps(sp, DG, 4, step)
                for o in (out2, out3, outx, outh):
                    for w in range(2):
                        sp.wait_ge(o[w], 16 * ((DG + 1 - w) // 2))

            @block.gpsimd
            def _(pool):
                nc.gpsimd.memset(x[:].rearrange("p a b c -> p (a b c)"), 0.0).then_inc(s["cleared"], 1)
                self.slot_gathers(pool, sb, sem)

            @block.tensor
            def _(pe):
                def step(k, u):
                    i = UN * k + u
                    if live(k, u, 0, DG):
                        pe.wait_ge(arrived[u], 16 * (k + 1))
                        wait(pe, s["act_x3t"], i - 3)
                        for j in range(G4):
                            m = nc.tensor.transpose(p_x[:, j * D:(j + 1) * D], x[:, u, j, :], self.ident[:])
                        m.then_inc(s["pe_xt"], 1)
                    if live(k, u, 1, DG):
                        pe.wait_ge(s["act_c"], 2 * i)
                        wait(pe, s["dve_r"], i - 1)
                        for j in range(G4):
                            for t in range(2):
                                m = nc.tensor.matmul(p_o[:, j * D:(j + 1) * D], hh[:, t, j * D:(j + 1) * D],
                                                     self.wc[:, t, :], start=(t == 0), stop=(t == 1))
                        m.then_inc(s["pe_o"], 1)
                    if live(k, u, 0, DG):
                        pe.wait_ge(s["act_xt"], i + 1)
                        wait(pe, s["act_a"], i)
                        wait(pe, s["dve_h1"], i)
                        nc.tensor.matmul(p_a[0:H, :], self.w1a[:], xt[:], start=True, stop=True).then_inc(s["pe_a"], 1)
                    if live(k, u, 3, DG):
                        pe.wait_ge(s["act_x3"], i - 2)
                        pe.wait_ge(s["act_xt"], (i if not isinstance(i, int) else min(i, DG - 1)) + 1)
                        for j in range(G4):
                            m = nc.tensor.transpose(p_x[:, j * D:(j + 1) * D], x3[:, (u - 3) % 2, j, :], self.ident[:])
                        m.then_inc(s["pe_x3t"], 1)
                    if live(k, u, 0, DG):
                        self.hold(pe, (s["act_a"], i + 1), (s["act_b"], i))
                        nc.tensor.matmul(p_b[0:H, :], self.w1b[:], ha[:], start=True, stop=True).then_inc(s["pe_b"], 1)
                    if live(k, u, 3, DG):
                        pe.wait_ge(s["act_x3t"], i - 2)
                        wait(pe, s["dve_h0"], i - 3)
                        self.gat_rows(x3t, p_h, 0).then_inc(s["pe_h0"], 1)
                    if live(k, u, 0, DG):
                        self.hold(pe, (s["act_b"], i + 1))
                        for j in range(G4):
                            m = nc.tensor.transpose(p_a[:, j * H:(j + 1) * H], ht[:, j * D:(j + 1) * D], self.ident[0:H, 0:H])
                        m.then_inc(s["pe_h1"], 1)
                        for t, bank in enumerate((p_c0, p_c1)):
                            wait(pe, s["act_c"], 2 * i + t - 1)
                            nc.tensor.matmul(bank[:], self.w2a[:, t * D:(t + 1) * D], ht[:], start=True, stop=True).then_inc(s["pe_c"], 1)

                steps(pe, DG, 3, step)

            @block.scalar
            def _(act):
                def step(k, u):
                    i = UN * k + u
                    if live(k, u, 0, DG):
                        act.wait_ge(s["pe_xt"], i + 1)
                        wait(act, s["pe_a"], i)
                        nc.scalar.activation(xt[:], p_x[:], ACT.Copy).then_inc(s["act_xt"], 1)
                    if live(k, u, 3, DG):
                        w = (u - 3) % 2
                        act.wait_ge(s["dve_nb2"], i - 2)
                        stored(act, outx, k, u, 3)
                        self.norm_apply(x3[:, w], v[:, w], rs2[:, w], nb2[:, w]).then_inc(s["act_x3"], 1)
                    if live(k, u, 0, DG):
                        act.wait_ge(s["pe_a"], i + 1)
                        wait(act, s["pe_b"], i)
                        nc.scalar.activation(ha[:], p_a[0:H, :], ACT.Relu, bias=self.b1a[:]).then_inc(s["act_a"], 1)
                    if live(k, u, 2, DG):
                        w = u % 2
                        act.wait_ge(s["dve_nb"], i - 1)
                        stored(act, out3, k, u, 2)
                        wait(act, s["dve_v"], i - 3)
                        self.norm_apply(x1[:, w], r[:, w], rs[:, w, 0], nb[:, w]).then_inc(s["act_x1"], 1)
                    if live(k, u, 0, DG):
                        act.wait_ge(s["pe_b"], i + 1)
                        wait(act, s["pe_c"], 2 * i)
                        wait(act, s["pe_h1"], i)
                        nc.scalar.activation(ht[:], p_b[0:H, :], ACT.Relu, bias=self.b1b[:]).then_inc(s["act_b"], 1)
                    if live(k, u, 3, DG):
                        act.wait_ge(s["pe_x3t"], i - 2)
                        wait(act, s["pe_h0"], i - 3)
                        nc.scalar.activation(x3t[:], p_x[:], ACT.Copy).then_inc(s["act_x3t"], 1)
                    if live(k, u, 0, DG):
                        for t, bank in enumerate((p_c0, p_c1)):
                            act.wait_ge(s["pe_c"], 2 * i + t + 1)
                            wait(act, s["pe_o"], i)
                            nc.scalar.activation(hh[:, t, :], bank[:], ACT.Relu, bias=self.b2a[:, t:t + 1]).then_inc(s["act_c"], 1)
                    if live(k, u, 1, DG):
                        w = (u - 1) % 2
                        act.wait_ge(s["dve_inv"], i)
                        wait(act, s["dve_v"], i - 2)
                        nc.scalar.activation(rs[:, w], inv[:, w], ACT.Sqrt).then_inc(s["act_rs"], 1)
                    if live(k, u, 2, DG):
                        w = u % 2
                        act.wait_ge(s["dve_inv2"], i - 1)
                        nc.scalar.activation(rs2[:, w], inv2[:, w], ACT.Sqrt).then_inc(s["act_rs2"], 1)

                steps(act, DG, 3, step)

            @block.vector
            def _(dve):
                link1 = Chain(dve, s["link1"], 7)
                link2 = Chain(dve, s["link2"], 3)

                def step(k, u):
                    i = UN * k + u
                    if live(k, u, 3, DG):
                        w = (u - 3) % 2
                        dve.wait_ge(s["act_rs2"], i - 2)
                        self.norm_shift(mv2[:, w], rs2[:, w], nb2[:, w]).then_inc(s["dve_nb2"], 1)
                    if live(k, u, 2, DG):
                        w = u % 2
                        dve.wait_ge(s["act_rs"], i - 1)
                        self.norm_shift(mv[:, w], rs[:, w, 0], nb[:, w]).then_inc(s["dve_nb"], 1)
                    if live(k, u, 1, DG):
                        w = (u - 1) % 2
                        link1.group(i - 1)
                        dve.wait_ge(s["pe_o"], i)
                        wait(dve, s["act_x1"], i - 2)
                        nc.vector.tensor_tensor(r[:, w].rearrange("p a b -> p (a b)"), p_o[:],
                                                x[:, (u - 1) % UN].rearrange("p a b -> p (a b)"), ALU.add).then_inc(s["dve_r"], 1)
                        dve.wait_ge(s["dve_r"], i)
                        link1(nc.vector.tensor_tensor(r[:, w], r[:, w], self.each(self.bc[:]), ALU.add))
                        self.norm_stats(lambda j: r[:, w, j, :], st, mv[:, w], link1)
                        link1(self.norm_inverse(mv[:, w], inv[:, w, 0], link1))
                        link1(nc.vector.tensor_tensor(inv[:, w, 1], mv[:, w, :, 1], inv[:, w, 0], ALU.mult))
                        link1(nc.vector.tensor_scalar(inv[:, w, 1], inv[:, w, 1], EPS, None, ALU.add))
                        nc.vector.reciprocal(inv[:, w, 1], inv[:, w, 1]).then_inc(s["dve_inv"], 1)
                    if live(k, u, 3, DG):
                        w = (u - 3) % 2
                        dve.wait_ge(s["pe_h0"], i - 2)
                        stored(dve, outh, k, u, 3)
                        self.gat_rows_out(h0[:, w], p_h, 0).then_inc(s["dve_h0"], 1)
                    if live(k, u, 2, DG):
                        w = u % 2
                        link2.group(i - 2)
                        dve.wait_ge(s["act_x1"], i - 1)
                        wait(dve, s["act_x3"], i - 3)
                        for j in range(G4):
                            m = nc.vector.scalar_tensor_tensor(out=v[:, w, j, :], in0=x1[:, w, j, :], scalar=rs[:, w, 1, j:j + 1],
                                                               in1=self.bg[:], op0=ALU.mult, op1=ALU.add)
                        m.then_inc(s["dve_v"], 1)
                        dve.wait_ge(s["dve_v"], i - 1)
                        self.norm_stats(lambda j: v[:, w, j, :], st2, mv2[:, w], link2)
                        self.norm_inverse(mv2[:, w], inv2[:, w], link2).then_inc(s["dve_inv2"], 1)
                    if live(k, u, 0, DG):
                        dve.wait_ge(s["pe_h1"], i + 1)
                        stored(dve, out2, k, u, 0)
                        nc.vector.tensor_copy(h1[:, u % 2].rearrange("p a b -> p (a b)"), p_a[:, 0:G4 * H]).then_inc(s["dve_h1"], 1)

                steps(dve, DG, 3, step)

    def cx2(self, l):
        return self.cx[:, l, :].rearrange("p (o f) -> p o f", o=1).to_broadcast([128, 2, XW])

    def select_group(self, m, k, u, lag, weight=None):
        nc = self.nc
        c0 = (UN * k + u - lag) * G4
        if weight is None:
            q = self.q[:, bass.ds(c0, G4)].rearrange("p (c o) -> p c o", o=1).to_broadcast([128, G4, 128])
            return nc.vector.tensor_tensor(m, self.each(self.iota[:]), q, ALU.is_equal)
        for j in range(G4):
            last = nc.vector.tensor_scalar(m[:, j, :], self.iota[:], self.q[:, bass.ds(c0 + j, 1)],
                                           weight[:, bass.ds(c0 + j, 1)], ALU.is_equal, ALU.mult)
        return last

    def sum_chunk(self, pe, n, j, out, m, msg, carried, summed):
        wait(pe, carried, n * G4 + j)
        self.nc.tensor.matmul(out, m[:, j, :], msg, start=True, stop=True).then_inc(summed, 1)

    def carry_chunk(self, act, n, j, row0, out, carried, summed):
        act.wait_ge(summed, n * G4 + j)
        self.nc.scalar.activation(row0, out, ACT.Copy).then_inc(carried, 1)

    def wait_sums(self, dve, n, carried, summed):
        dve.wait_ge(summed, (n + 1) * G4)
        dve.wait_ge(carried, min(n + 1, AG - 1) * G4 + (G4 - 1 if n == AG - 1 else 0) if isinstance(n, int) else (n + 1) * G4)

    def ring_gather(self, nc, pool, sb, sem, idx, table, width, ring, arrived, summed, count=AG):
        stage = sb("g_stage", [128, UN, G4], I32)
        staged = sem("g_staged")

        def step(k, u):
            def freed(k, u):
                return ((summed, (UN * k + u - UN + 1) * G4),)
            self.gather_group(pool, k, u, count, idx, stage, staged, table, ring, width, arrived, freed)

        steps(pool, count, 0, step)

    def stored(self, eng, sems, k, u, lag):
        n = UN * k + u - lag
        if not isinstance(n, int):
            eng.wait_ge(sems[(u - lag) % 2], 16 * (2 * k + (u - lag) // 2))
        elif n >= 2:
            eng.wait_ge(sems[n % 2], 16 * (n // 2))

    def all_stored(self, eng, sems, count):
        for w in range(2):
            eng.wait_ge(sems[w], 16 * ((count + 1 - w) // 2))

    def phase_gin1(self):
        nc = self.nc
        ctx, sb, ps, sem = self.scope("g1")
        W1 = XW
        with ctx:
            xd = sb("xd", [128, UN, G4, D]); m = sb("m", [128, 2, G4, 128])
            r = sb("r", [128, 2, G4, D]); rt = sb("rt", [D, GN]); ha = sb("ha", [H, GN]); ht = sb("ht", [H, GN])
            h1 = sb("h1", [128, 2, G4, H]); tmp = sb("tmp", [128, 3, CHUNKS])
            p_s = ps("p_s", (128, 2, 2, 512)); p_t, p_a, p_b, p_h = (ps(n) for n in ("p_t", "p_a", "p_b", "p_h"))
            arrived = [sem(f"arrived{u}") for u in range(UN)]
            out2 = [sem(f"out2_{u}") for u in range(2)]
            names = ("dve_m", "summed", "carried", "dve_r", "pe_t", "act_t", "pe_a", "act_a", "pe_b", "act_b", "pe_h", "dve_h", "fin", "root")
            s = {n: sem(n) for n in names}
            block = ctx.enter_context(nc.Block())
            place = lambda w, j: (w, j // 2, slice((j % 2) * XW, (j % 2) * XW + W1))

            @block.sync
            def _(sp):
                def step(k, u):
                    i = UN * k + u
                    if live(k, u, 0, AG):
                        wait(sp, s["dve_r"], i - UN + 1)
                        sp.dma_start(xd[:, u], self.slots(self.xd, k, u)).then_inc(arrived[u], 16)
                    if live(k, u, 2, AG):
                        sp.wait_ge(s["dve_h"], i - 1)
                        sp.dma_start(self.slots(self.t2, k, u, 2), h1[:, u % 2]).then_inc(out2[u % 2], 16)

                steps(sp, AG, 2, step)
                self.all_stored(sp, out2, AG)

            @block.tensor
            def _(pe):
                def step(k, u):
                    i = UN * k + u
                    w1, n1 = (u - 1) % 2, i - 1

                    def sums(j):
                        if live(k, u, 1, AG):
                            if j == 0:
                                pe.wait_ge(s["dve_m"], i)
                                wait(pe, s["dve_r"], i - 2)
                            a_, b_, c_ = place(w1, j)
                            self.sum_chunk(pe, n1, j, p_s[:, a_, b_, c_], m[:, w1],
                                           self.msgs[:, bass.ds(n1 * G4 + j, 1), :].rearrange("p o f -> p (o f)"),
                                           s["carried"], s["summed"])

                    sums(0)
                    if live(k, u, 2, AG):
                        pe.wait_ge(s["dve_r"], i - 1)
                        wait(pe, s["act_t"], i - 2)
                        for j in range(G4):
                            t = nc.tensor.transpose(p_t[:, j * D:(j + 1) * D], r[:, u % 2, j, :], self.ident[:])
                        t.then_inc(s["pe_t"], 1)
                    sums(1)
                    if live(k, u, 2, AG):
                        pe.wait_ge(s["act_t"], i - 1)
                        wait(pe, s["act_a"], i - 2)
                        nc.tensor.matmul(p_a[0:H, :], self.w1a[:], rt[:], start=True, stop=True).then_inc(s["pe_a"], 1)
                    sums(2)
                    if live(k, u, 2, AG):
                        self.hold(pe, (s["act_a"], i - 1), (s["act_b"], i - 2))
                        nc.tensor.matmul(p_b[0:H, :], self.w1b[:], ha[:], start=True, stop=True).then_inc(s["pe_b"], 1)
                    sums(3)
                    if live(k, u, 2, AG):
                        self.hold(pe, (s["dve_h"], i - 2), (s["act_b"], i - 1))
                        for j in range(G4):
                            t = nc.tensor.transpose(p_h[:, j * H:(j + 1) * H], ht[:, j * D:(j + 1) * D], self.ident[0:H, 0:H])
                        t.then_inc(s["pe_h"], 1)

                steps(pe, AG, 2, step)

            @block.scalar
            def _(act):
                def step(k, u):
                    i = UN * k + u
                    w1, n1 = (u - 1) % 2, i - 1

                    def carry(j):
                        if live(k, u, 1, AG):
                            if j == G4 and isinstance(i, int) and n1 == AG - 1:
                                return
                            a_, b_, c_ = place(w1, j - 1)
                            self.carry_chunk(act, n1, j, self.msgs[0:1, bass.ds(n1 * G4 + j, 1), :].rearrange("p o f -> p (o f)"),
                                             p_s[0:1, a_, b_, c_], s["carried"], s["summed"])

                    carry(1)
                    if live(k, u, 2, AG):
                        act.wait_ge(s["pe_t"], i - 1)
                        wait(act, s["pe_a"], i - 2)
                        nc.scalar.activation(rt[:], p_t[:], ACT.Copy).then_inc(s["act_t"], 1)
                    carry(2)
                    if live(k, u, 2, AG):
                        act.wait_ge(s["pe_a"], i - 1)
                        wait(act, s["pe_b"], i - 2)
                        nc.scalar.activation(ha[:], p_a[0:H, :], ACT.Relu, bias=self.b1a[:]).then_inc(s["act_a"], 1)
                    carry(3)
                    carry(4)
                    if live(k, u, 2, AG):
                        act.wait_ge(s["pe_b"], i - 1)
                        wait(act, s["pe_h"], i - 2)
                        nc.scalar.activation(ht[:], p_b[0:H, :], ACT.Relu, bias=self.b1b[:]).then_inc(s["act_b"], 1)

                steps(act, AG, 2, step)
                act.wait_ge(s["fin"], 2)
                nc.scalar.activation(self.dis[:], tmp[:, 1, :], ACT.Sqrt).then_inc(s["root"], 1)

            @block.vector
            def _(dve):
                def step(k, u):
                    i = UN * k + u
                    if live(k, u, 0, AG):
                        wait(dve, s["summed"], (i - 1) * G4)
                        self.select_group(m[:, u % 2], k, u, 0).then_inc(s["dve_m"], 1)
                    if live(k, u, 1, AG):
                        w = (u - 1) % 2
                        self.wait_sums(dve, i - 1, s["carried"], s["summed"])
                        dve.wait_ge(arrived[(u - 1) % UN], 16 * (k + (0 if u < 1 else 1)))
                        wait(dve, s["pe_t"], i - 2)
                        for b in range(2):
                            t = p_s[:, w, b, 0:2 * XW].rearrange("p (a f) -> p a f", a=2)
                            nc.vector.tensor_copy(self.deg[:, bass.ds((i - 1) * G4 + 2 * b, 2), :], t[:, :, D:XW])
                            last = nc.vector.tensor_tensor(r[:, w, 2 * b:2 * b + 2, :], t[:, :, 0:D],
                                                           xd[:, (u - 1) % UN, 2 * b:2 * b + 2, :], ALU.add)
                        last.then_inc(s["dve_r"], 1)
                    if live(k, u, 2, AG):
                        dve.wait_ge(s["pe_h"], i - 1)
                        self.stored(dve, out2, k, u, 2)
                        nc.vector.tensor_copy(h1[:, u % 2].rearrange("p a b -> p (a b)"), p_h[:, 0:G4 * H]).then_inc(s["dve_h"], 1)

                steps(dve, AG, 2, step)
                dve.wait_ge(s["dve_r"], AG)
                deg = self.deg[:, :, 0]
                nc.vector.tensor_scalar(tmp[:, 0, :], deg, 1.0, None, ALU.max).then_inc(s["fin"], 1)
                dve.wait_ge(s["fin"], 1)
                nc.vector.reciprocal(tmp[:, 1, :], tmp[:, 0, :]).then_inc(s["fin"], 1)
                nc.vector.tensor_scalar(tmp[:, 2, :], deg, 0.5, None, ALU.is_gt).then_inc(s["fin"], 1)
                dve.wait_ge(s["fin"], 3)
                dve.wait_ge(s["root"], 1)
                nc.vector.tensor_tensor(self.dis[:], self.dis[:], tmp[:, 2, :], ALU.mult).then_inc(s["fin"], 1)
                for l in range(3):
                    nc.vector.tensor_tensor(self.deg[:, :, 1 + l], self.deg[:, :, 1 + l], tmp[:, 1, :], ALU.mult).then_inc(s["fin"], 1)

    def phase_gin2(self):
        nc = self.nc
        ctx, sb, ps, sem = self.scope("g2")
        with ctx:
            ring = sb("ring", [128, UN, G4, H]); hs = sb("hs", [128, UN, G4, H]); xd = sb("xd", [128, UN, G4, D])
            m = sb("m", [128, 2, G4, 128]); r = sb("r", [128, 2, G4, H]); rt = sb("rt", [H, GN])
            hh = sb("hh", [D, 2, GN]); y = sb("y", [128, 2, G4, D]); x1 = sb("x1", [128, 2, G4, D])
            st = sb("st", [128, G4, 6]); mv = sb("mv", [128, 2, G4, 2])
            inv = sb("inv", [128, 2, G4]); rs = sb("rs", [128, 2, G4]); nb = sb("nb", [128, 2, G4])
            p_s = [ps(f"p_s{w}") for w in range(2)]
            p_t, p_c0, p_c1, p_o = (ps(n) for n in ("p_t", "p_c0", "p_c1", "p_o"))
            garr = [sem(f"garr{u}") for u in range(UN)]
            arrived = [sem(f"arrived{u}") for u in range(UN)]
            arrivedx = [sem(f"arrivedx{u}") for u in range(UN)]
            out3 = [sem(f"out3_{u}") for u in range(2)]
            names = ("dve_m", "summed", "carried", "dve_r", "pe_t", "act_t", "pe_c", "act_c", "pe_o", "dve_y",
                     "dve_inv", "act_rs", "dve_nb", "act_x1", "link")
            s = {n: sem(n) for n in names}
            block = ctx.enter_context(nc.Block())

            @block.gpsimd
            def _(pool):
                self.ring_gather(nc, pool, sb, sem, self.row_i, self.t2, H, ring, garr, s["summed"])

            @block.sync
            def _(sp):
                def step(k, u):
                    i = UN * k + u
                    if live(k, u, 0, AG):
                        wait(sp, s["dve_r"], i - UN + 1)
                        sp.dma_start(hs[:, u], self.slots(self.t2, k, u)).then_inc(arrived[u], 16)
                        wait(sp, s["dve_y"], i - UN + 1)
                        sp.dma_start(xd[:, u], self.slots(self.xd, k, u)).then_inc(arrivedx[u], 16)
                    if live(k, u, 3, AG):
                        w = (u - 3) % 2
                        sp.wait_ge(s["act_x1"], i - 2)
                        sp.dma_start(self.slots(self.t3, k, u, 3), x1[:, w]).then_inc(out3[w], 16)

                steps(sp, AG, 3, step)
                self.all_stored(sp, out3, AG)

            @block.tensor
            def _(pe):
                def step(k, u):
                    i = UN * k + u
                    w1, n1 = (u - 1) % 2, i - 1

                    def sums(j):
                        if live(k, u, 1, AG):
                            if j == 0:
                                pe.wait_ge(s["dve_m"], i)
                                pe.wait_ge(garr[(u - 1) % UN], 16 * G4 * (k + (0 if u < 1 else 1)))
                                wait(pe, s["dve_r"], i - 2)
                            self.sum_chunk(pe, n1, j, p_s[w1][:, j * H:(j + 1) * H], m[:, w1],
                                           ring[:, (u - 1) % UN, j, :], s["carried"], s["summed"])

                    sums(0)
                    if live(k, u, 2, AG):
                        self.hold(pe, (s["dve_r"], i - 1), (s["act_t"], i - 2))
                        for j in range(G4):
                            t = nc.tensor.transpose(p_t[0:H, j * D:(j + 1) * D], r[:, u % 2, j, :], self.ident[:])
                        t.then_inc(s["pe_t"], 1)
                    sums(1)
                    if live(k, u, 2, AG):
                        pe.wait_ge(s["act_t"], i - 1)
                        wait(pe, s["act_c"], 2 * (i - 2))
                        for t, bank in enumerate((p_c0, p_c1)):
                            nc.tensor.matmul(bank[:], self.w2a[:, t * D:(t + 1) * D], rt[:], start=True, stop=True).then_inc(s["pe_c"], 1)
                    sums(2)
                    sums(3)
                    if live(k, u, 2, AG):
                        pe.wait_ge(s["act_c"], 2 * (i - 1))
                        wait(pe, s["dve_y"], i - 2)
                        for j in range(G4):
                            for t in range(2):
                                mm = nc.tensor.matmul(p_o[:, j * D:(j + 1) * D], hh[:, t, j * D:(j + 1) * D],
                                                      self.wc[:, t, :], start=(t == 0), stop=(t == 1))
                        mm.then_inc(s["pe_o"], 1)

                steps(pe, AG, 3, step)

            @block.scalar
            def _(act):
                def step(k, u):
                    i = UN * k + u
                    w1, n1 = (u - 1) % 2, i - 1

                    def carry(j):
                        if live(k, u, 1, AG):
                            if j == G4 and isinstance(i, int) and n1 == AG - 1:
                                return
                            if j == G4:
                                act.wait_ge(garr[u], 16 * G4 * (k + 1))
                            if j == 1:
                                act.wait_ge(garr[(u - 1) % UN], 16 * G4 * (k + (0 if u < 1 else 1)))
                            self.carry_chunk(act, n1, j, ring[0:1, (u - 1 + j // G4) % UN, j % G4, :],
                                             p_s[w1][0:1, (j - 1) * H:j * H], s["carried"], s["summed"])

                    carry(1)
                    if live(k, u, 2, AG):
                        act.wait_ge(s["pe_t"], i - 1)
                        wait(act, s["pe_c"], 2 * (i - 2))
                        nc.scalar.activation(rt[:], p_t[0:H, :], ACT.Copy).then_inc(s["act_t"], 1)
                    carry(2)
                    if live(k, u, 2, AG):
                        for t, bank in enumerate((p_c0, p_c1)):
                            act.wait_ge(s["pe_c"], 2 * (i - 2) + t + 1)
                            wait(act, s["pe_o"], i - 2)
                            nc.scalar.activation(hh[:, t, :], bank[:], ACT.Relu, bias=self.b2a[:, t:t + 1]).then_inc(s["act_c"], 1)
                            if t == 0:
                                carry(3)
                    else:
                        carry(3)
                    carry(4)
                    if live(k, u, 3, AG):
                        w = (u - 3) % 2
                        act.wait_ge(s["dve_nb"], i - 2)
                        self.stored(act, out3, k, u, 3)
                        self.norm_apply(x1[:, w], y[:, w], rs[:, w], nb[:, w]).then_inc(s["act_x1"], 1)
                    if live(k, u, 2, AG):
                        w = u % 2
                        act.wait_ge(s["dve_inv"], i - 1)
                        nc.scalar.activation(rs[:, w], inv[:, w], ACT.Sqrt).then_inc(s["act_rs"], 1)

                steps(act, AG, 3, step)

            @block.vector
            def _(dve):
                link = Chain(dve, s["link"], 4)

                def step(k, u):
                    i = UN * k + u
                    if live(k, u, 3, AG):
                        w = (u - 3) % 2
                        dve.wait_ge(s["act_rs"], i - 2)
                        self.norm_shift(mv[:, w], rs[:, w], nb[:, w]).then_inc(s["dve_nb"], 1)
                    if live(k, u, 0, AG):
                        wait(dve, s["summed"], (i - 1) * G4)
                        self.select_group(m[:, u % 2], k, u, 0).then_inc(s["dve_m"], 1)
                    if live(k, u, 1, AG):
                        w = (u - 1) % 2
                        self.wait_sums(dve, i - 1, s["carried"], s["summed"])
                        dve.wait_ge(arrived[(u - 1) % UN], 16 * (k + (0 if u < 1 else 1)))
                        wait(dve, s["pe_t"], i - 2)
                        nc.vector.tensor_tensor(r[:, w].rearrange("p a b -> p (a b)"), p_s[w][:, 0:G4 * H],
                                                hs[:, (u - 1) % UN].rearrange("p a b -> p (a b)"), ALU.add).then_inc(s["dve_r"], 1)
                    if live(k, u, 2, AG):
                        w = u % 2
                        link.group(i - 2)
                        dve.wait_ge(s["pe_o"], i - 1)
                        dve.wait_ge(arrivedx[(u - 2) % UN], 16 * (k + (0 if u < 2 else 1)))
                        wait(dve, s["act_x1"], i - 3)
                        nc.vector.tensor_tensor(y[:, w].rearrange("p a b -> p (a b)"), p_o[:],
                                                xd[:, (u - 2) % UN].rearrange("p a b -> p (a b)"), ALU.add).then_inc(s["dve_y"], 1)
                        dve.wait_ge(s["dve_y"], i - 1)
                        link(nc.vector.tensor_tensor(y[:, w], y[:, w], self.each(self.bc[:]), ALU.add))
                        self.norm_stats(lambda j: y[:, w, j, :], st, mv[:, w], link)
                        self.norm_inverse(mv[:, w], inv[:, w], link).then_inc(s["dve_inv"], 1)

                steps(dve, AG, 3, step)

    def phase_rgcn(self):
        nc = self.nc
        ctx, sb, ps, sem = self.scope("rg")
        with ctx:
            ring = sb("ring", [128, UN, G4, D]); x1 = sb("x1", [128, UN, G4, D])
            gt = sb("gt", [D, 2, GN]); mg = sb("mg", [128, 2, G4, D]); m = sb("m", [128, 2, G4, 128])
            r = sb("r", [128, 2, G4, D]); x2 = sb("x2", [128, 2, G4, D]); z = sb("z", [128, 2, G4, D])
            st = sb("st", [128, G4, 6]); mv = sb("mv", [128, 2, G4, 2])
            inv = sb("inv", [128, 2, G4]); rs = sb("rs", [128, 2, G4]); nb = sb("nb", [128, 2, G4])
            p_t = ps("p_t"); p_b = [ps(f"p_b{j}") for j in range(G4)]; p_s = [ps(f"p_s{w}") for w in range(2)]
            garr = [sem(f"garr{u}") for u in range(UN)]
            arrived = [sem(f"arrived{u}") for u in range(UN)]
            outx = [sem(f"outx_{u}") for u in range(2)]; outz = [sem(f"outz_{u}") for u in range(2)]
            names = ("pe_t", "act_t", "pe_b", "act_m", "dve_part", "dve_m", "summed", "carried", "dve_r",
                     "dve_inv", "act_rs", "dve_nb", "act_x2", "dve_z", "link")
            s = {n: sem(n) for n in names}
            block = ctx.enter_context(nc.Block())

            @block.gpsimd
            def _(pool):
                stage = sb("g_stage", [128, UN, G4], I32)
                staged = sem("g_staged")

                def step(k, u):
                    def freed(k, u):
                        return ((s["pe_t"], UN * k + u - UN + 1),)
                    self.gather_group(pool, k, u, AG, self.row_i, stage, staged, self.t3, ring, D, garr, freed)

                steps(pool, AG, 0, step)

            @block.sync
            def _(sp):
                def step(k, u):
                    i = UN * k + u
                    if live(k, u, 0, AG):
                        wait(sp, s["dve_r"], i - UN + 1)
                        sp.dma_start(x1[:, u], self.slots(self.t3, k, u)).then_inc(arrived[u], 16)
                    if live(k, u, 3, AG):
                        w = (u - 3) % 2
                        sp.wait_ge(s["act_x2"], i - 2)
                        sp.dma_start(self.slots(self.x2, k, u, 3), x2[:, w]).then_inc(outx[w], 16)
                        sp.wait_ge(s["dve_z"], i - 2)
                        sp.dma_start(self.slots(self.t4, k, u, 3), z[:, w]).then_inc(outz[w], 16)

                steps(sp, AG, 3, step)
                self.all_stored(sp, outx, AG)
                self.all_stored(sp, outz, AG)

            @block.tensor
            def _(pe):
                def step(k, u):
                    i = UN * k + u
                    if live(k, u, 0, AG):
                        pe.wait_ge(garr[u], 16 * G4 * (k + 1))
                        wait(pe, s["act_t"], i)
                        for j in range(G4):
                            t = nc.tensor.transpose(p_t[:, j * D:(j + 1) * D], ring[:, u, j, :], self.ident[:])
                        t.then_inc(s["pe_t"], 1)
                    for j in range(G4):
                        if live(k, u, 0, AG):
                            if j == 0:
                                pe.wait_ge(s["act_t"], i + 1)
                            wait(pe, s["dve_part"], (i - 1) * G4 + j + 1)
                            nc.tensor.matmul(p_b[j][:], gt[:, u % 2, j * D:(j + 1) * D],
                                             self.bases[:].rearrange("i b o -> i (b o)"),
                                             start=True, stop=True).then_inc(s["pe_b"], 1)
                        if live(k, u, 1, AG):
                            w = (u - 1) % 2
                            if j == 0:
                                pe.wait_ge(s["dve_m"], i)
                                pe.wait_ge(s["dve_part"], i * G4)
                                wait(pe, s["dve_r"], i - 2)
                            self.sum_chunk(pe, i - 1, j, p_s[w][:, j * D:(j + 1) * D], m[:, w], mg[:, w, j, :],
                                           s["carried"], s["summed"])

                steps(pe, AG, 1, step)

            @block.scalar
            def _(act):
                def step(k, u):
                    i = UN * k + u

                    def carry(j):
                        if live(k, u, 1, AG):
                            n1 = i - 1
                            if isinstance(i, int) and j == G4 and n1 == AG - 1:
                                return
                            w = (u - 1) % 2
                            if j == G4:
                                act.wait_ge(s["dve_part"], (i + 1) * G4)
                            if j == 1:
                                act.wait_ge(s["dve_part"], i * G4)
                            self.carry_chunk(act, n1, j, mg[0:1, (w + j // G4) % 2, j % G4, :],
                                             p_s[w][0:1, (j - 1) * D:j * D], s["carried"], s["summed"])

                    if live(k, u, 0, AG):
                        act.wait_ge(s["pe_t"], i + 1)
                        wait(act, s["pe_b"], (i - 1) * G4)
                        nc.scalar.activation(gt[:, u % 2, :], p_t[:], ACT.Copy).then_inc(s["act_t"], 1)
                    carry(1)
                    if live(k, u, 3, AG):
                        w = (u - 3) % 2
                        act.wait_ge(s["dve_nb"], i - 2)
                        self.stored(act, outx, k, u, 3)
                        wait(act, s["dve_z"], i - 4)
                        self.norm_apply(x2[:, w], r[:, w], rs[:, w], nb[:, w]).then_inc(s["act_x2"], 1)
                    for j in range(G4):
                        if live(k, u, 0, AG):
                            act.wait_ge(s["pe_b"], i * G4 + j + 1)
                            wait(act, s["summed"], (i - 1) * G4)
                            nc.scalar.activation(mg[:, u % 2, j, :], p_b[j][:, 0:D], ACT.Copy,
                                                 scale=self.coef[:, 0, bass.ds(i * G4 + j, 1)]).then_inc(s["act_m"], 1)
                        if j == 1:
                            carry(2)
                        if j == 3:
                            carry(3)
                    carry(4)
                    if live(k, u, 2, AG):
                        w = u % 2
                        act.wait_ge(s["dve_inv"], i - 1)
                        nc.scalar.activation(rs[:, w], inv[:, w], ACT.Sqrt).then_inc(s["act_rs"], 1)

                steps(act, AG, 3, step)

            @block.vector
            def _(dve):
                link = Chain(dve, s["link"], 3)
                parts = Chain(dve, sem("parts"), 2)

                def step(k, u):
                    i = UN * k + u
                    if live(k, u, 3, AG):
                        w = (u - 3) % 2
                        dve.wait_ge(s["act_rs"], i - 2)
                        self.norm_shift(mv[:, w], rs[:, w], nb[:, w]).then_inc(s["dve_nb"], 1)
                    if live(k, u, 0, AG):
                        wait(dve, s["summed"], (i - 1) * G4)
                        self.select_group(m[:, u % 2], k, u, 0).then_inc(s["dve_m"], 1)
                        parts.group(i)
                        for b in range(1, 4):
                            for j in range(G4):
                                if b == 1:
                                    dve.wait_ge(s["act_m"], i * G4 + j + 1)
                                last = nc.vector.scalar_tensor_tensor(
                                    out=mg[:, u % 2, j, :], in0=p_b[j][:, b * D:(b + 1) * D],
                                    scalar=self.coef[:, b, bass.ds(i * G4 + j, 1)], in1=mg[:, u % 2, j, :],
                                    op0=ALU.mult, op1=ALU.add)
                                if b == 3:
                                    last.then_inc(s["dve_part"], 1)
                            if b < 3:
                                parts(last)
                    if live(k, u, 1, AG):
                        w = (u - 1) % 2
                        link.group(i - 1)
                        self.wait_sums(dve, i - 1, s["carried"], s["summed"])
                        dve.wait_ge(arrived[(u - 1) % UN], 16 * (k + (0 if u < 1 else 1)))
                        wait(dve, s["act_x2"], i - 2)
                        nc.vector.tensor_tensor(r[:, w].rearrange("p a b -> p (a b)"), p_s[w][:],
                                                x1[:, (u - 1) % UN].rearrange("p a b -> p (a b)"), ALU.add).then_inc(s["dve_r"], 1)
                        dve.wait_ge(s["dve_r"], i)
                        self.norm_stats(lambda j: r[:, w, j, :], st, mv[:, w], link)
                        self.norm_inverse(mv[:, w], inv[:, w], link).then_inc(s["dve_inv"], 1)
                    if live(k, u, 3, AG):
                        w = (u - 3) % 2
                        dve.wait_ge(s["act_x2"], i - 2)
                        self.stored(dve, outz, k, u, 3)
                        dis = self.dis[:, bass.ds((i - 3) * G4, G4)].rearrange("p (c o) -> p c o", o=1).to_broadcast([128, G4, D])
                        nc.vector.tensor_tensor(z[:, w], x2[:, w], dis, ALU.mult).then_inc(s["dve_z"], 1)

                steps(dve, AG, 3, step)

    def gat_rows(self, xt, p_h, layer):
        for j in range(G4):
            last = self.nc.tensor.matmul(p_h[:, j // 2, (j % 2) * XW:(j % 2 + 1) * XW], xt[:, j * D:(j + 1) * D],
                                         self.wx[:, layer, :], start=True, stop=True)
        return last

    def gat_rows_out(self, rows, p_h, layer, group=None):
        for b in range(2):
            if group is not None:
                self.nc.vector.tensor_tensor(self.att_s[:, bass.ds(group * G4 + 2 * b, 2), :],
                                             p_h[:, b, 0:2 * XW].rearrange("p (b f) -> p b f", b=2)[:, :, D:D + 3],
                                             self.cx2(layer)[:, :, D:D + 3], ALU.add)
            last = self.nc.vector.tensor_tensor(rows[:, 2 * b:2 * b + 2, :],
                                                p_h[:, b, 0:2 * XW].rearrange("p (b f) -> p b f", b=2),
                                                self.cx2(layer), ALU.add)
        return last

    def phase_gcn(self):
        nc = self.nc
        ctx, sb, ps, sem = self.scope("gc")
        with ctx:
            ring = sb("ring", [128, UN, G4, D]); x2 = sb("x2", [128, UN, G4, D])
            m = sb("m", [128, 2, G4, 128]); g = sb("g", [128, 2, G4, D]); gt = sb("gt", [D, GN])
            v = sb("v", [128, 2, G4, D]); x3 = sb("x3", [128, 2, G4, D]); x3t = sb("x3t", [D, GN])
            h0 = sb("h0", [128, 2, G4, XW])
            st = sb("st", [128, G4, 6]); mv = sb("mv", [128, 2, G4, 2])
            inv = sb("inv", [128, 2, G4]); rs = sb("rs", [128, 2, G4]); nb = sb("nb", [128, 2, G4])
            p_s = [ps(f"p_s{w}") for w in range(2)]; p_t, p_g, p_x = ps("p_t"), ps("p_g"), ps("p_x")
            p_h = ps("p_h", (128, 2, 512))
            garr = [sem(f"garr{u}") for u in range(UN)]
            arrived = [sem(f"arrived{u}") for u in range(UN)]
            outx = [sem(f"outx_{u}") for u in range(2)]; outh = [sem(f"outh_{u}") for u in range(2)]
            names = ("dve_m", "summed", "carried", "dve_g", "pe_t", "act_t", "pe_g", "dve_v", "dve_inv", "act_rs",
                     "dve_nb", "act_x3", "pe_x", "act_x", "pe_h", "dve_h", "link")
            s = {n: sem(n) for n in names}
            block = ctx.enter_context(nc.Block())

            @block.gpsimd
            def _(pool):
                self.ring_gather(nc, pool, sb, sem, self.row4_i, self.t4, D, ring, garr, s["summed"])

            @block.sync
            def _(sp):
                def step(k, u):
                    i = UN * k + u
                    if live(k, u, 0, AG):
                        wait(sp, s["dve_v"], i - UN + 1)
                        sp.dma_start(x2[:, u], self.slots(self.x2, k, u)).then_inc(arrived[u], 16)
                    if live(k, u, 3, AG):
                        w = (u - 3) % 2
                        sp.wait_ge(s["act_x3"], i - 2)
                        sp.dma_start(self.slots(self.x3, k, u, 3), x3[:, w]).then_inc(outx[w], 16)
                        sp.wait_ge(s["dve_h"], i - 2)
                        sp.dma_start(self.slots(self.th[0], k, u, 3), h0[:, w]).then_inc(outh[w], 16)

                steps(sp, AG, 3, step)
                self.all_stored(sp, outx, AG)
                self.all_stored(sp, outh, AG)

            @block.tensor
            def _(pe):
                def step(k, u):
                    i = UN * k + u

                    def sums(j):
                        if live(k, u, 1, AG):
                            w = (u - 1) % 2
                            if j == 0:
                                pe.wait_ge(s["dve_m"], i)
                                pe.wait_ge(garr[(u - 1) % UN], 16 * G4 * (k + (0 if u < 1 else 1)))
                                wait(pe, s["dve_g"], i - 2)
                            self.sum_chunk(pe, i - 1, j, p_s[w][:, j * D:(j + 1) * D], m[:, w],
                                           ring[:, (u - 1) % UN, j, :], s["carried"], s["summed"])

                    sums(0)
                    if live(k, u, 2, AG):
                        pe.wait_ge(s["dve_g"], i - 1)
                        wait(pe, s["act_t"], i - 2)
                        for j in range(G4):
                            t = nc.tensor.transpose(p_t[:, j * D:(j + 1) * D], g[:, u % 2, j, :], self.ident[:])
                        t.then_inc(s["pe_t"], 1)
                    sums(1)
                    if live(k, u, 3, AG):
                        pe.wait_ge(s["act_x3"], i - 2)
                        wait(pe, s["act_x"], i - 3)
                        for j in range(G4):
                            t = nc.tensor.transpose(p_x[:, j * D:(j + 1) * D], x3[:, (u - 3) % 2, j, :], self.ident[:])
                        t.then_inc(s["pe_x"], 1)
                    sums(2)
                    if live(k, u, 2, AG):
                        pe.wait_ge(s["act_t"], i - 1)
                        wait(pe, s["dve_v"], i - 2)
                        for j in range(G4):
                            t = nc.tensor.matmul(p_g[:, j * D:(j + 1) * D], gt[:, j * D:(j + 1) * D], self.wg[:],
                                                 start=True, stop=True)
                        t.then_inc(s["pe_g"], 1)
                    sums(3)
                    if live(k, u, 3, AG):
                        pe.wait_ge(s["act_x"], i - 2)
                        wait(pe, s["dve_h"], i - 3)
                        self.gat_rows(x3t, p_h, 0).then_inc(s["pe_h"], 1)

                steps(pe, AG, 3, step)

            @block.scalar
            def _(act):
                def step(k, u):
                    i = UN * k + u

                    def carry(j):
                        if live(k, u, 1, AG):
                            if isinstance(i, int) and j == G4 and i == AG:
                                return
                            if j == G4:
                                act.wait_ge(garr[u], 16 * G4 * (k + 1))
                            if j == 1:
                                act.wait_ge(garr[(u - 1) % UN], 16 * G4 * (k + (0 if u < 1 else 1)))
                            self.carry_chunk(act, i - 1, j, ring[0:1, (u - 1 + j // G4) % UN, j % G4, :],
                                             p_s[(u - 1) % 2][0:1, (j - 1) * D:j * D], s["carried"], s["summed"])

                    carry(1)
                    if live(k, u, 3, AG):
                        w = (u - 3) % 2
                        act.wait_ge(s["dve_nb"], i - 2)
                        self.stored(act, outx, k, u, 3)
                        wait(act, s["pe_x"], i - 4)
                        self.norm_apply(x3[:, w], v[:, w], rs[:, w], nb[:, w]).then_inc(s["act_x3"], 1)
                    carry(2)
                    if live(k, u, 2, AG):
                        act.wait_ge(s["pe_t"], i - 1)
                        wait(act, s["pe_g"], i - 2)
                        nc.scalar.activation(gt[:], p_t[:], ACT.Copy).then_inc(s["act_t"], 1)
                    carry(3)
                    if live(k, u, 3, AG):
                        act.wait_ge(s["pe_x"], i - 2)
                        wait(act, s["pe_h"], i - 3)
                        nc.scalar.activation(x3t[:], p_x[:], ACT.Copy).then_inc(s["act_x"], 1)
                    carry(4)
                    if live(k, u, 2, AG):
                        w = u % 2
                        act.wait_ge(s["dve_inv"], i - 1)
                        nc.scalar.activation(rs[:, w], inv[:, w], ACT.Sqrt).then_inc(s["act_rs"], 1)

                steps(act, AG, 3, step)

            @block.vector
            def _(dve):
                link = Chain(dve, s["link"], 4)

                def step(k, u):
                    i = UN * k + u
                    if live(k, u, 3, AG):
                        w = (u - 3) % 2
                        dve.wait_ge(s["act_rs"], i - 2)
                        self.norm_shift(mv[:, w], rs[:, w], nb[:, w]).then_inc(s["dve_nb"], 1)
                    if live(k, u, 0, AG):
                        wait(dve, s["summed"], (i - 1) * G4)
                        self.select_group(m[:, u % 2], k, u, 0).then_inc(s["dve_m"], 1)
                    if live(k, u, 1, AG):
                        w = (u - 1) % 2
                        self.wait_sums(dve, i - 1, s["carried"], s["summed"])
                        wait(dve, s["pe_t"], i - 2)
                        dis = self.dis[:, bass.ds((i - 1) * G4, G4)].rearrange("p (c o) -> p c o", o=1).to_broadcast([128, G4, D])
                        nc.vector.tensor_tensor(g[:, w], p_s[w][:].rearrange("p (a b) -> p a b", a=G4), dis,
                                                ALU.mult).then_inc(s["dve_g"], 1)
                    if live(k, u, 2, AG):
                        w = u % 2
                        link.group(i - 2)
                        dve.wait_ge(s["pe_g"], i - 1)
                        dve.wait_ge(arrived[(u - 2) % UN], 16 * (k + (0 if u < 2 else 1)))
                        wait(dve, s["act_x3"], i - 3)
                        nc.vector.tensor_tensor(v[:, w].rearrange("p a b -> p (a b)"), p_g[:],
                                                x2[:, (u - 2) % UN].rearrange("p a b -> p (a b)"), ALU.add).then_inc(s["dve_v"], 1)
                        dve.wait_ge(s["dve_v"], i - 1)
                        link(nc.vector.tensor_tensor(v[:, w], v[:, w], self.each(self.bg[:]), ALU.add))
                        self.norm_stats(lambda j: v[:, w, j, :], st, mv[:, w], link)
                        self.norm_inverse(mv[:, w], inv[:, w], link).then_inc(s["dve_inv"], 1)
                    if live(k, u, 3, AG):
                        w = (u - 3) % 2
                        dve.wait_ge(s["pe_h"], i - 2)
                        self.stored(dve, outh, k, u, 3)
                        self.gat_rows_out(h0[:, w], p_h, 0, i - 3).then_inc(s["dve_h"], 1)

                steps(dve, AG, 3, step)

    def phase_gat_nodes(self, layer):
        nc = self.nc
        last_layer = layer == 2
        ctx, sb, ps, sem = self.scope(f"n{layer}")
        with ctx:
            h = sb("h", [128, UN, G4, XW]); o = sb("o", [128, 2, G4, D]); n_ = sb("n", [128, 2, G4, D])
            st = sb("st", [128, G4, 6]); mv = sb("mv", [128, 2, G4, 2])
            inv = sb("inv", [128, 2, G4]); rs = sb("rs", [128, 2, G4]); nb = sb("nb", [128, 2, G4])
            arrived = [sem(f"arrived{u}") for u in range(UN)]
            outs = [sem(f"outs{u}") for u in range(2)]
            got = sem("got")
            names = ["dve_o", "dve_inv", "act_rs", "dve_nb", "act_n", "link"]
            if last_layer:
                x3 = sb("x3", [128, UN, G4, D]); y = sb("y", [128, 2, G4, D]); res = sb("res", [128, 2, G4, D])
                st2 = sb("st2", [128, G4, 6]); mv2 = sb("mv2", [128, 2, G4, 2])
                inv2 = sb("inv2", [128, 2, G4]); rs2 = sb("rs2", [128, 2, G4]); nb2 = sb("nb2", [128, 2, G4])
                arrivedx = [sem(f"arrivedx{u}") for u in range(UN)]
                names += ["dve_y", "dve_inv2", "act_rs2", "dve_nb2", "act_res", "link2"]
            else:
                nt = sb("nt", [D, GN]); hn = sb("hn", [128, 2, G4, XW])
                p_t = ps("p_t"); p_h = ps("p_h", (128, 2, 512))
                names += ["pe_t", "act_t", "pe_h", "dve_h"]
            s = {name: sem(name) for name in names}
            last_rows = (N - (DG - 1) * GN) // G4
            block = ctx.enter_context(nc.Block())

            @block.gpsimd
            def _(pool):
                self.resident_gather(self.row_i, self.th[layer], XW, got)
                pool.wait_ge(got, 16 * CHUNKS)

            @block.sync
            def _(sp):
                def step(k, u):
                    i = UN * k + u
                    if live(k, u, 0, DG):
                        wait(sp, s["dve_o"], i - UN + 1)
                        sp.dma_start(h[:, u], self.nodes(self.th[layer], k, u)).then_inc(arrived[u], 16)
                        if last_layer:
                            wait(sp, s["dve_y"], i - UN + 1)
                            sp.dma_start(x3[:, u], self.nodes(self.x3, k, u)).then_inc(arrivedx[u], 16)
                    if live(k, u, 2, DG) and not last_layer:
                        w = u % 2
                        sp.wait_ge(s["dve_h"], i - 1)
                        sp.dma_start(self.nodes(self.th[layer + 1], k, u, 2), hn[:, w]).then_inc(outs[w], 16)
                    if live(k, u, 3, DG) and last_layer:
                        w = (u - 3) % 2
                        self.hold(sp, (s["act_res"], i - 2))
                        if isinstance(i, int) and i - 3 == DG - 1:
                            sp.dma_start(self.out[(DG - 1) * GN:N, :].rearrange("(p j) f -> p j f", j=G4),
                                         res[0:last_rows, w]).then_inc(outs[w], 16)
                        else:
                            t = self.out[0:(DG - 1) * GN, :].rearrange("(g p j) f -> g p j f", p=128, j=G4)
                            sp.dma_start(t[bass.ds(i - 3, 1)].rearrange("g p j f -> p (g j) f"), res[:, w]).then_inc(outs[w], 16)

                steps(sp, DG, 3, step)
                self.all_stored(sp, outs, DG)

            if not last_layer:
                @block.tensor
                def _(pe):
                    def step(k, u):
                        i = UN * k + u
                        if live(k, u, 1, DG):
                            w = (u - 1) % 2
                            pe.wait_ge(s["act_n"], i)
                            wait(pe, s["act_t"], i - 1)
                            for j in range(G4):
                                t = nc.tensor.transpose(p_t[:, j * D:(j + 1) * D], n_[:, w, j, :], self.ident[:])
                            t.then_inc(s["pe_t"], 1)
                            pe.wait_ge(s["act_t"], i)
                            wait(pe, s["dve_h"], i - 1)
                            self.gat_rows(nt, p_h, layer + 1).then_inc(s["pe_h"], 1)

                    steps(pe, DG, 1, step)

            @block.scalar
            def _(act):
                def step(k, u):
                    i = UN * k + u
                    if live(k, u, 1, DG):
                        w = (u - 1) % 2
                        act.wait_ge(s["dve_nb"], i)
                        wait(act, s["dve_y"] if last_layer else s["pe_t"], i - 2)
                        self.norm_apply(n_[:, w], o[:, w], rs[:, w], nb[:, w]).then_inc(s["act_n"], 1)
                        if not last_layer:
                            act.wait_ge(s["pe_t"], i)
                            wait(act, s["pe_h"], i - 1)
                            nc.scalar.activation(nt[:], p_t[:], ACT.Copy).then_inc(s["act_t"], 1)
                    if live(k, u, 2, DG) and last_layer:
                        w = u % 2
                        act.wait_ge(s["dve_nb2"], i - 1)
                        self.stored(act, outs, k, u, 2)
                        self.norm_apply(res[:, w], y[:, w], rs2[:, w], nb2[:, w]).then_inc(s["act_res"], 1)
                    if live(k, u, 0, DG):
                        act.wait_ge(s["dve_inv"], i + 1)
                        nc.scalar.activation(rs[:, u % 2], inv[:, u % 2], ACT.Sqrt).then_inc(s["act_rs"], 1)
                    if live(k, u, 1, DG) and last_layer:
                        w = (u - 1) % 2
                        act.wait_ge(s["dve_inv2"], i)
                        nc.scalar.activation(rs2[:, w], inv2[:, w], ACT.Sqrt).then_inc(s["act_rs2"], 1)

                steps(act, DG, 2, step)

            @block.vector
            def _(dve):
                link = Chain(dve, s["link"], 3)
                link2 = Chain(dve, s["link2"], 5) if last_layer else None

                def step(k, u):
                    i = UN * k + u
                    if live(k, u, 1, DG):
                        w = (u - 1) % 2
                        dve.wait_ge(s["act_rs"], i)
                        self.norm_shift(mv[:, w], rs[:, w], nb[:, w]).then_inc(s["dve_nb"], 1)
                    if live(k, u, 2, DG) and last_layer:
                        w = u % 2
                        dve.wait_ge(s["act_rs2"], i - 1)
                        self.norm_shift(mv2[:, w], rs2[:, w], nb2[:, w]).then_inc(s["dve_nb2"], 1)
                    if live(k, u, 0, DG):
                        w = u % 2
                        link.group(i)
                        dve.wait_ge(arrived[u], 16 * (k + 1))
                        wait(dve, s["act_n"], i - 1)
                        nc.vector.tensor_tensor(o[:, w], h[:, u, :, 0:D], self.each(self.bl[:, layer, :]), ALU.add).then_inc(s["dve_o"], 1)
                        dve.wait_ge(s["dve_o"], i + 1)
                        self.norm_stats(lambda j: o[:, w, j, :], st, mv[:, w], link)
                        self.norm_inverse(mv[:, w], inv[:, w], link).then_inc(s["dve_inv"], 1)
                    if live(k, u, 1, DG):
                        w = (u - 1) % 2
                        if last_layer:
                            link2.group(i - 1)
                            dve.wait_ge(s["act_n"], i)
                            dve.wait_ge(arrivedx[(u - 1) % UN], 16 * (k + (0 if u < 1 else 1)))
                            wait(dve, s["act_res"], i - 2)
                            link2(nc.vector.tensor_tensor(y[:, w], n_[:, w], self.each(self.gam[:]), ALU.mult))
                            link2(nc.vector.tensor_tensor(y[:, w], y[:, w], self.each(self.bet[:]), ALU.add))
                            nc.vector.tensor_tensor(y[:, w], y[:, w], x3[:, (u - 1) % UN], ALU.add).then_inc(s["dve_y"], 1)
                            dve.wait_ge(s["dve_y"], i)
                            self.norm_stats(lambda j: y[:, w, j, :], st2, mv2[:, w], link2)
                            self.norm_inverse(mv2[:, w], inv2[:, w], link2).then_inc(s["dve_inv2"], 1)
                        else:
                            dve.wait_ge(s["pe_h"], i)
                            self.stored(dve, outs, k, u, 1)
                            self.gat_rows_out(hn[:, w], p_h, layer + 1).then_inc(s["dve_h"], 1)

                steps(dve, DG, 2, step)

    def phase_gat_weights(self, layer):
        nc = self.nc
        ctx, sb, ps, sem = self.scope(f"s{layer}")
        with ctx:
            own = sb("own", [128, CHUNKS]); col = sb("col", [ROWP, 3, 256])
            b = sb("b", [ROWP, 256]); mx = sb("mx", [ROWP, 256]); z = sb("z", [ROWP, 256])
            tmp = sb("tmp", [ROWP, 2, 256]); fill = sb("fill", [ROWP, 2, 256]); ex = sb("ex", [ROWP, 2, 256])
            edge1 = sb("edge1", [1, ROWP]); run1 = sb("run1", [1, ROWP + 1]); in1 = sb("in1", [ROWP, 1])
            edge2 = sb("edge2", [1, 2, ROWP]); run2 = sb("run2", [1, 2, ROWP + 1]); in2 = sb("in2", [ROWP, 2])
            one = sb("one", [1, 1])
            p_c = ps("p_c", (128, 3, 512)); p_1 = ps("p_1"); p_2 = ps("p_2"); p_w = ps("p_w", (128, 2, 512))
            v, own_done, cols_in, last1, row1, run1_done, first2, back2, exp_in, exp_out, wide = (
                sem(n) for n in ("v", "own_done", "cols_in", "last1", "row1", "run1_done", "first2", "back2",
                                 "exp_in", "exp_out", "wide"))
            pe_last, pe_in1, pe_first, pe_in2 = (sem(n) for n in ("pe_last", "pe_in1", "pe_first", "pe_in2"))
            idp = self.ident[0:ROWP, 0:ROWP]
            block = ctx.enter_context(nc.Block())

            @block.tensor
            def _(pe):
                pe.wait_ge(own_done, 1)
                for n, t in enumerate((self.msgs[:, :, D], self.att_s[:, :, 2], own[:])):
                    for j in range(2):
                        last = nc.tensor.transpose(p_c[0:ROWP, n, j * 128:(j + 1) * 128],
                                                   t.rearrange("q (p j) -> q j p", j=2)[:, j, :], self.ident[:])
                last.then_inc(cols_in, 1)
                pe.wait_ge(last1, 1)
                nc.tensor.transpose(p_1[0:1, 0:ROWP], mx[:, 255:256], idp).then_inc(pe_last, 1)
                pe.wait_ge(run1_done, 1)
                nc.tensor.matmul(p_2[0:ROWP, 0:1], run1[0:1, 0:ROWP], one[:], start=True, stop=True).then_inc(pe_in1, 1)
                pe.wait_ge(first2, 1)
                for n in range(2):
                    last = nc.tensor.transpose(p_1[0:1, n * 128:n * 128 + ROWP], fill[:, n, 0:1], idp)
                last.then_inc(pe_first, 1)
                pe.wait_ge(back2, 1)
                for n in range(2):
                    last = nc.tensor.matmul(p_2[0:ROWP, n:n + 1], run2[0:1, n, 1:ROWP + 1], one[:], start=True, stop=True)
                last.then_inc(pe_in2, 1)
                pe.wait_ge(exp_out, 1)
                for n in range(2):
                    for j in range(2):
                        last = nc.tensor.transpose(p_w[:, n, j * ROWP:(j + 1) * ROWP], ex[:, n, j * 128:(j + 1) * 128], idp)
                last.then_inc(wide, 1)

            @block.scalar
            def _(act):
                act.wait_ge(exp_in, 1)
                nc.scalar.activation(ex[:], tmp[:], ACT.Exp).then_inc(exp_out, 1)

            @block.vector
            def _(dve):
                count = [0]

                def after(ins):
                    count[0] += 1
                    ins.then_inc(v, 1)
                    dve.wait_ge(v, count[0])

                def leaky(out, x, t):
                    after(nc.vector.tensor_scalar(t, x, 0.2, None, ALU.mult))
                    after(nc.vector.tensor_tensor(out, x, t, ALU.max))

                nc.vector.memset(one[:], 1.0).then_inc(v, 1)
                nc.vector.memset(run1[:], -BIG).then_inc(v, 1)
                nc.vector.memset(run2[:], 0.0).then_inc(v, 1)
                count[0] += 3
                after(nc.vector.tensor_tensor(own[:], self.att_s[:, :, 0], self.att_s[:, :, 2], ALU.add))
                nc.vector.tensor_tensor(own[:], own[:], self.deg[:, :, 1 + layer], ALU.add).then_inc(own_done, 1)
                dve.wait_ge(cols_in, 1)
                after(nc.vector.tensor_copy(col[:], p_c[0:ROWP, :, 0:256]))
                after(nc.vector.tensor_tensor(b[:], col[:, 0], self.edge_t[:, layer], ALU.add))
                nc.vector.tensor_tensor_scan(mx[:], self.startneg[:], b[:], -BIG, ALU.add, ALU.max).then_inc(last1, 1)
                dve.wait_ge(pe_last, 1)
                after(nc.vector.tensor_copy(edge1[:], p_1[0:1, 0:ROWP]))
                nc.vector.tensor_tensor_scan(run1[:, 1:ROWP + 1], self.flag_rows[:, 0, :], edge1[:], -BIG,
                                             ALU.add, ALU.max).then_inc(run1_done, 1)
                dve.wait_ge(pe_in1, 1)
                after(nc.vector.tensor_copy(in1[:], p_2[0:ROWP, 0:1]))
                after(nc.vector.scalar_tensor_tensor(out=mx[:], in0=self.preneg[:], scalar=in1[:], in1=mx[:],
                                                     op0=ALU.add, op1=ALU.max))
                after(nc.vector.tensor_tensor(mx[:], mx[:], col[:, 1], ALU.add))
                after(nc.vector.tensor_tensor(mx[:], mx[:], col[:, 2], ALU.max))
                leaky(z[:], mx[:], tmp[:, 0])
                after(nc.vector.tensor_tensor(tmp[:, 0], z[:], self.end[:], ALU.mult))
                after(nc.vector.tensor_tensor(tmp[:, 1], col[:, 1], self.end[:], ALU.mult))
                for n in range(2):
                    last = nc.vector.tensor_tensor_scan(fill[:, n, ::-1], self.notend[:, ::-1], tmp[:, n, ::-1], 0.0,
                                                        ALU.mult, ALU.add)
                last.then_inc(first2, 1)
                dve.wait_ge(pe_first, 1)
                after(nc.vector.tensor_copy(edge2[:], p_1[0:1, 0:256].rearrange("o (n p) -> o n p", n=2)[:, :, 0:ROWP]))
                for n in range(2):
                    last = nc.vector.tensor_tensor_scan(run2[:, n, 0:ROWP][:, ::-1], self.flag_rows[:, 1, ::-1],
                                                        edge2[:, n, ::-1], 0.0, ALU.mult, ALU.add)
                last.then_inc(back2, 1)
                dve.wait_ge(pe_in2, 1)
                after(nc.vector.tensor_copy(in2[:], p_2[0:ROWP, 0:2]))
                for n in range(2):
                    last = nc.vector.scalar_tensor_tensor(out=fill[:, n], in0=self.open[:], scalar=in2[:, n:n + 1],
                                                          in1=fill[:, n], op0=ALU.mult, op1=ALU.add)
                after(last)
                after(nc.vector.tensor_tensor(b[:], b[:], fill[:, 1], ALU.add))
                leaky(b[:], b[:], tmp[:, 0])
                leaky(col[:, 2], col[:, 2], tmp[:, 1])
                after(nc.vector.tensor_tensor(tmp[:, 0], b[:], fill[:, 0], ALU.subtract))
                nc.vector.tensor_tensor(tmp[:, 1], col[:, 2], z[:], ALU.subtract).then_inc(exp_in, 1)
                dve.wait_ge(wide, 1)
                for n, t in enumerate((self.w_edge, self.w_self)):
                    last = nc.vector.tensor_copy(t[:].rearrange("q (p j) -> q j p", j=2),
                                                 p_w[:, n, 0:CHUNKS].rearrange("q (j p) -> q j p", j=2))
                after(last)
                after(nc.vector.memset(self.w_edge[0:1, :], 1.0))

    def phase_gat_sums(self, layer):
        nc = self.nc
        last_layer = layer == 2
        ctx, sb, ps, sem = self.scope(f"a{layer}")
        with ctx:
            h = sb("h", [128, UN, G4, XW]); m = sb("m", [128, 2, G4, 128])
            t_ = sb("t", [128, G4, XW]); rden = sb("rden", [128, G4]); o = sb("o", [128, 2, G4, D])
            n_ = sb("n", [128, 2, G4, D])
            st = sb("st", [128, G4, 6]); mv = sb("mv", [128, 2, G4, 2])
            inv = sb("inv", [128, 2, G4]); rs = sb("rs", [128, 2, G4]); nb = sb("nb", [128, 2, G4])
            p_s = ps("p_s", (128, 2, 2, 512))
            arrived = [sem(f"arrived{u}") for u in range(UN)]
            outs = [sem(f"outs{u}") for u in range(UN if last_layer else 2)]
            names = ["dve_m", "summed", "carried", "dve_t", "dve_inv", "act_rs", "dve_nb", "act_n", "link"]
            if last_layer:
                x3 = sb("x3", [128, UN, G4, D]); y = sb("y", [128, 2, G4, D]); res = sb("res", [128, UN, G4, D])
                st2 = sb("st2", [128, G4, 6]); mv2 = sb("mv2", [128, 2, G4, 2])
                inv2 = sb("inv2", [128, 2, G4]); rs2 = sb("rs2", [128, 2, G4]); nb2 = sb("nb2", [128, 2, G4])
                stage = sb("stage", [128, UN, G4], I32)
                arrivedx = [sem(f"arrivedx{u}") for u in range(UN)]
                names += ["dve_y", "dve_inv2", "act_rs2", "dve_nb2", "act_res", "link2", "staged"]
            else:
                nt = sb("nt", [D, GN]); hn = sb("hn", [128, 2, G4, XW])
                p_t = ps("p_t"); p_h = ps("p_h", (128, 2, 512))
                names += ["pe_t", "act_t", "pe_h", "dve_h"]
            s = {name: sem(name) for name in names}
            place = lambda w, j: (w, j // 2, slice((j % 2) * XW, (j % 2 + 1) * XW))
            msg = lambda c: self.msgs[:, bass.ds(c, 1), :].rearrange("p o f -> p (o f)")
            block = ctx.enter_context(nc.Block())

            @block.sync
            def _(sp):
                def step(k, u):
                    i = UN * k + u
                    if live(k, u, 0, AG):
                        wait(sp, s["dve_t"], i - UN + 1)
                        sp.dma_start(h[:, u], self.slots(self.th[layer], k, u)).then_inc(arrived[u], 16)
                        if last_layer:
                            wait(sp, s["dve_y"], i - UN + 1)
                            sp.dma_start(x3[:, u], self.slots(self.x3, k, u)).then_inc(arrivedx[u], 16)
                    if live(k, u, 3, AG) and not last_layer:
                        w = (u - 3) % 2
                        sp.wait_ge(s["dve_h"], i - 2)
                        sp.dma_start(self.slots(self.th[layer + 1], k, u, 3), hn[:, w]).then_inc(outs[w], 16)

                steps(sp, AG, 3, step)
                if not last_layer:
                    self.all_stored(sp, outs, AG)

            if last_layer:
                @block.gpsimd
                def _(pool):
                    def step(k, u):
                        i = UN * k + u
                        if live(k, u, 3, AG):
                            n, w = i - 3, (u - 3) % UN
                            kk = k - (1 if u < 3 else 0)
                            if not isinstance(i, int) or n >= UN:
                                pool.wait_ge(outs[w], 16 * G4 * kk)
                            nc.gpsimd.tensor_copy(stage[:, w, :], self.own_i[:, bass.ds(n * G4, G4)]).then_inc(s["staged"], 1)
                            self.hold(pool, (s["staged"], n + 1), (s["act_res"], n + 1))
                            for j in range(G4):
                                nc.gpsimd.indirect_dma_start(
                                    out=self.out, out_offset=bass.IndirectOffsetOnAxis(ap=stage[:, w, j:j + 1], axis=0),
                                    in_=res[:, w, j, :], in_offset=None, bounds_check=N - 1,
                                    oob_is_err=False).then_inc(outs[w], 16)

                    steps(pool, AG, 3, step)
                    for w in range(UN):
                        pool.wait_ge(outs[w], 16 * G4 * ((AG - w + UN - 1) // UN))

            @block.tensor
            def _(pe):
                def step(k, u):
                    i = UN * k + u

                    def sums(j):
                        if live(k, u, 1, AG):
                            w = (u - 1) % 2
                            if j == 0:
                                pe.wait_ge(s["dve_m"], i)
                                wait(pe, s["dve_t"], i - 2)
                            a_, b_, c_ = place(w, j)
                            self.sum_chunk(pe, i - 1, j, p_s[:, a_, b_, c_], m[:, w], msg((i - 1) * G4 + j),
                                           s["carried"], s["summed"])

                    sums(0)
                    sums(1)
                    if live(k, u, 3, AG) and not last_layer:
                        pe.wait_ge(s["act_n"], i - 2)
                        wait(pe, s["act_t"], i - 3)
                        for j in range(G4):
                            t = nc.tensor.transpose(p_t[:, j * D:(j + 1) * D], n_[:, (u - 3) % 2, j, :], self.ident[:])
                        t.then_inc(s["pe_t"], 1)
                    sums(2)
                    sums(3)
                    if live(k, u, 3, AG) and not last_layer:
                        pe.wait_ge(s["act_t"], i - 2)
                        wait(pe, s["dve_h"], i - 3)
                        self.gat_rows(nt, p_h, layer + 1).then_inc(s["pe_h"], 1)

                steps(pe, AG, 3, step)

            @block.scalar
            def _(act):
                def step(k, u):
                    i = UN * k + u

                    def carry(j):
                        if live(k, u, 1, AG):
                            if isinstance(i, int) and j == G4 and i == AG:
                                return
                            a_, b_, c_ = place((u - 1) % 2, j - 1)
                            row0 = self.msgs[0:1, bass.ds((i - 1) * G4 + j, 1), :].rearrange("p o f -> p (o f)")
                            self.carry_chunk(act, i - 1, j, row0, p_s[0:1, a_, b_, c_], s["carried"], s["summed"])

                    carry(1)
                    if live(k, u, 3, AG):
                        w = (u - 3) % 2
                        act.wait_ge(s["dve_nb"], i - 2)
                        wait(act, s["dve_y"] if last_layer else s["pe_t"], i - 4)
                        self.norm_apply(n_[:, w], o[:, w], rs[:, w], nb[:, w]).then_inc(s["act_n"], 1)
                    carry(2)
                    carry(3)
                    if live(k, u, 3, AG) and not last_layer:
                        act.wait_ge(s["pe_t"], i - 2)
                        wait(act, s["pe_h"], i - 3)
                        nc.scalar.activation(nt[:], p_t[:], ACT.Copy).then_inc(s["act_t"], 1)
                    carry(4)
                    if live(k, u, 4, AG) and last_layer:
                        w, x_ = u % 2, (u - 4) % UN
                        act.wait_ge(s["dve_nb2"], i - 3)
                        if not isinstance(i, int) or i - 4 >= UN:
                            act.wait_ge(outs[x_], 16 * G4 * (k - 1))
                        self.norm_apply(res[:, x_], y[:, w], rs2[:, w], nb2[:, w]).then_inc(s["act_res"], 1)
                    if live(k, u, 1, AG):
                        w = (u - 1) % 2
                        act.wait_ge(s["dve_inv"], i)
                        nc.scalar.activation(rs[:, w], inv[:, w], ACT.Sqrt).then_inc(s["act_rs"], 1)
                    if live(k, u, 3, AG) and last_layer:
                        w = (u - 3) % 2
                        act.wait_ge(s["dve_inv2"], i - 2)
                        nc.scalar.activation(rs2[:, w], inv2[:, w], ACT.Sqrt).then_inc(s["act_rs2"], 1)

                steps(act, AG, 4, step)

            @block.vector
            def _(dve):
                link = Chain(dve, s["link"], 6)
                link2 = Chain(dve, s["link2"], 5) if last_layer else None

                def step(k, u):
                    i = UN * k + u
                    if live(k, u, 2, AG):
                        w = u % 2
                        dve.wait_ge(s["act_rs"], i - 1)
                        self.norm_shift(mv[:, w], rs[:, w], nb[:, w]).then_inc(s["dve_nb"], 1)
                    if live(k, u, 4, AG) and last_layer:
                        w = u % 2
                        dve.wait_ge(s["act_rs2"], i - 3)
                        self.norm_shift(mv2[:, w], rs2[:, w], nb2[:, w]).then_inc(s["dve_nb2"], 1)
                    if live(k, u, 0, AG):
                        wait(dve, s["summed"], (i - 1) * G4)
                        self.select_group(m[:, u % 2], k, u, 0, self.w_edge).then_inc(s["dve_m"], 1)
                    if live(k, u, 1, AG):
                        w, c0 = (u - 1) % 2, (i - 1) * G4
                        link.group(i - 1)
                        self.wait_sums(dve, i - 1, s["carried"], s["summed"])
                        dve.wait_ge(arrived[(u - 1) % UN], 16 * (k + (0 if u < 1 else 1)))
                        wait(dve, s["act_n"], i - 2)
                        for j in range(G4):
                            a_, b_, c_ = place(w, j)
                            last = nc.vector.scalar_tensor_tensor(
                                out=t_[:, j, :], in0=h[:, (u - 1) % UN, j, :], scalar=self.w_self[:, bass.ds(c0 + j, 1)],
                                in1=p_s[:, a_, b_, c_], op0=ALU.mult, op1=ALU.add)
                        last.then_inc(s["dve_t"], 1)
                        dve.wait_ge(s["dve_t"], i)
                        link(nc.vector.tensor_scalar(rden[:], t_[:, :, D + 1], 1e-30, None, ALU.max))
                        link(nc.vector.reciprocal(rden[:], rden[:]))
                        for j in range(G4):
                            last = nc.vector.scalar_tensor_tensor(out=o[:, w, j, :], in0=t_[:, j, 0:D], scalar=rden[:, j:j + 1],
                                                                  in1=self.bl[:, layer, :], op0=ALU.mult, op1=ALU.add)
                        link(last)
                        self.norm_stats(lambda j: o[:, w, j, :], st, mv[:, w], link)
                        self.norm_inverse(mv[:, w], inv[:, w], link).then_inc(s["dve_inv"], 1)
                    if live(k, u, 3, AG):
                        w = (u - 3) % 2
                        if last_layer:
                            link2.group(i - 3)
                            dve.wait_ge(s["act_n"], i - 2)
                            dve.wait_ge(arrivedx[(u - 3) % UN], 16 * (k + (0 if u < 3 else 1)))
                            wait(dve, s["act_res"], i - 4)
                            link2(nc.vector.tensor_tensor(y[:, w], n_[:, w], self.each(self.gam[:]), ALU.mult))
                            link2(nc.vector.tensor_tensor(y[:, w], y[:, w], self.each(self.bet[:]), ALU.add))
                            nc.vector.tensor_tensor(y[:, w], y[:, w], x3[:, (u - 3) % UN], ALU.add).then_inc(s["dve_y"], 1)
                            dve.wait_ge(s["dve_y"], i - 2)
                            self.norm_stats(lambda j: y[:, w, j, :], st2, mv2[:, w], link2)
                            self.norm_inverse(mv2[:, w], inv2[:, w], link2).then_inc(s["dve_inv2"], 1)
                        else:
                            dve.wait_ge(s["pe_h"], i - 2)
                            self.stored(dve, outs, k, u, 3)
                            self.gat_rows_out(hn[:, w], p_h, layer + 1, i - 3).then_inc(s["dve_h"], 1)

                steps(dve, AG, 4, step)


def resnorm_gnn(nc, args, out):
    net = Net(nc, args, out)
    with ExitStack() as ctx:
        net.allocate(ctx)
        net.phase_weights()
        net.phase_terms()
        net.phase_segments()
        net.phase_dense()
        net.phase_gin1()
        net.phase_gin2()
        net.phase_rgcn()
        net.phase_gcn()
        for layer in range(3):
            net.phase_gat_nodes(layer)
            net.phase_gat_weights(layer)
            net.phase_gat_sums(layer)


_INS = ["x", "src", "dst", "edge_attr_128", "edge_type_8", "edge_weight", "L0_gnn_w1a", "L0_gnn_b1a",
        "L0_gnn_w1b", "L0_gnn_b1b", "L0_gnn_w2a", "L0_gnn_b2a", "L0_gnn_w2b", "L0_gnn_b2b", "L0_gnn_wl",
        "L0_gnn_bl", "L1_gnn_bases", "L1_gnn_w_comp", "L2_gnn_W", "L2_gnn_bias", "L3_gnn_W",
        "L3_gnn_att_src", "L3_gnn_att_dst", "L3_gnn_W_e", "L3_gnn_att_edge", "L3_gnn_bias",
        "L3_gnn_ln_gamma", "L3_gnn_ln_beta"]


def kernel(**inputs):
    import concourse.bacc as bacc
    from concourse.bass_utils import run_bass_kernel_spmd

    nc = bacc.Bacc("TRN2", target_bir_lowering=False, num_devices=1)
    arrays, args = {}, {}
    for name in _INS:
        a = np.ascontiguousarray(inputs[name])
        arrays[f"in_{name}"] = a
        args[name] = nc.dram_tensor(f"in_{name}", a.shape, mybir.dt.from_np(a.dtype), kind="ExternalInput").ap()
    out = nc.dram_tensor("out_rows", (N, D), F32, kind="ExternalOutput").ap()
    resnorm_gnn(nc, args, out)
    r = run_bass_kernel_spmd(nc, [arrays], core_ids=[0])
    return r.results[0]["out_rows"]
```

```python
from contextlib import ExitStack

import numpy as np
import concourse.bass as bass
from concourse import mybir

F32 = mybir.dt.float32
I32 = mybir.dt.int32
ALU = mybir.AluOpType
ACT = mybir.ActivationFunctionType
AXX = mybir.AxisListType.X

N = 50000
E = 25000
D = 128
H = 64
CE = 127
G4 = 4
ROWP = 100
CHUNKS = 2 * ROWP
AG = CHUNKS // G4
SLOTS = 128 * CHUNKS
GN = 128 * G4
DG = -(-N // GN)
NPAD = DG * GN
XW = D + 4
RE = 2 * CE
EPS = 1e-5
FAR = 65535
BIG = 1e30
UN = 4


def steps(eng, count, lag, step, first=1):
    full = (count - 1) // UN
    for i in range(UN * first):
        step(i // UN, i % UN)
    with eng.Fori(first, full) as k:
        for u in range(UN):
            step(k, u)
    for i in range(full * UN, count + lag):
        step(i // UN, i % UN)


def live(k, u, lag, count):
    return not isinstance(k, int) or 0 <= UN * k + u - lag < count


def wait(eng, sem, value):
    if not isinstance(value, int) or value > 0:
        eng.wait_ge(sem, value)


class Chain:

    def __init__(self, eng, sem, per):
        self.eng, self.sem, self.per, self.j = eng, sem, per, per

    def group(self, n):
        assert self.j == self.per
        self.n, self.j = n, 0

    def put(self, ins):
        self.j += 1
        assert self.j <= self.per
        ins.then_inc(self.sem, 1)

    def last(self, hold=None):
        if hold:
            hold(self.eng, (self.sem, self.n * self.per + self.j))
        else:
            self.eng.wait_ge(self.sem, self.n * self.per + self.j)

    def __call__(self, ins):
        self.put(ins)
        self.last()


class Net:

    def __init__(self, nc, a, out):
        self.nc, self.a, self.out = nc, a, out
        self.n_sems = 0

    def scope(self, phase):
        ctx = ExitStack()
        nc = self.nc

        def sb(name, shape, dt=F32):
            return ctx.enter_context(nc.sbuf_tensor(f"{phase}_{name}", shape, dt))

        def ps(name, shape=(128, 512)):
            return ctx.enter_context(nc.psum_tensor(f"{phase}_{name}", list(shape), F32))

        sems = []

        def sem(name):
            sems.append(nc.alloc_semaphore(name=f"{phase}_{name}"))
            return sems[-1]

        def finish():
            nc.clear_and_free_semaphores(sems)
            nc.all_engine_barrier()

        ctx.callback(finish)
        return ctx, sb, ps, sem

    def allocate(self, ctx):
        nc = self.nc
        self.begun = ctx.enter_context(nc.semaphore("begun"))

        def sb(name, shape, dt=F32):
            return ctx.enter_context(nc.sbuf_tensor(name, shape, dt))

        def dram(name, rows, width, dt=F32):
            return nc.dram_tensor(name, (rows, width), dt, kind="Internal").ap()

        self.ident = sb("ident", [128, 128])
        self.iota = sb("iota", [128, 128])
        self.msgs = sb("msgs", [128, CHUNKS, XW])
        self.slot_id = sb("slot_id", [128, CHUNKS], I32)
        self.q = sb("q", [128, CHUNKS])
        self.src_i = sb("src_i", [128, CHUNKS], I32)
        self.dst_i = sb("dst_i", [128, CHUNKS], I32)
        self.own_i = sb("own_i", [128, CHUNKS], I32)
        self.row_i = sb("row_i", [128, CHUNKS], I32)
        self.row4_i = sb("row4_i", [128, CHUNKS], I32)
        self.coef = sb("coef", [128, 4, CHUNKS])
        self.deg = sb("deg", [128, CHUNKS, 4])
        self.dis = sb("dis", [128, CHUNKS])
        self.att_s = sb("att_s", [128, CHUNKS, 3])
        self.w_edge = sb("w_edge", [128, CHUNKS])
        self.w_self = sb("w_self", [128, CHUNKS])
        self.end = sb("end", [ROWP, 256])
        self.notend = sb("notend", [ROWP, 256])
        self.startneg = sb("startneg", [ROWP, 256])
        self.preneg = sb("preneg", [ROWP, 256])
        self.open = sb("open", [ROWP, 256])
        self.edge_t = sb("edge_t", [ROWP, 3, 256])
        self.flag_rows = sb("flag_rows", [1, 2, ROWP])
        self.w1a = sb("w1a", [D, H]); self.w1b = sb("w1b", [H, H])
        self.b1a = sb("b1a", [H, 1]); self.b1b = sb("b1b", [H, 1])
        self.w2a = sb("w2a", [H, 2 * D]); self.b2a = sb("b2a", [D, 2])
        self.wc = sb("wc", [D, 2, D])
        self.bc = sb("bc", [128, D])
        self.bases = sb("bases", [D, 4, D])
        self.wg = sb("wg", [D, D])
        self.bg = sb("bg", [128, D])
        self.wx = sb("wx", [D, 3, XW])
        self.cx = sb("cx", [128, 3, XW])
        self.gam = sb("gam", [128, D]); self.bet = sb("bet", [128, D])
        self.eps = sb("eps", [128, 1])
        self.ve = sb("ve", [D, 3])
        self.t2 = dram("t_h1", SLOTS + NPAD, H)
        self.t3 = dram("t_x1", SLOTS + NPAD, D)
        self.t4 = dram("t_x2", SLOTS + 128, D)
        self.th = [dram(f"t_gat{l}", SLOTS + NPAD, XW) for l in range(3)]
        self.x3 = dram("t_x3", SLOTS + NPAD, D)
        self.xd = dram("t_xd", SLOTS, D)
        self.x2 = dram("t_x2s", SLOTS, D)
        self.where = dram("t_where", NPAD, 1, I32)
        self.terms = dram("t_terms", 3, E)

    def hold(self, eng, *waits):
        waits = [(sem, v if isinstance(v, int) else eng.to_reg(v)) for sem, v in waits]
        eng.wait_ge(self.begun, 1)
        for sem, value in waits:
            wait(eng, sem, value)

    def slots(self, t, k, u, lag=0):
        v = t[0:SLOTS, :].rearrange("(p c) f -> p c f", p=128)
        return v[:, bass.ds((UN * k + u - lag) * G4, G4), :]

    def nodes(self, t, k, u, lag=0, base=SLOTS):
        v = t[base:base + NPAD, :].rearrange("(g p j) f -> g p j f", p=128, j=G4)
        return v[bass.ds(UN * k + u - lag, 1), :, :, :].rearrange("g p j f -> p (g j) f")

    def phase_weights(self):
        nc, a = self.nc, self.a
        ctx, sb, ps, sem = self.scope("wt")
        with ctx:
            w2b = sb("w2b", [D, 2, 2 * D]); wl = sb("wl", [D, 2, D]); b2b = sb("b2b", [D, 2])
            w2bt = sb("w2bt", [D, 4, D]); wgr = sb("wgr", [D, D])
            asr = sb("asr", [128, 3, D]); adr = sb("adr", [128, 3, D]); aer = sb("aer", [128, 3, D])
            we = sb("we", [D, 3, D]); prod = sb("prod", [D, 3, 3, D]); wraw = sb("wraw", [D, 3, D])
            bl = sb("bl", [128, 3, D]); begin = sb("begin", [1, 1]); gcol = sb("gcol", [D, 2]); bcol = sb("bcol", [D, 2]); spread = sb("spread", [D, 4, D])
            ones = sb("ones", [128, 128])
            p_t = ps("p_t"); p_w = ps("p_w"); p_b = ps("p_b"); p_c = ps("p_c")
            loaded, ready, folded, turned, kept, made = (
                sem("loaded"), sem("ready"), sem("folded"), sem("turned"), sem("kept"), sem("made"))
            zeroed, stored = sem("zeroed"), sem("stored")
            row = lambda v: v.rearrange("(o n) -> o n", o=1).to_broadcast([128, v.shape[0]])
            rows3 = lambda v: v.rearrange("(o l) n -> o l n", o=1).to_broadcast([128, 3, D])
            cols = lambda v: v.rearrange("(t p) -> p t", p=128)
            loads = [
                (self.w1a[:], a["L0_gnn_w1a"]), (self.w1b[:], a["L0_gnn_w1b"]),
                (self.b1a[:], a["L0_gnn_b1a"].rearrange("(h o) -> h o", o=1)),
                (self.b1b[:], a["L0_gnn_b1b"].rearrange("(h o) -> h o", o=1)),
                (self.w2a[:], a["L0_gnn_w2a"]), (self.b2a[:], cols(a["L0_gnn_b2a"])),
                (w2b[:], a["L0_gnn_w2b"].rearrange("(t p) n -> p t n", p=128)),
                (wl[:], a["L0_gnn_wl"].rearrange("(t p) n -> p t n", p=128)),
                (b2b[:], cols(a["L0_gnn_b2b"])), (self.bc[:], row(a["L0_gnn_bl"])),
                (self.bases[:], a["L1_gnn_bases"].rearrange("b i o -> i b o")),
                (wgr[:], a["L2_gnn_W"]), (self.bg[:], row(a["L2_gnn_bias"])),
                (wraw[:], a["L3_gnn_W"].rearrange("l i o -> i l o")),
                (we[:], a["L3_gnn_W_e"].rearrange("l i o -> i l o")),
                (asr[:], rows3(a["L3_gnn_att_src"])), (adr[:], rows3(a["L3_gnn_att_dst"])),
                (aer[:], rows3(a["L3_gnn_att_edge"])), (bl[:], rows3(a["L3_gnn_bias"])),
                (gcol[:], a["L3_gnn_ln_gamma"][0:2, :].rearrange("l i -> i l")),
                (bcol[:], a["L3_gnn_ln_beta"][0:2, :].rearrange("l i -> i l")),
                (self.gam[:], row(a["L3_gnn_ln_gamma"][2, :])),
                (self.bet[:], row(a["L3_gnn_ln_beta"][2, :])),
            ]
            block = ctx.enter_context(nc.Block())

            @block.sync
            def _(sp):
                with nc.allow_non_contiguous_dma(reason="columns of biases, once"):
                    for dst, src in loads:
                        sp.dma_start(dst, src).then_inc(loaded, 16)
                sp.wait_ge(zeroed, 1)
                sp.dma_start(self.t4[SLOTS:SLOTS + 128, :], spread[:, 3, :]).then_inc(stored, 16)
                sp.wait_ge(loaded, 16 * len(loads))
                sp.wait_ge(stored, 16)

            @block.gpsimd
            def _(pool):
                nc.gpsimd.memset(self.ident[:], 0.0).then_inc(ready, 1)
                nc.gpsimd.memset(ones[:], 1.0).then_inc(ready, 1)
                nc.gpsimd.memset(self.eps[:], EPS).then_inc(ready, 1)
                nc.gpsimd.memset(spread[:, 3, :], 0.0).then_inc(zeroed, 1)
                nc.gpsimd.memset(begin[:], 0.0).then_inc(self.begun, 1)
                pool.wait_ge(ready, 3)
                nc.gpsimd.affine_select(out=self.ident[:], in_=self.ident[:], compare_op=ALU.not_equal,
                                        fill=1.0, base=0, pattern=[[-1, 128]],
                                        channel_multiplier=1).then_inc(ready, 1)
                nc.gpsimd.iota(self.iota[:], pattern=[[1, 128]], base=0, channel_multiplier=0,
                               allow_small_or_imprecise_dtypes=True).then_inc(ready, 1)

            @block.vector
            def _(dve):
                dve.wait_ge(loaded, 16 * len(loads))
                dve.wait_ge(ready, 5)
                for n, (w, v) in enumerate(((wraw, asr), (wraw, adr), (we, aer))):
                    nc.vector.tensor_tensor(prod[:, n], w[:], v[:], ALU.mult).then_inc(folded, 1)
                nc.vector.memset(self.wx[:], 0.0).then_inc(folded, 1)
                nc.vector.memset(self.cx[:], 0.0).then_inc(folded, 1)
                dve.wait_ge(folded, 5)
                nc.vector.tensor_copy(self.wx[:, :, 0:D], wraw[:]).then_inc(folded, 1)
                nc.vector.tensor_reduce(self.wx[:, :, D], prod[:, 0], AXX, ALU.add).then_inc(folded, 1)
                nc.vector.tensor_reduce(self.wx[:, :, D + 2], prod[:, 1], AXX, ALU.add).then_inc(folded, 1)
                nc.vector.tensor_reduce(self.ve[:], prod[:, 2], AXX, ALU.add).then_inc(folded, 1)
                for n, c in enumerate((b2b[:, 0:1], b2b[:, 1:2], bcol[:, 0:1], bcol[:, 1:2])):
                    if n == 3:
                        dve.wait_ge(stored, 16)
                    nc.vector.tensor_scalar(spread[:, n], ones[:], c, None, ALU.mult).then_inc(folded, 1)
                dve.wait_ge(turned, 1)
                nc.vector.tensor_copy(w2bt[:].rearrange("p a b -> p (a b)"), p_t[:]).then_inc(kept, 1)
                nc.vector.tensor_copy(self.wg[:], p_b[:, 0:D]).then_inc(kept, 1)
                dve.wait_ge(made, 1)
                nc.vector.tensor_copy(self.wc[:].rearrange("p a b -> p (a b)"), p_w[:, 0:2 * D]).then_inc(kept, 1)
                nc.vector.tensor_tensor(self.bc[:], p_w[:, 2 * D:3 * D], self.bc[:], ALU.add).then_inc(kept, 1)
                nc.vector.tensor_copy(self.cx[:, 1:3, :], p_c[:, 0:2 * XW].rearrange("p (a b) -> p a b", a=2)).then_inc(kept, 1)
                for l in (1, 2):
                    nc.vector.tensor_scalar(self.wx[:, l, :], self.wx[:, l, :], gcol[:, l - 1:l], None,
                                            ALU.mult).then_inc(kept, 1)
                dve.wait_ge(kept, 7)
                nc.vector.memset(self.cx[:, :, D + 1], 1.0).then_inc(kept, 1)
                nc.vector.tensor_tensor(self.cx[:, :, 0:D], self.cx[:, :, 0:D], bl[:], ALU.add).then_inc(kept, 1)

            @block.tensor
            def _(pe):
                pe.wait_ge(loaded, 16 * len(loads))
                pe.wait_ge(ready, 5)
                for t in range(2):
                    for k in range(2):
                        n = 2 * t + k
                        nc.tensor.transpose(p_t[:, n * D:(n + 1) * D], w2b[:, t, k * D:(k + 1) * D], self.ident[:])
                nc.tensor.transpose(p_b[:, 0:D], wgr[:], self.ident[:]).then_inc(turned, 1)
                pe.wait_ge(kept, 1)
                pe.wait_ge(folded, 13)
                for t in range(2):
                    for k in range(2):
                        nc.tensor.matmul(p_w[:, t * D:(t + 1) * D], w2bt[:, 2 * t + k, :], wl[:, k, :],
                                         start=(k == 0), stop=(k == 1))
                for k in range(2):
                    nc.tensor.matmul(p_w[:, 2 * D:3 * D], spread[:, k, :], wl[:, k, :], start=(k == 0), stop=(k == 1))
                for l in (1, 2):
                    last = nc.tensor.matmul(p_c[:, (l - 1) * XW:l * XW], spread[:, 1 + l, :], self.wx[:, l, :],
                                            start=True, stop=True)
                last.then_inc(made, 1)

    def phase_terms(self):
        nc, a = self.nc, self.a
        ctx, sb, ps, sem = self.scope("et")
        full, rest = E // GN, E % GN // G4
        whole, rest_row = E // RE, E % RE
        assert rest_row <= CE
        with ctx:
            rows = sb("rows", [128, UN, G4, D]); turned = sb("turned", [D, 2, GN]); res = sb("res", [3, UN, GN])
            p_t = [ps(f"p_t{i}") for i in range(2)]; p_r = [ps(f"p_r{i}") for i in range(2)]
            p_e = [ps(f"p_e{l}") for l in range(3)]
            arrived = [sem(f"arrived{i}") for i in range(UN)]
            stored = [sem(f"stored{i}") for i in range(UN)]
            cleared, pe_t, act_t, pe_r, dve_r = sem("cleared"), sem("pe_t"), sem("act_t"), sem("pe_r"), sem("dve_r")
            blank, back, columns, put = sem("blank"), sem("back"), sem("columns"), sem("put")
            attr = a["edge_attr_128"]
            groups = full + 1
            halves = lambda x: x.rearrange("p (j k) -> p j k", j=2)
            block = ctx.enter_context(nc.Block())

            @block.sync
            def _(sp):
                sp.wait_ge(cleared, 1)

                def step(k, u):
                    if live(k, u, 0, groups):
                        i = UN * k + u
                        wait(sp, pe_t, i - UN + 1)
                        if isinstance(i, int) and i == full:
                            sp.dma_start(rows[0:rest, u], attr[full * GN:E, :].rearrange("(p j) f -> p j f", j=G4)).then_inc(arrived[u], 16)
                        else:
                            v = attr[0:full * GN, :].rearrange("(g p j) f -> g p j f", p=128, j=G4)
                            sp.dma_start(rows[:, u], v[bass.ds(i, 1)].rearrange("g p j f -> p (g j) f")).then_inc(arrived[u], 16)
                    if live(k, u, 4, groups):
                        n = UN * k + u - 4
                        sp.wait_ge(dve_r, n + 1)
                        size = rest * G4 if isinstance(n, int) and n == full else GN
                        sp.dma_start(self.terms[:, bass.ds(n * GN, size)], res[:, u, 0:size]).then_inc(stored[u], 16)

                steps(sp, groups, 4, step, 2)
                self.all_stored(sp, stored, groups)
                sp.wait_ge(blank, 1)
                with nc.allow_non_contiguous_dma(reason="rows of 127"):
                    for l in range(3):
                        t = halves(self.edge_t[:, l, :])[:, :, 1:128]
                        r = self.terms[l, :]
                        sp.dma_start(t[0:whole], r[0:whole * RE].rearrange("(p j k) -> p j k", j=2, k=CE)).then_inc(back, 16)
                        sp.dma_start(t[whole:whole + 1, 0, 0:rest_row],
                                     r[whole * RE:E].rearrange("(o k) -> o k", o=1)).then_inc(back, 16)
                sp.wait_ge(back, 96)

            @block.gpsimd
            def _(pool):
                nc.gpsimd.memset(rows[:].rearrange("p a b c -> p (a b c)"), 0.0).then_inc(cleared, 1)
                nc.gpsimd.memset(self.edge_t[:].rearrange("p a b -> p (a b)"), 0.0).then_inc(blank, 1)

            @block.tensor
            def _(pe):
                def step(k, u):
                    i = UN * k + u
                    if live(k, u, 0, groups):
                        pe.wait_ge(arrived[u], 16 * (k + 1))
                        wait(pe, act_t, i - 1)
                        for j in range(G4):
                            last = nc.tensor.transpose(p_t[u % 2][:, j * D:(j + 1) * D], rows[:, u, j, :], self.ident[:])
                        last.then_inc(pe_t, 1)
                    if live(k, u, 2, groups):
                        pe.wait_ge(act_t, i - 1)
                        wait(pe, dve_r, i - 3)
                        nc.tensor.matmul(p_r[u % 2][0:3, :], self.ve[:], turned[:, u % 2, :],
                                         start=True, stop=True).then_inc(pe_r, 1)

                steps(pe, groups, 2, step, 2)
                pe.wait_ge(back, 96)
                for l in range(3):
                    for j in range(2):
                        last = nc.tensor.transpose(p_e[l][:, j * ROWP:(j + 1) * ROWP],
                                                   self.edge_t[:, l, j * 128:(j + 1) * 128], self.ident[0:ROWP, 0:ROWP])
                last.then_inc(columns, 1)

            @block.scalar
            def _(act):
                def step(k, u):
                    i = UN * k + u
                    if live(k, u, 1, groups):
                        w = (u - 1) % 2
                        act.wait_ge(pe_t, i)
                        wait(act, pe_r, i - 2)
                        nc.scalar.activation(turned[:, w, :], p_t[w][:], ACT.Copy).then_inc(act_t, 1)

                steps(act, groups, 1, step, 2)

            @block.vector
            def _(dve):
                def step(k, u):
                    i = UN * k + u
                    if live(k, u, 3, groups):
                        w = (u - 3) % UN
                        dve.wait_ge(pe_r, i - 2)
                        self.stored(dve, stored, k, u, 3)
                        nc.vector.tensor_copy(res[:, w, :].rearrange("r (p j) -> r j p", j=G4),
                                              p_r[w % 2][0:3, :].rearrange("r (j p) -> r j p", j=G4)).then_inc(dve_r, 1)

                steps(dve, groups, 3, step, 2)
                dve.wait_ge(columns, 1)
                for l in range(3):
                    nc.vector.tensor_copy(self.msgs[:, :, D + 1 + l].rearrange("q (p j) -> q j p", j=2),
                                          p_e[l][:, 0:CHUNKS].rearrange("q (j p) -> q j p", j=2)).then_inc(put, 1)
                    nc.vector.memset(halves(self.edge_t[:, l, :])[:, :, 0], -BIG).then_inc(put, 1)
                dve.wait_ge(put, 6)

    def phase_segments(self):
        nc, a = self.nc, self.a
        ctx, sb, ps, sem = self.scope("sg")
        whole = E // RE
        rest = E - whole * RE
        with ctx:
            dst_raw = sb("dst_raw", [ROWP, RE + 2], I32)
            raw = sb("raw", [ROWP, 2, RE], I32)
            wr = sb("wr", [ROWP, RE])
            dstf = sb("dstf", [ROWP, RE + 2])
            row = sb("row", [ROWP, 6, 256])
            start = sb("start", [ROWP, 256]); pos = sb("pos", [ROWP, 256]); tmp = sb("tmp", [ROWP, 256])
            ty = sb("ty", [128, CHUNKS]); wcol = sb("wcol", [128, CHUNKS]); pick = sb("pick", [128, 8, CHUNKS])
            wcomp = sb("wcomp", [128, 8, 4])
            deg_tmp = sb("nodes", [128, NPAD // 128], I32)
            p = [ps(f"p{i}") for i in range(7)]
            loaded, cleared, told, v, turned, rows_done, gone = (
                sem("loaded"), sem("cleared"), sem("told"), sem("v"), sem("turned"), sem("rows_done"), sem("gone"))
            halves = lambda x: x.rearrange("p (j k) -> p j k", j=2)

            dst_loads = [
                (dst_raw[0:1, 1:RE + 2], bass.AP(tensor=a["dst"].tensor, offset=0, ap=[[RE, 1], [1, RE + 1]])),
                (dst_raw[1:whole, :], bass.AP(tensor=a["dst"].tensor, offset=RE - 1, ap=[[RE, whole - 1], [1, RE + 2]])),
                (dst_raw[whole:whole + 1, 0:rest + 1],
                 bass.AP(tensor=a["dst"].tensor, offset=whole * RE - 1, ap=[[RE, 1], [1, rest + 1]])),
            ]
            other_loads = []
            for t, name in ((raw[:, 0], "src"), (raw[:, 1], "edge_type_8"), (wr[:], "edge_weight")):
                other_loads.append((t[0:whole, :], a[name][0:whole * RE].rearrange("(p k) -> p k", k=RE)))
                other_loads.append((t[whole:whole + 1, 0:rest],
                                    a[name][whole * RE:E].rearrange("(o k) -> o k", o=1)))
            n_loads = len(dst_loads) + len(other_loads) + 1
            block = ctx.enter_context(nc.Block())

            @block.sync
            def _(sp):
                sp.wait_ge(cleared, 4)
                for dst, src in dst_loads + other_loads:
                    sp.dma_start(dst, src).then_inc(loaded, 16)
                sp.dma_start(wcomp[:], a["L1_gnn_w_comp"].rearrange("(o r) b -> o r b", o=1).to_broadcast([128, 8, 4])).then_inc(loaded, 16)
                sp.wait_ge(told, 2)
                sp.dma_start(self.where.rearrange("(p t) o -> p (t o)", p=128), deg_tmp[:]).then_inc(gone, 16)
                sp.wait_ge(gone, 16)
                sp.wait_ge(loaded, 16 * n_loads)

            @block.gpsimd
            def _(pool):
                nc.gpsimd.memset(dst_raw[:], FAR).then_inc(cleared, 1)
                nc.gpsimd.memset(raw[:].rearrange("p a b -> p (a b)"), 0).then_inc(cleared, 1)
                nc.gpsimd.memset(wr[:], 0.0).then_inc(cleared, 1)
                nc.gpsimd.memset(row[:].rearrange("p a b -> p (a b)"), 0.0).then_inc(cleared, 1)
                nc.gpsimd.iota(halves(pos[:]), pattern=[[0, 2], [1, 128]], base=0, channel_multiplier=0,
                               allow_small_or_imprecise_dtypes=True).then_inc(told, 1)
                nc.gpsimd.iota(deg_tmp[:], pattern=[[1, NPAD // 128]], base=SLOTS,
                               channel_multiplier=NPAD // 128).then_inc(told, 1)
                nc.gpsimd.iota(self.slot_id[:], pattern=[[1, CHUNKS]], base=0,
                               channel_multiplier=CHUNKS).then_inc(told, 1)
                nc.gpsimd.memset(self.end[:], 0.0).then_inc(told, 1)
                nc.gpsimd.memset(start[:], 0.0).then_inc(told, 1)
                nc.gpsimd.memset(self.startneg[:], 0.0).then_inc(told, 1)

            @block.vector
            def _(dve):
                count = [0]

                def after(ins):
                    count[0] += 1
                    ins.then_inc(v, 1)
                    dve.wait_ge(v, count[0])

                dve.wait_ge(loaded, 16 * n_loads)
                dve.wait_ge(told, 6)
                after(nc.vector.tensor_copy(dstf[:], dst_raw[:]))
                after(nc.vector.memset(dstf[0:1, 0:1], -1.0))
                cur = halves(dstf[:, 1:RE + 1])
                at = lambda t: halves(t[:])[:, :, 1:128]
                nc.vector.tensor_tensor(at(start), cur, halves(dstf[:, 0:RE]), ALU.not_equal).then_inc(v, 1)
                nc.vector.tensor_tensor(at(self.end), cur, halves(dstf[:, 2:RE + 2]), ALU.not_equal).then_inc(v, 1)
                nc.vector.tensor_copy(halves(row[:, 0])[:, :, 1:128], halves(raw[:, 0])).then_inc(v, 1)
                nc.vector.tensor_scalar(halves(row[:, 1])[:, :, 1:128], cur, float(N - 1), None, ALU.min).then_inc(v, 1)
                nc.vector.tensor_copy(halves(row[:, 3])[:, :, 1:128], halves(wr[:])).then_inc(v, 1)
                nc.vector.tensor_copy(halves(row[:, 4])[:, :, 1:128], halves(raw[:, 1])).then_inc(v, 1)
                count[0] += 6
                dve.wait_ge(v, count[0])
                nc.vector.tensor_scalar(self.notend[:], self.end[:], -1.0, 1.0, ALU.mult, ALU.add).then_inc(v, 1)
                nc.vector.tensor_scalar(self.startneg[:], start[:], -BIG, None, ALU.mult).then_inc(v, 1)
                nc.vector.tensor_scalar(halves(row[:, 2])[:, :, 1:128], cur, float(-FAR), None, ALU.add).then_inc(v, 1)
                nc.vector.tensor_tensor(tmp[:], self.end[:], pos[:], ALU.mult).then_inc(v, 1)
                count[0] += 4
                dve.wait_ge(v, count[0])
                after(nc.vector.tensor_tensor(row[:, 2], row[:, 2], self.end[:], ALU.mult))
                after(nc.vector.tensor_scalar(row[:, 2], row[:, 2], float(FAR), None, ALU.add))
                for j in range(2):
                    lo, hi = j * 128, (j + 1) * 128
                    back = slice(hi - 1, lo - 1 if lo else None, -1)
                    after(nc.vector.tensor_tensor_scan(row[:, 5, back], self.notend[:, back], tmp[:, back], 0.0,
                                                       ALU.mult, ALU.add))
                q0, q1, s1 = (halves(t)[:, :, k] for t, k in ((row[:, 5], 0), (row[:, 5], 1), (start[:], 1)))
                after(nc.vector.tensor_scalar(q0, q1, 1.0, None, ALU.add))
                after(nc.vector.tensor_tensor(q0, q0, s1, ALU.mult))
                after(nc.vector.tensor_tensor(q0, q1, q0, ALU.subtract))
                after(nc.vector.tensor_tensor_scan(self.preneg[:], self.startneg[:], self.startneg[:], 0.0,
                                                   ALU.min, ALU.min))
                after(nc.vector.tensor_tensor_scan(self.open[:, ::-1], self.notend[:, ::-1], self.notend[:, ::-1], 1.0,
                                                   ALU.mult, ALU.mult))
                nc.vector.tensor_copy(tmp[:, 0:2], self.open[:, 0:2]).then_inc(rows_done, 1)
                dve.wait_ge(turned, 1)
                both = lambda t: t.rearrange("q (p j) -> q j p", j=2)
                of = lambda n: p[n][:, 0:CHUNKS].rearrange("q (j p) -> q j p", j=2)
                nc.vector.tensor_copy(both(self.src_i[:]), of(0)).then_inc(v, 1)
                nc.vector.tensor_copy(both(self.dst_i[:]), of(1)).then_inc(v, 1)
                nc.vector.tensor_copy(both(self.own_i[:]), of(2)).then_inc(v, 1)
                nc.vector.tensor_copy(both(wcol[:]), of(3)).then_inc(v, 1)
                nc.vector.tensor_copy(both(ty[:]), of(4)).then_inc(v, 1)
                nc.vector.tensor_copy(both(self.q[:]), of(5)).then_inc(v, 1)
                nc.vector.tensor_copy(self.flag_rows[:].rearrange("o a b -> o (a b)"), p[6][0:1, 0:2 * ROWP]).then_inc(v, 1)
                count[0] += 7
                dve.wait_ge(v, count[0])
                after(nc.vector.memset(self.msgs[:, :, D], 1.0))
                for r in range(8):
                    nc.vector.tensor_scalar(pick[:, r], ty[:], float(r), None, ALU.is_equal).then_inc(v, 1)
                count[0] += 8
                dve.wait_ge(v, count[0])
                for b in range(4):
                    after(nc.vector.tensor_scalar(self.coef[:, b], pick[:, 0], wcomp[:, 0, b:b + 1], None, ALU.mult))
                    for r in range(1, 8):
                        after(nc.vector.scalar_tensor_tensor(out=self.coef[:, b], in0=pick[:, r], scalar=wcomp[:, r, b:b + 1],
                                                             in1=self.coef[:, b], op0=ALU.mult, op1=ALU.add))
                    after(nc.vector.tensor_tensor(self.coef[:, b], self.coef[:, b], wcol[:], ALU.mult))

            @block.tensor
            def _(pe):
                pe.wait_ge(rows_done, 1)
                idp = self.ident[0:ROWP, 0:ROWP]
                for n in range(6):
                    for j in range(2):
                        nc.tensor.transpose(p[n][:, j * ROWP:(j + 1) * ROWP], row[:, n, j * 128:(j + 1) * 128], idp)
                nc.tensor.transpose(p[6][0:1, 0:ROWP], self.preneg[:, 255:256], idp)
                nc.tensor.transpose(p[6][0:1, ROWP:2 * ROWP], self.open[:, 0:1], idp).then_inc(turned, 1)

    def gather_group(self, pool, k, u, count, idx, stage, staged, table, ring, width, arrived, freed):
        nc = self.nc

        def put(k, u):
            if not isinstance(k, int) or k > 0:
                pool.wait_ge(arrived[u], 16 * G4 * k)
            i = UN * k + u
            nc.gpsimd.tensor_copy(stage[:, u, :], idx[:, bass.ds(i * G4, G4)]).then_inc(staged, 1)

        i = UN * k + u
        if isinstance(i, int) and i == 0:
            put(k, u)
        if not isinstance(i, int) or i + 1 < count:
            put(k + (u + 1) // UN, (u + 1) % UN)
        self.hold(pool, (staged, i + 1), *freed(k, u))
        for j in range(G4):
            nc.gpsimd.indirect_dma_start(
                out=ring[:, u, j, 0:width], out_offset=None, in_=table,
                in_offset=bass.IndirectOffsetOnAxis(ap=stage[:, u, j:j + 1], axis=0)).then_inc(arrived[u], 16)

    def resident_gather(self, idx, table, width, arrived, chunks=range(CHUNKS)):
        for c in chunks:
            self.nc.gpsimd.indirect_dma_start(
                out=self.msgs[:, c, 0:width], out_offset=None, in_=table,
                in_offset=bass.IndirectOffsetOnAxis(ap=idx[:, c:c + 1], axis=0)).then_inc(arrived, 16)

    def slot_gathers(self, pool, sb, sem):
        nc, a = self.nc, self.a
        ring = sb("g_ring", [128, UN, G4, D])
        stage_x = sb("g_stage_x", [128, UN, G4], I32); stage_own = sb("g_stage_own", [128, UN, G4], I32)
        stage_id = sb("g_stage_id", [128, UN, G4], I32)
        got, staged_x, staged_map = sem("g_got"), sem("g_staged_x"), sem("g_staged_map")
        arrived, stored, mapped = ([sem(f"g_{n}{u}") for u in range(UN)] for n in ("arrived", "stored", "mapped"))
        lag = UN - 1

        self.resident_gather(self.src_i, a["x"], D, got)

        def rows(k, u):
            def freed(k, u):
                return ((stored[u], 16 * k),)
            if live(k, u, 0, AG):
                self.gather_group(pool, k, u, AG, self.dst_i, stage_x, staged_x, a["x"], ring, D, arrived, freed)
            if live(k, u, lag, AG):
                v = (u - lag) % UN
                kk = k - (1 if u < lag else 0)
                pool.wait_ge(arrived[v], 16 * G4 * (kk + 1))
                pool.dma_start(self.slots(self.xd, kk, v), ring[:, v]).then_inc(stored[v], 16)

        steps(pool, AG, lag, rows)

        def owners(k, u):
            i = UN * k + u
            if not isinstance(k, int) or k > 0:
                pool.wait_ge(mapped[u], 16 * G4 * k)
            nc.gpsimd.tensor_copy(stage_own[:, u, :], self.own_i[:, bass.ds(i * G4, G4)]).then_inc(staged_map, 1)
            nc.gpsimd.tensor_copy(stage_id[:, u, :], self.slot_id[:, bass.ds(i * G4, G4)]).then_inc(staged_map, 1)
            self.hold(pool, (staged_map, 2 * i + 2))
            for j in range(G4):
                nc.gpsimd.indirect_dma_start(
                    out=self.where, out_offset=bass.IndirectOffsetOnAxis(ap=stage_own[:, u, j:j + 1], axis=0),
                    in_=stage_id[:, u, j:j + 1], in_offset=None, bounds_check=N - 1,
                    oob_is_err=False).then_inc(mapped[u], 16)

        steps(pool, AG, 0, owners)
        for u in range(UN):
            groups = (AG - u + UN - 1) // UN
            pool.wait_ge(mapped[u], 16 * G4 * groups)
            pool.wait_ge(stored[u], 16 * groups)
        pool.wait_ge(got, 16 * CHUNKS)

    def map_gathers(self, pool, sb, sem):
        nc = self.nc
        rows = sb("g_rows", [128, UN, G4, 1], I32); stage = sb("g_stage", [128, UN, G4], I32)
        arrived = [sem(f"g_arrived{u}") for u in range(UN)]
        staged, taken, least = sem("g_staged"), sem("g_taken"), sem("g_least")
        lag = UN - 1

        def step(k, u):
            def freed(k, u):
                return ((taken, UN * k + u - UN + 1),)
            if live(k, u, 0, AG):
                self.gather_group(pool, k, u, AG, self.src_i, stage, staged, self.where, rows, 1, arrived, freed)
            if live(k, u, lag, AG):
                v = (u - lag) % UN
                kk = k - (1 if u < lag else 0)
                pool.wait_ge(arrived[v], 16 * G4 * (kk + 1))
                nc.gpsimd.tensor_copy(self.row_i[:, bass.ds((UN * kk + v) * G4, G4)],
                                      rows[:, v].rearrange("p j o -> p (j o)")).then_inc(taken, 1)

        steps(pool, AG, lag, step)
        pool.wait_ge(taken, AG)
        nc.gpsimd.tensor_scalar(self.row4_i[:], self.row_i[:], SLOTS, None, ALU.min).then_inc(least, 1)

    def norm_part(self, part, rows, st, mv, inv, chain):
        nc = self.nc
        if part == 0:
            for j in range(G4):
                last = nc.vector.bn_stats(out=st[:, j, :], in_=rows(j))
            chain.put(last)
        elif part == 1:
            chain.last(self.hold)
            for j in range(G4):
                last = nc.vector.bn_aggr(out=mv[:, j, :], in_=st[:, j, :])
            chain.put(last)
        elif part == 2:
            chain.last()
            chain.put(nc.vector.tensor_scalar(inv, mv[:, :, 1], EPS, None, ALU.add))
        else:
            chain.last()
            return nc.vector.reciprocal(inv, inv)

    def norm_shift(self, mv, rs, nb):
        return self.nc.vector.scalar_tensor_tensor(out=nb, in0=mv[:, :, 0], scalar=-1.0, in1=rs,
                                                   op0=ALU.mult, op1=ALU.mult)

    def norm_apply(self, out, rows, rs, nb, tiles=range(G4)):
        for j in tiles:
            last = self.nc.scalar.activation(out[:, j, :], rows[:, j, :], ACT.Identity,
                                             bias=nb[:, j:j + 1], scale=rs[:, j:j + 1])
        return last

    def each(self, row):
        return row.rearrange("p (o f) -> p o f", o=1).to_broadcast([128, G4, row.shape[1]])

    def phase_dense(self):
        nc, a = self.nc, self.a
        ctx, sb, ps, sem = self.scope("de")
        with ctx:
            x = sb("x", [128, UN, G4, D])
            xt = sb("xt", [D, GN]); ha = sb("ha", [H, GN]); ht = sb("ht", [H, GN]); hh = sb("hh", [D, 2, 2, GN])
            h1 = sb("h1", [128, 2, G4, H])
            r = sb("r", [128, 2, G4, D]); x1 = sb("x1", [128, 2, G4, D]); v = sb("v", [128, 2, G4, D])
            x3 = sb("x3", [128, 2, G4, D]); x3t = sb("x3t", [D, GN]); h0 = sb("h0", [128, 2, G4, XW])
            st = sb("st", [128, G4, 6]); st2 = sb("st2", [128, G4, 6])
            mv = sb("mv", [128, UN, G4, 2]); mv2 = sb("mv2", [128, UN, G4, 2])
            inv = sb("inv", [128, UN, 2, G4]); rs = sb("rs", [128, UN, 2, G4]); nb = sb("nb", [128, UN, G4])
            inv2 = sb("inv2", [128, UN, G4]); rs2 = sb("rs2", [128, UN, G4]); nb2 = sb("nb2", [128, UN, G4])
            p_x, p_a, p_b, p_c0, p_c1, p_o = (ps(n) for n in ("p_x", "p_a", "p_b", "p_c0", "p_c1", "p_o"))
            p_h = ps("p_h", (128, 2, 512))
            arrived = [sem(f"arrived{u}") for u in range(UN)]
            out2, out3, outx, outh = ([sem(f"{n}{u}") for u in range(2)] for n in ("out2_", "out3_", "outx_", "outh_"))
            names = ("pe_xt", "act_xt", "pe_a", "act_a", "pe_b", "act_b", "pe_h1", "dve_h1", "pe_c", "act_c",
                     "pe_o", "dve_r", "dve_inv", "act_rs", "dve_nb", "act_x1", "dve_v", "dve_inv2", "act_rs2",
                     "dve_nb2", "act_x3", "pe_x3t", "act_x3t", "pe_h0", "dve_h0", "link1", "link2", "cleared")
            s = {n: sem(n) for n in names}
            last_rows = (N - (DG - 1) * GN) // G4
            block = ctx.enter_context(nc.Block())


            @block.sync
            def _(sp):
                sp.wait_ge(s["cleared"], 1)

                def step(k, u):
                    i = UN * k + u
                    if live(k, u, 0, DG):
                        wait(sp, s["dve_r"], i - UN + 1)
                        if isinstance(i, int) and i == DG - 1:
                            sp.dma_start(x[0:last_rows, u], a["x"][(DG - 1) * GN:N, :].rearrange("(p j) f -> p j f", j=G4)).then_inc(arrived[u], 16)
                        else:
                            t = a["x"][0:(DG - 1) * GN, :].rearrange("(g p j) f -> g p j f", p=128, j=G4)
                            sp.dma_start(x[:, u], t[bass.ds(i, 1)].rearrange("g p j f -> p (g j) f")).then_inc(arrived[u], 16)
                    for lag, done, table, rows, sems in ((2, "dve_h1", self.t2, h1, out2), (5, "act_x1", self.t3, x1, out3),
                                                         (7, "act_x3", self.x3, x3, outx), (9, "dve_h0", self.th[0], h0, outh)):
                        if live(k, u, lag, DG):
                            w = (u - lag) % 2
                            sp.wait_ge(s[done], i - lag + 1)
                            sp.dma_start(self.nodes(table, k, u, lag), rows[:, w]).then_inc(sems[w], 16)

                steps(sp, DG, 9, step, 3)
                for o in (out2, out3, outx, outh):
                    self.all_stored(sp, o, DG)

            @block.gpsimd
            def _(pool):
                nc.gpsimd.memset(x[:].rearrange("p a b c -> p (a b c)"), 0.0).then_inc(s["cleared"], 1)
                self.slot_gathers(pool, sb, sem)

            @block.tensor
            def _(pe):
                def step(k, u):
                    i = UN * k + u

                    def folded(tiles):
                        if live(k, u, 2, DG):
                            if tiles[0] == 0:
                                pe.wait_ge(s["act_c"], 2 * (i - 1))
                                wait(pe, s["dve_r"], i - 2)
                            for j in tiles:
                                for t in range(2):
                                    m = nc.tensor.matmul(p_o[:, j * D:(j + 1) * D], hh[:, u % 2, t, j * D:(j + 1) * D],
                                                         self.wc[:, t, :], start=(t == 0), stop=(t == 1))
                            if tiles[-1] == G4 - 1:
                                m.then_inc(s["pe_o"], 1)

                    def second(t):
                        if live(k, u, 1, DG):
                            wait(pe, s["act_c"], 2 * i - 3 + t)
                            nc.tensor.matmul((p_c0, p_c1)[t][:], self.w2a[:, t * D:(t + 1) * D], ht[:],
                                             start=True, stop=True).then_inc(s["pe_c"], 1)

                    if live(k, u, 1, DG):
                        self.hold(pe, (s["act_a"], i), (s["dve_h1"], i - 1))
                        nc.tensor.matmul(p_b[0:H, :], self.w1b[:], ha[:], start=True, stop=True).then_inc(s["pe_b"], 1)
                    if live(k, u, 0, DG):
                        pe.wait_ge(arrived[u], 16 * (k + 1))
                        wait(pe, s["act_x3t"], i - 7)
                        for j in range(G4):
                            m = nc.tensor.transpose(p_x[:, j * D:(j + 1) * D], x[:, u, j, :], self.ident[:])
                        m.then_inc(s["pe_xt"], 1)
                    folded((0, 1))
                    if live(k, u, 1, DG):
                        self.hold(pe, (s["act_b"], i))
                        for j in range(G4):
                            m = nc.tensor.transpose(p_b[:, j * H:(j + 1) * H], ht[:, j * D:(j + 1) * D], self.ident[0:H, 0:H])
                        m.then_inc(s["pe_h1"], 1)
                    second(0)
                    if live(k, u, 0, DG):
                        pe.wait_ge(s["act_xt"], i + 1)
                        wait(pe, s["act_a"], i)
                        nc.tensor.matmul(p_a[0:H, :], self.w1a[:], xt[:], start=True, stop=True).then_inc(s["pe_a"], 1)
                    second(1)
                    if live(k, u, 7, DG):
                        pe.wait_ge(s["act_x3"], i - 6)
                        pe.wait_ge(s["act_xt"], (i if not isinstance(i, int) else min(i, DG - 1)) + 1)
                        for j in range(G4):
                            m = nc.tensor.transpose(p_x[:, j * D:(j + 1) * D], x3[:, (u - 7) % 2, j, :], self.ident[:])
                        m.then_inc(s["pe_x3t"], 1)
                    folded((2, 3))
                    if live(k, u, 7, DG):
                        pe.wait_ge(s["act_x3t"], i - 6)
                        wait(pe, s["dve_h0"], i - 7)
                        self.gat_rows(x3t, p_h, 0).then_inc(s["pe_h0"], 1)

                steps(pe, DG, 7, step, 3)

            @block.scalar
            def _(act):
                def step(k, u):
                    i = UN * k + u

                    def rectify(t):
                        if live(k, u, 1, DG):
                            act.wait_ge(s["pe_c"], 2 * (i - 1) + t + 1)
                            wait(act, s["pe_o"], i - 2)
                            nc.scalar.activation(hh[:, (u - 1) % 2, t, :], (p_c0, p_c1)[t][:], ACT.Relu,
                                                 bias=self.b2a[:, t:t + 1]).then_inc(s["act_c"], 1)

                    if live(k, u, 1, DG):
                        act.wait_ge(s["pe_b"], i)
                        wait(act, s["pe_c"], 2 * (i - 1))
                        wait(act, s["pe_h1"], i - 1)
                        nc.scalar.activation(ht[:], p_b[0:H, :], ACT.Relu, bias=self.b1b[:]).then_inc(s["act_b"], 1)
                    if live(k, u, 0, DG):
                        act.wait_ge(s["pe_xt"], i + 1)
                        wait(act, s["pe_a"], i)
                        nc.scalar.activation(xt[:], p_x[:], ACT.Copy).then_inc(s["act_xt"], 1)
                    if live(k, u, 4, DG):
                        w = (u - 4) % UN
                        act.wait_ge(s["dve_nb"], i - 3)
                        self.stored(act, out3, k, u, 4)
                        wait(act, s["dve_v"], i - 5)
                        self.norm_apply(x1[:, w % 2], r[:, w % 2], rs[:, w, 0], nb[:, w]).then_inc(s["act_x1"], 1)
                    rectify(0)
                    if live(k, u, 0, DG):
                        act.wait_ge(s["pe_a"], i + 1)
                        wait(act, s["pe_b"], i)
                        nc.scalar.activation(ha[:], p_a[0:H, :], ACT.Relu, bias=self.b1a[:]).then_inc(s["act_a"], 1)
                    rectify(1)
                    if live(k, u, 7, DG):
                        act.wait_ge(s["pe_x3t"], i - 6)
                        wait(act, s["pe_h0"], i - 7)
                        nc.scalar.activation(x3t[:], p_x[:], ACT.Copy).then_inc(s["act_x3t"], 1)
                    if live(k, u, 6, DG):
                        w = (u - 6) % UN
                        act.wait_ge(s["dve_nb2"], i - 5)
                        self.stored(act, outx, k, u, 6)
                        wait(act, s["pe_x3t"], i - 7)
                        self.norm_apply(x3[:, w % 2], v[:, w % 2], rs2[:, w], nb2[:, w]).then_inc(s["act_x3"], 1)
                    if live(k, u, 3, DG):
                        w = (u - 3) % UN
                        act.wait_ge(s["dve_inv"], i - 2)
                        nc.scalar.activation(rs[:, w], inv[:, w], ACT.Sqrt).then_inc(s["act_rs"], 1)
                    if live(k, u, 5, DG):
                        w = (u - 5) % UN
                        act.wait_ge(s["dve_inv2"], i - 4)
                        nc.scalar.activation(rs2[:, w], inv2[:, w], ACT.Sqrt).then_inc(s["act_rs2"], 1)

                steps(act, DG, 7, step, 3)

            @block.vector
            def _(dve):
                link1 = Chain(dve, s["link1"], 7)
                link2 = Chain(dve, s["link2"], 3)

                def step(k, u):
                    i = UN * k + u
                    w3, w5 = (u - 3) % UN, (u - 5) % UN

                    def rows_out(half):
                        if live(k, u, 8, DG):
                            if half == 0:
                                dve.wait_ge(s["pe_h0"], i - 7)
                                self.stored(dve, outh, k, u, 8)
                            last = self.gat_rows_out(h0[:, u % 2], p_h, 0, half=(half,))
                            if half == 1:
                                last.then_inc(s["dve_h0"], 1)

                    def stats1(n):
                        if live(k, u, 3, DG):
                            if n == 0:
                                link1.last()
                            last = self.norm_part(n, lambda j: r[:, w3 % 2, j, :], st, mv[:, w3], inv[:, w3, 0], link1)
                            if n == 3:
                                link1(last)
                                link1(nc.vector.tensor_tensor(inv[:, w3, 1], mv[:, w3, :, 1], inv[:, w3, 0], ALU.mult))
                                link1(nc.vector.tensor_scalar(inv[:, w3, 1], inv[:, w3, 1], EPS, None, ALU.add))
                                nc.vector.reciprocal(inv[:, w3, 1], inv[:, w3, 1]).then_inc(s["dve_inv"], 1)

                    def stats2(n):
                        if live(k, u, 5, DG):
                            if n == 0:
                                dve.wait_ge(s["dve_v"], i - 4)
                            last = self.norm_part(n, lambda j: v[:, w5 % 2, j, :], st2, mv2[:, w5], inv2[:, w5], link2)
                            if n == 3:
                                last.then_inc(s["dve_inv2"], 1)

                    if live(k, u, 3, DG):
                        link1.group(i - 3)
                        dve.wait_ge(s["pe_o"], i - 2)
                        wait(dve, s["act_x1"], i - 4)
                        nc.vector.tensor_tensor(r[:, w3 % 2].rearrange("p a b -> p (a b)"), p_o[:],
                                                x[:, w3].rearrange("p a b -> p (a b)"), ALU.add).then_inc(s["dve_r"], 1)
                    rows_out(0)
                    if live(k, u, 3, DG):
                        dve.wait_ge(s["dve_r"], i - 2)
                        link1.put(nc.vector.tensor_tensor(r[:, w3 % 2], r[:, w3 % 2], self.each(self.bc[:]), ALU.add))
                    rows_out(1)
                    if live(k, u, 4, DG):
                        w = (u - 4) % UN
                        dve.wait_ge(s["act_rs"], i - 3)
                        self.norm_shift(mv[:, w], rs[:, w, 0], nb[:, w]).then_inc(s["dve_nb"], 1)
                    stats1(0)
                    if live(k, u, 5, DG):
                        link2.group(i - 5)
                        dve.wait_ge(s["act_x1"], i - 4)
                        wait(dve, s["act_x3"], i - 6)
                        for j in range(G4):
                            m = nc.vector.scalar_tensor_tensor(out=v[:, w5 % 2, j, :], in0=x1[:, w5 % 2, j, :], scalar=rs[:, w5, 1, j:j + 1],
                                                               in1=self.bg[:], op0=ALU.mult, op1=ALU.add)
                        m.then_inc(s["dve_v"], 1)
                    stats1(1)
                    if live(k, u, 6, DG):
                        w = (u - 6) % UN
                        dve.wait_ge(s["act_rs2"], i - 5)
                        self.norm_shift(mv2[:, w], rs2[:, w], nb2[:, w]).then_inc(s["dve_nb2"], 1)
                    if live(k, u, 1, DG):
                        dve.wait_ge(s["pe_h1"], i)
                        self.stored(dve, out2, k, u, 1)
                        nc.vector.tensor_copy(h1[:, (u - 1) % 2].rearrange("p a b -> p (a b)"), p_b[:, 0:G4 * H]).then_inc(s["dve_h1"], 1)
                    stats1(2)
                    stats2(0)
                    stats1(3)
                    stats2(1)
                    stats2(2)
                    stats2(3)

                steps(dve, DG, 8, step, 3)

    def cx2(self, l):
        return self.cx[:, l, :].rearrange("p (o f) -> p o f", o=1).to_broadcast([128, 2, XW])

    def select_group(self, m, k, u, lag, weight=None, tiles=range(G4)):
        nc = self.nc
        c0 = (UN * k + u - lag) * G4
        if weight is None:
            q = self.q[:, bass.ds(c0, G4)].rearrange("p (c o) -> p c o", o=1).to_broadcast([128, G4, 128])
            return nc.vector.tensor_tensor(m, self.each(self.iota[:]), q, ALU.is_equal)
        for j in tiles:
            last = nc.vector.tensor_scalar(m[:, j, :], self.iota[:], self.q[:, bass.ds(c0 + j, 1)],
                                           weight[:, bass.ds(c0 + j, 1)], ALU.is_equal, ALU.mult)
        return last

    def sum_chunk(self, pe, n, j, out, m, msg, carried, summed):
        wait(pe, carried, n * G4 + j)
        self.nc.tensor.matmul(out, m[:, j, :], msg, start=True, stop=True).then_inc(summed, 1)

    def carry_chunk(self, act, n, j, row0, out, carried, summed):
        act.wait_ge(summed, n * G4 + j)
        self.nc.scalar.activation(row0, out, ACT.Copy).then_inc(carried, 1)

    def wait_sums(self, dve, n, carried, summed):
        dve.wait_ge(summed, (n + 1) * G4)
        dve.wait_ge(carried, min(n + 1, AG - 1) * G4 + (G4 - 1 if n == AG - 1 else 0) if isinstance(n, int) else (n + 1) * G4)

    def ring_gather(self, nc, pool, sb, sem, idx, table, width, ring, arrived, summed, count=AG):
        stage = sb("g_stage", [128, UN, G4], I32)
        staged = sem("g_staged")

        def step(k, u):
            def freed(k, u):
                return ((summed, (UN * k + u - UN + 1) * G4),)
            self.gather_group(pool, k, u, count, idx, stage, staged, table, ring, width, arrived, freed)

        steps(pool, count, 0, step)

    def stored(self, eng, sems, k, u, lag):
        n = UN * k + u - lag
        if len(sems) == UN:
            if not isinstance(n, int):
                eng.wait_ge(sems[(u - lag) % UN], 16 * (k + (u - lag) // UN))
            elif n >= UN:
                eng.wait_ge(sems[n % UN], 16 * (n // UN))
        elif not isinstance(n, int):
            eng.wait_ge(sems[(u - lag) % 2], 16 * (2 * k + (u - lag) // 2))
        elif n >= 2:
            eng.wait_ge(sems[n % 2], 16 * (n // 2))

    def stored_rows(self, eng, sem, times):
        wait(eng, sem, 16 * G4 * times)

    def all_stored(self, eng, sems, count):
        for w, sem in enumerate(sems):
            eng.wait_ge(sem, 16 * ((count + len(sems) - 1 - w) // len(sems)))

    def phase_gin1(self):
        nc = self.nc
        ctx, sb, ps, sem = self.scope("g1")
        W1 = XW
        with ctx:
            xd = sb("xd", [128, UN, G4, D]); m = sb("m", [128, 2, G4, 128])
            r = sb("r", [128, 2, G4, D]); rt = sb("rt", [D, GN]); ha = sb("ha", [H, GN]); ht = sb("ht", [H, 2, GN])
            h1 = sb("h1", [128, 2, G4, H]); tmp = sb("tmp", [128, 3, CHUNKS])
            p_s = ps("p_s", (128, 2, 2, 512)); p_t, p_a, p_b, p_h = (ps(n) for n in ("p_t", "p_a", "p_b", "p_h"))
            arrived = [sem(f"arrived{u}") for u in range(UN)]
            out2 = [sem(f"out2_{u}") for u in range(2)]
            names = ("dve_m", "summed", "carried", "dve_r", "pe_t", "act_t", "pe_a", "act_a", "pe_b", "act_b", "pe_h", "dve_h", "fin", "root")
            s = {n: sem(n) for n in names}
            block = ctx.enter_context(nc.Block())
            place = lambda w, j: (w, j // 2, slice((j % 2) * XW, (j % 2) * XW + W1))


            @block.gpsimd
            def _(pool):
                self.map_gathers(pool, sb, sem)

            @block.sync
            def _(sp):
                def step(k, u):
                    i = UN * k + u
                    if live(k, u, 0, AG):
                        wait(sp, s["dve_r"], i - UN + 1)
                        sp.dma_start(xd[:, u], self.slots(self.xd, k, u)).then_inc(arrived[u], 16)
                    if live(k, u, 7, AG):
                        w = (u - 7) % 2
                        sp.wait_ge(s["dve_h"], i - 6)
                        sp.dma_start(self.slots(self.t2, k, u, 7), h1[:, w]).then_inc(out2[w], 16)

                steps(sp, AG, 7, step, 2)
                self.all_stored(sp, out2, AG)

            @block.tensor
            def _(pe):
                def step(k, u):
                    i = UN * k + u
                    w1, n1 = (u - 1) % 2, i - 1

                    def sums(j):
                        if live(k, u, 1, AG):
                            if j == 0:
                                pe.wait_ge(s["dve_m"], i)
                                wait(pe, s["dve_r"], i - 2)
                            a_, b_, c_ = place(w1, j)
                            self.sum_chunk(pe, n1, j, p_s[:, a_, b_, c_], m[:, w1],
                                           self.msgs[:, bass.ds(n1 * G4 + j, 1), :].rearrange("p o f -> p (o f)"),
                                           s["carried"], s["summed"])

                    sums(0)
                    if live(k, u, 4, AG):
                        pe.wait_ge(s["act_t"], i - 3)
                        wait(pe, s["act_a"], i - 4)
                        nc.tensor.matmul(p_a[0:H, :], self.w1a[:], rt[:], start=True, stop=True).then_inc(s["pe_a"], 1)
                    sums(1)
                    if live(k, u, 3, AG):
                        pe.wait_ge(s["dve_r"], i - 2)
                        wait(pe, s["act_t"], i - 3)
                        for j in range(G4):
                            t = nc.tensor.transpose(p_t[:, j * D:(j + 1) * D], r[:, (u - 3) % 2, j, :], self.ident[:])
                        t.then_inc(s["pe_t"], 1)
                    sums(2)
                    if live(k, u, 4, AG):
                        self.hold(pe, (s["act_a"], i - 3), (s["act_b"], i - 4))
                        nc.tensor.matmul(p_b[0:H, :], self.w1b[:], ha[:], start=True, stop=True).then_inc(s["pe_b"], 1)
                    sums(3)
                    if live(k, u, 5, AG):
                        w = (u - 5) % 2
                        self.hold(pe, (s["dve_h"], i - 5), (s["act_b"], i - 4))
                        for j in range(G4):
                            t = nc.tensor.transpose(p_h[:, j * H:(j + 1) * H], ht[:, w, j * D:(j + 1) * D], self.ident[0:H, 0:H])
                        t.then_inc(s["pe_h"], 1)

                steps(pe, AG, 5, step, 2)

            @block.scalar
            def _(act):
                def step(k, u):
                    i = UN * k + u
                    w1, n1 = (u - 1) % 2, i - 1

                    def carry(j):
                        if live(k, u, 1, AG):
                            if j == G4 and isinstance(i, int) and n1 == AG - 1:
                                return
                            a_, b_, c_ = place(w1, j - 1)
                            self.carry_chunk(act, n1, j, self.msgs[0:1, bass.ds(n1 * G4 + j, 1), :].rearrange("p o f -> p (o f)"),
                                             p_s[0:1, a_, b_, c_], s["carried"], s["summed"])

                    carry(1)
                    if live(k, u, 4, AG):
                        act.wait_ge(s["pe_a"], i - 3)
                        wait(act, s["pe_b"], i - 4)
                        nc.scalar.activation(ha[:], p_a[0:H, :], ACT.Relu, bias=self.b1a[:]).then_inc(s["act_a"], 1)
                    carry(2)
                    if live(k, u, 3, AG):
                        act.wait_ge(s["pe_t"], i - 2)
                        wait(act, s["pe_a"], i - 3)
                        nc.scalar.activation(rt[:], p_t[:], ACT.Copy).then_inc(s["act_t"], 1)
                    carry(3)
                    if live(k, u, 4, AG):
                        act.wait_ge(s["pe_b"], i - 3)
                        wait(act, s["pe_h"], i - 5)
                        nc.scalar.activation(ht[:, u % 2], p_b[0:H, :], ACT.Relu, bias=self.b1b[:]).then_inc(s["act_b"], 1)
                    carry(4)

                steps(act, AG, 4, step, 2)
                act.wait_ge(s["fin"], 2)
                nc.scalar.activation(self.dis[:], tmp[:, 1, :], ACT.Sqrt).then_inc(s["root"], 1)

            @block.vector
            def _(dve):
                def step(k, u):
                    i = UN * k + u
                    if live(k, u, 6, AG):
                        w = u % 2
                        dve.wait_ge(s["pe_h"], i - 5)
                        self.stored(dve, out2, k, u, 6)
                        nc.vector.tensor_copy(h1[:, w].rearrange("p a b -> p (a b)"), p_h[:, 0:G4 * H]).then_inc(s["dve_h"], 1)
                    if live(k, u, 2, AG):
                        w = u % 2
                        self.wait_sums(dve, i - 2, s["carried"], s["summed"])
                        dve.wait_ge(arrived[(u - 2) % UN], 16 * (k + (u - 2) // UN + 1))
                        wait(dve, s["pe_t"], i - 3)
                        for b in range(2):
                            t = p_s[:, w, b, 0:2 * XW].rearrange("p (a f) -> p a f", a=2)
                            nc.vector.tensor_copy(self.deg[:, bass.ds((i - 2) * G4 + 2 * b, 2), :], t[:, :, D:XW])
                            last = nc.vector.tensor_tensor(r[:, w, 2 * b:2 * b + 2, :], t[:, :, 0:D],
                                                           xd[:, (u - 2) % UN, 2 * b:2 * b + 2, :], ALU.add)
                        last.then_inc(s["dve_r"], 1)
                    if live(k, u, 0, AG):
                        wait(dve, s["summed"], (i - 1) * G4)
                        self.select_group(m[:, u % 2], k, u, 0).then_inc(s["dve_m"], 1)

                steps(dve, AG, 6, step, 2)
                dve.wait_ge(s["dve_r"], AG)
                deg = self.deg[:, :, 0]
                nc.vector.tensor_scalar(tmp[:, 0, :], deg, 1.0, None, ALU.max).then_inc(s["fin"], 1)
                dve.wait_ge(s["fin"], 1)
                nc.vector.reciprocal(tmp[:, 1, :], tmp[:, 0, :]).then_inc(s["fin"], 1)
                nc.vector.tensor_scalar(tmp[:, 2, :], deg, 0.5, None, ALU.is_gt).then_inc(s["fin"], 1)
                dve.wait_ge(s["fin"], 3)
                dve.wait_ge(s["root"], 1)
                nc.vector.tensor_tensor(self.dis[:], self.dis[:], tmp[:, 2, :], ALU.mult).then_inc(s["fin"], 1)
                for l in range(3):
                    nc.vector.tensor_tensor(self.deg[:, :, 1 + l], self.deg[:, :, 1 + l], tmp[:, 1, :], ALU.mult).then_inc(s["fin"], 1)

    def phase_gin2(self):
        nc = self.nc
        ctx, sb, ps, sem = self.scope("g2")
        with ctx:
            ring = sb("ring", [128, UN, G4, H]); hs = sb("hs", [128, UN, G4, H]); xd = sb("xd", [128, UN, G4, D])
            m = sb("m", [128, 2, G4, 128]); r = sb("r", [128, 2, G4, H]); rt = sb("rt", [H, GN])
            hh = sb("hh", [D, 2, 2, GN]); y = sb("y", [128, UN, G4, D]); x1 = sb("x1", [128, 2, G4, D])
            st = sb("st", [128, G4, 6]); mv = sb("mv", [128, UN, G4, 2])
            inv = sb("inv", [128, UN, G4]); rs = sb("rs", [128, UN, G4]); nb = sb("nb", [128, UN, G4])
            p_s = [ps(f"p_s{w}") for w in range(2)]
            p_t, p_c0, p_c1, p_o = (ps(n) for n in ("p_t", "p_c0", "p_c1", "p_o"))
            garr = [sem(f"garr{u}") for u in range(UN)]
            arrived = [sem(f"arrived{u}") for u in range(UN)]
            arrivedx = [sem(f"arrivedx{u}") for u in range(UN)]
            out3 = [sem(f"out3_{u}") for u in range(2)]
            names = ("dve_m", "summed", "carried", "dve_r", "pe_t", "act_t", "pe_c", "act_c", "pe_o", "dve_y",
                     "dve_inv", "act_rs", "dve_nb", "act_x1", "link")
            s = {n: sem(n) for n in names}
            block = ctx.enter_context(nc.Block())

            @block.gpsimd
            def _(pool):
                self.ring_gather(nc, pool, sb, sem, self.row_i, self.t2, H, ring, garr, s["summed"])

            @block.sync
            def _(sp):
                def step(k, u):
                    i = UN * k + u
                    if live(k, u, 0, AG):
                        wait(sp, s["dve_r"], i - UN + 1)
                        sp.dma_start(hs[:, u], self.slots(self.t2, k, u)).then_inc(arrived[u], 16)
                    if live(k, u, 3, AG):
                        w = (u - 3) % UN
                        wait(sp, s["dve_y"], i - 3 - UN + 1)
                        sp.dma_start(xd[:, w], self.slots(self.xd, k, u, 3)).then_inc(arrivedx[w], 16)
                    if live(k, u, 8, AG):
                        w = u % 2
                        sp.wait_ge(s["act_x1"], i - 7)
                        sp.dma_start(self.slots(self.t3, k, u, 8), x1[:, w]).then_inc(out3[w], 16)

                steps(sp, AG, 8, step, 3)
                self.all_stored(sp, out3, AG)

            @block.tensor
            def _(pe):
                def step(k, u):
                    i = UN * k + u
                    w1, n1 = (u - 1) % 2, i - 1

                    def sums(j):
                        if live(k, u, 1, AG):
                            if j == 0:
                                pe.wait_ge(s["dve_m"], i)
                                pe.wait_ge(garr[(u - 1) % UN], 16 * G4 * (k + (0 if u < 1 else 1)))
                                wait(pe, s["dve_r"], i - 2)
                            self.sum_chunk(pe, n1, j, p_s[w1][:, j * H:(j + 1) * H], m[:, w1],
                                           ring[:, (u - 1) % UN, j, :], s["carried"], s["summed"])

                    def second(j):
                        if live(k, u, 4, AG):
                            if j == 0:
                                pe.wait_ge(s["act_c"], 2 * (i - 3))
                                wait(pe, s["dve_y"], i - 4)
                            for t in range(2):
                                mm = nc.tensor.matmul(p_o[:, j * D:(j + 1) * D], hh[:, u % 2, t, j * D:(j + 1) * D],
                                                      self.wc[:, t, :], start=(t == 0), stop=(t == 1))
                            if j == G4 - 1:
                                mm.then_inc(s["pe_o"], 1)

                    def first(t):
                        if live(k, u, 3, AG):
                            if t == 0:
                                pe.wait_ge(s["act_t"], i - 2)
                            wait(pe, s["act_c"], 2 * (i - 3) + t - 1)
                            nc.tensor.matmul((p_c0, p_c1)[t][:], self.w2a[:, t * D:(t + 1) * D], rt[:],
                                             start=True, stop=True).then_inc(s["pe_c"], 1)

                    sums(0)
                    if live(k, u, 3, AG):
                        self.hold(pe, (s["dve_r"], i - 2), (s["act_t"], i - 3))
                        for j in range(G4):
                            t = nc.tensor.transpose(p_t[0:H, j * D:(j + 1) * D], r[:, (u - 3) % 2, j, :], self.ident[:])
                        t.then_inc(s["pe_t"], 1)
                    sums(1)
                    second(0)
                    sums(2)
                    first(0)
                    sums(3)
                    first(1)
                    for j in range(1, G4):
                        second(j)

                steps(pe, AG, 4, step, 3)

            @block.scalar
            def _(act):
                def step(k, u):
                    i = UN * k + u
                    w1, n1 = (u - 1) % 2, i - 1

                    def carry(j):
                        if live(k, u, 1, AG):
                            if j == G4 and isinstance(i, int) and n1 == AG - 1:
                                return
                            if j == G4:
                                act.wait_ge(garr[u], 16 * G4 * (k + 1))
                            if j == 1:
                                act.wait_ge(garr[(u - 1) % UN], 16 * G4 * (k + (0 if u < 1 else 1)))
                            self.carry_chunk(act, n1, j, ring[0:1, (u - 1 + j // G4) % UN, j % G4, :],
                                             p_s[w1][0:1, (j - 1) * H:j * H], s["carried"], s["summed"])

                    def rectify(t):
                        if live(k, u, 3, AG):
                            act.wait_ge(s["pe_c"], 2 * (i - 3) + t + 1)
                            wait(act, s["pe_o"], i - 4)
                            nc.scalar.activation(hh[:, (u - 3) % 2, t, :], (p_c0, p_c1)[t][:], ACT.Relu,
                                                 bias=self.b2a[:, t:t + 1]).then_inc(s["act_c"], 1)

                    def norm(tiles):
                        if live(k, u, 7, AG):
                            w = (u - 7) % UN
                            if tiles[0] == 0:
                                act.wait_ge(s["dve_nb"], i - 6)
                                self.stored(act, out3, k, u, 7)
                            last = self.norm_apply(x1[:, w % 2], y[:, w], rs[:, w], nb[:, w], tiles)
                            if tiles[-1] == G4 - 1:
                                last.then_inc(s["act_x1"], 1)

                    if live(k, u, 6, AG):
                        w = (u - 6) % UN
                        act.wait_ge(s["dve_inv"], i - 5)
                        nc.scalar.activation(rs[:, w], inv[:, w], ACT.Sqrt).then_inc(s["act_rs"], 1)
                    carry(1)
                    if live(k, u, 3, AG):
                        act.wait_ge(s["pe_t"], i - 2)
                        wait(act, s["pe_c"], 2 * (i - 3))
                        nc.scalar.activation(rt[:], p_t[0:H, :], ACT.Copy).then_inc(s["act_t"], 1)
                    carry(2)
                    norm((0, 1))
                    carry(3)
                    rectify(0)
                    carry(4)
                    norm((2, 3))
                    rectify(1)

                steps(act, AG, 7, step, 3)

            @block.vector
            def _(dve):
                link = Chain(dve, s["link"], 4)

                def step(k, u):
                    i = UN * k + u
                    v = (u - 5) % UN

                    def stats(n):
                        if live(k, u, 5, AG):
                            if n == 0:
                                link.last()
                            last = self.norm_part(n, lambda j: y[:, v, j, :], st, mv[:, v], inv[:, v], link)
                            if n == 3:
                                last.then_inc(s["dve_inv"], 1)

                    if live(k, u, 5, AG):
                        link.group(i - 5)
                        dve.wait_ge(s["pe_o"], i - 4)
                        dve.wait_ge(arrivedx[v], 16 * (k + (u - 5) // UN + 1))
                        wait(dve, s["act_x1"], i - 5 - UN + 1)
                        nc.vector.tensor_tensor(y[:, v].rearrange("p a b -> p (a b)"), p_o[:],
                                                xd[:, v].rearrange("p a b -> p (a b)"), ALU.add).then_inc(s["dve_y"], 1)
                    if live(k, u, 2, AG):
                        w = u % 2
                        self.wait_sums(dve, i - 2, s["carried"], s["summed"])
                        dve.wait_ge(arrived[(u - 2) % UN], 16 * (k + (u - 2) // UN + 1))
                        wait(dve, s["pe_t"], i - 3)
                        nc.vector.tensor_tensor(r[:, w].rearrange("p a b -> p (a b)"), p_s[w][:, 0:G4 * H],
                                                hs[:, (u - 2) % UN].rearrange("p a b -> p (a b)"), ALU.add).then_inc(s["dve_r"], 1)
                    if live(k, u, 5, AG):
                        dve.wait_ge(s["dve_y"], i - 4)
                        link.put(nc.vector.tensor_tensor(y[:, v], y[:, v], self.each(self.bc[:]), ALU.add))
                    if live(k, u, 0, AG):
                        wait(dve, s["summed"], (i - 1) * G4)
                        self.select_group(m[:, u % 2], k, u, 0).then_inc(s["dve_m"], 1)
                    stats(0)
                    stats(1)
                    stats(2)
                    stats(3)
                    if live(k, u, 6, AG):
                        w = (u - 6) % UN
                        dve.wait_ge(s["act_rs"], i - 5)
                        self.norm_shift(mv[:, w], rs[:, w], nb[:, w]).then_inc(s["dve_nb"], 1)

                steps(dve, AG, 6, step, 3)

    def phase_rgcn(self):
        nc = self.nc
        ctx, sb, ps, sem = self.scope("rg")
        with ctx:
            ring = sb("ring", [128, UN, G4, D]); x1 = sb("x1", [128, UN, G4, D])
            gt = sb("gt", [D, 2, GN]); mg = sb("mg", [128, 2, G4, D]); m = sb("m", [128, 2, G4, 128])
            r = sb("r", [128, UN, G4, D]); x2 = sb("x2", [128, UN, G4, D]); z = sb("z", [128, 2, G4, D])
            st = sb("st", [128, G4, 6]); mv = sb("mv", [128, UN, G4, 2])
            inv = sb("inv", [128, UN, G4]); rs = sb("rs", [128, UN, G4]); nb = sb("nb", [128, UN, G4])
            p_t = ps("p_t"); p_b = [ps(f"p_b{j}") for j in range(G4)]; p_s = [ps(f"p_s{w}") for w in range(2)]
            garr = [sem(f"garr{u}") for u in range(UN)]
            arrived = [sem(f"arrived{u}") for u in range(UN)]
            outx = [sem(f"outx_{u}") for u in range(UN)]; outz = [sem(f"outz_{u}") for u in range(2)]
            names = ("pe_t", "act_t", "pe_b", "act_m", "dve_part", "dve_m", "summed", "carried", "dve_r",
                     "dve_inv", "act_rs", "dve_nb", "act_x2", "pool_z", "link")
            s = {n: sem(n) for n in names}
            block = ctx.enter_context(nc.Block())

            @block.gpsimd
            def _(pool):
                stage = sb("g_stage", [128, UN, G4], I32)
                staged = sem("g_staged")

                def step(k, u):
                    def freed(k, u):
                        return ((s["pe_t"], UN * k + u - UN + 1),)
                    if live(k, u, 0, AG):
                        self.gather_group(pool, k, u, AG, self.row_i, stage, staged, self.t3, ring, D, garr, freed)
                    if live(k, u, 7, AG):
                        w, n = (u - 7) % UN, UN * k + u - 7
                        if isinstance(n, int) and n < 2:
                            self.hold(pool, (s["act_x2"], n + 1))
                        else:
                            times = n // 2 if isinstance(n, int) else 2 * k + (u - 7) // 2
                            self.hold(pool, (s["act_x2"], n + 1), (outz[w % 2], 16 * times))
                        dis = self.dis[:, bass.ds(n * G4, G4)].rearrange("p (c o) -> p c o", o=1).to_broadcast([128, G4, D])
                        nc.gpsimd.tensor_tensor(z[:, w % 2], x2[:, w], dis, ALU.mult).then_inc(s["pool_z"], 1)

                steps(pool, AG, 7, step, 3)

            @block.sync
            def _(sp):
                def step(k, u):
                    i = UN * k + u
                    if live(k, u, 2, AG):
                        w = (u - 2) % UN
                        wait(sp, s["dve_r"], i - 2 - UN + 1)
                        sp.dma_start(x1[:, w], self.slots(self.t3, k, u, 2)).then_inc(arrived[w], 16)
                    if live(k, u, 8, AG):
                        sp.wait_ge(s["act_x2"], i - 7)
                        sp.dma_start(self.slots(self.x2, k, u, 8), x2[:, u]).then_inc(outx[u], 16)
                        sp.wait_ge(s["pool_z"], i - 7)
                        sp.dma_start(self.slots(self.t4, k, u, 8), z[:, u % 2]).then_inc(outz[u % 2], 16)

                steps(sp, AG, 8, step, 3)
                self.all_stored(sp, outx, AG)
                self.all_stored(sp, outz, AG)

            @block.tensor
            def _(pe):
                def step(k, u):
                    i = UN * k + u

                    def product(j):
                        if live(k, u, 1, AG):
                            if j == 0:
                                pe.wait_ge(s["act_t"], i)
                            wait(pe, s["dve_part"], (i - 2) * G4 + j + 1)
                            nc.tensor.matmul(p_b[j][:], gt[:, (u - 1) % 2, j * D:(j + 1) * D],
                                             self.bases[:].rearrange("i b o -> i (b o)"),
                                             start=True, stop=True).then_inc(s["pe_b"], 1)

                    def sums(j):
                        if live(k, u, 3, AG):
                            w = (u - 3) % 2
                            if j == 0:
                                pe.wait_ge(s["dve_m"], i - 2)
                                pe.wait_ge(s["dve_part"], (i - 2) * G4)
                                wait(pe, s["dve_r"], i - 4)
                            self.sum_chunk(pe, i - 3, j, p_s[w][:, j * D:(j + 1) * D], m[:, w], mg[:, w, j, :],
                                           s["carried"], s["summed"])

                    sums(0)
                    if live(k, u, 0, AG):
                        pe.wait_ge(garr[u], 16 * G4 * (k + 1))
                        wait(pe, s["act_t"], i)
                        for j in range(G4):
                            t = nc.tensor.transpose(p_t[:, j * D:(j + 1) * D], ring[:, u, j, :], self.ident[:])
                        t.then_inc(s["pe_t"], 1)
                    sums(1)
                    product(0)
                    sums(2)
                    product(1)
                    sums(3)
                    product(2)
                    product(3)

                steps(pe, AG, 3, step, 3)

            @block.scalar
            def _(act):
                def step(k, u):
                    i = UN * k + u

                    def carry(j):
                        if live(k, u, 3, AG):
                            n1 = i - 3
                            if isinstance(i, int) and j == G4 and n1 == AG - 1:
                                return
                            w = (u - 3) % 2
                            if j == G4:
                                act.wait_ge(s["dve_part"], (n1 + 2) * G4)
                            if j == 1:
                                act.wait_ge(s["dve_part"], (n1 + 1) * G4)
                            self.carry_chunk(act, n1, j, mg[0:1, (w + j // G4) % 2, j % G4, :],
                                             p_s[w][0:1, (j - 1) * D:j * D], s["carried"], s["summed"])

                    def first(j):
                        if live(k, u, 2, AG):
                            act.wait_ge(s["pe_b"], (i - 2) * G4 + j + 1)
                            wait(act, s["summed"], (i - 3) * G4)
                            nc.scalar.activation(mg[:, u % 2, j, :], p_b[j][:, 0:D], ACT.Copy,
                                                 scale=self.coef[:, 0, bass.ds((i - 2) * G4 + j, 1)]).then_inc(s["act_m"], 1)

                    def norm(tiles):
                        if live(k, u, 6, AG):
                            w = (u - 6) % UN
                            if tiles[0] == 0:
                                act.wait_ge(s["dve_nb"], i - 5)
                                self.stored(act, outx, k, u, 6)
                                wait(act, s["pool_z"], i - 6 - UN + 1)
                            last = self.norm_apply(x2[:, w], r[:, w], rs[:, w], nb[:, w], tiles)
                            if tiles[-1] == G4 - 1:
                                last.then_inc(s["act_x2"], 1)

                    first(0)
                    first(1)
                    carry(1)
                    if live(k, u, 5, AG):
                        w = (u - 5) % UN
                        act.wait_ge(s["dve_inv"], i - 4)
                        nc.scalar.activation(rs[:, w], inv[:, w], ACT.Sqrt).then_inc(s["act_rs"], 1)
                    first(2)
                    first(3)
                    carry(2)
                    if live(k, u, 0, AG):
                        act.wait_ge(s["pe_t"], i + 1)
                        wait(act, s["pe_b"], (i - 1) * G4)
                        nc.scalar.activation(gt[:, u % 2, :], p_t[:], ACT.Copy).then_inc(s["act_t"], 1)
                    norm((0, 1))
                    carry(3)
                    norm((2, 3))
                    carry(4)

                steps(act, AG, 6, step, 3)

            @block.vector
            def _(dve):
                link = Chain(dve, s["link"], 3)
                parts = Chain(dve, sem("parts"), 4)

                def step(k, u):
                    i = UN * k + u
                    v = u % UN

                    def part(b, half):
                        if live(k, u, 2, AG):
                            if b == 1 and half == 0:
                                parts.group(i - 2)
                            if b > 1:
                                parts.last()
                            for j in (2 * half, 2 * half + 1):
                                if b == 1:
                                    dve.wait_ge(s["act_m"], (i - 2) * G4 + j + 1)
                                last = nc.vector.scalar_tensor_tensor(
                                    out=mg[:, u % 2, j, :], in0=p_b[j][:, b * D:(b + 1) * D],
                                    scalar=self.coef[:, b, bass.ds((i - 2) * G4 + j, 1)], in1=mg[:, u % 2, j, :],
                                    op0=ALU.mult, op1=ALU.add)
                                if b == 3:
                                    last.then_inc(s["dve_part"], 1)
                            if b < 3:
                                parts.put(last)

                    def stats(n):
                        if live(k, u, 4, AG):
                            if n == 0:
                                dve.wait_ge(s["dve_r"], i - 3)
                            last = self.norm_part(n, lambda j: r[:, v, j, :], st, mv[:, v], inv[:, v], link)
                            if n == 3:
                                last.then_inc(s["dve_inv"], 1)

                    part(1, 0)
                    if live(k, u, 4, AG):
                        link.group(i - 4)
                        self.wait_sums(dve, i - 4, s["carried"], s["summed"])
                        dve.wait_ge(arrived[v], 16 * k)
                        wait(dve, s["act_x2"], i - 4 - UN + 1)
                        nc.vector.tensor_tensor(r[:, v].rearrange("p a b -> p (a b)"), p_s[u % 2][:],
                                                x1[:, v].rearrange("p a b -> p (a b)"), ALU.add).then_inc(s["dve_r"], 1)
                    part(2, 0)
                    if live(k, u, 2, AG):
                        wait(dve, s["summed"], (i - 3) * G4)
                        self.select_group(m[:, u % 2], k, u, 2).then_inc(s["dve_m"], 1)
                    part(3, 0)
                    stats(0)
                    part(1, 1)
                    stats(1)
                    part(2, 1)
                    stats(2)
                    part(3, 1)
                    stats(3)
                    if live(k, u, 5, AG):
                        w = (u - 5) % UN
                        dve.wait_ge(s["act_rs"], i - 4)
                        self.norm_shift(mv[:, w], rs[:, w], nb[:, w]).then_inc(s["dve_nb"], 1)

                steps(dve, AG, 5, step, 3)

    def gat_rows(self, xt, p_h, layer, tiles=range(G4)):
        for j in tiles:
            last = self.nc.tensor.matmul(p_h[:, j // 2, (j % 2) * XW:(j % 2 + 1) * XW], xt[:, j * D:(j + 1) * D],
                                         self.wx[:, layer, :], start=True, stop=True)
        return last

    def gat_rows_out(self, rows, p_h, layer, group=None, half=(0, 1)):
        for b in half:
            if group is not None:
                self.nc.vector.tensor_tensor(self.att_s[:, bass.ds(group * G4 + 2 * b, 2), :],
                                             p_h[:, b, 0:2 * XW].rearrange("p (b f) -> p b f", b=2)[:, :, D:D + 3],
                                             self.cx2(layer)[:, :, D:D + 3], ALU.add)
            last = self.nc.vector.tensor_tensor(rows[:, 2 * b:2 * b + 2, :],
                                                p_h[:, b, 0:2 * XW].rearrange("p (b f) -> p b f", b=2),
                                                self.cx2(layer), ALU.add)
        return last

    def phase_gcn(self):
        nc = self.nc
        ctx, sb, ps, sem = self.scope("gc")
        with ctx:
            ring = sb("ring", [128, UN, G4, D]); x2 = sb("x2", [128, UN, G4, D])
            m = sb("m", [128, 2, G4, 128]); g = sb("g", [128, 2, G4, D]); gt = sb("gt", [D, GN])
            v = sb("v", [128, UN, G4, D]); x3 = sb("x3", [128, UN, G4, D]); x3t = sb("x3t", [D, GN])
            h0 = sb("h0", [128, 2, G4, XW])
            st = sb("st", [128, G4, 6]); mv = sb("mv", [128, UN, G4, 2])
            inv = sb("inv", [128, UN, G4]); rs = sb("rs", [128, UN, G4]); nb = sb("nb", [128, UN, G4])
            p_s = [ps(f"p_s{w}") for w in range(2)]; p_t, p_g, p_x = ps("p_t"), ps("p_g"), ps("p_x")
            p_h = ps("p_h", (128, 2, 512))
            garr = [sem(f"garr{u}") for u in range(UN)]
            arrived = [sem(f"arrived{u}") for u in range(UN)]
            outx = [sem(f"outx_{u}") for u in range(UN)]; outh = [sem(f"outh_{u}") for u in range(2)]
            names = ("dve_m", "summed", "carried", "dve_g", "pe_t", "act_t", "pe_g", "dve_v", "dve_inv", "act_rs",
                     "dve_nb", "act_x3", "pe_x", "act_x", "pe_h", "dve_h", "link")
            s = {n: sem(n) for n in names}
            block = ctx.enter_context(nc.Block())

            @block.gpsimd
            def _(pool):
                self.ring_gather(nc, pool, sb, sem, self.row4_i, self.t4, D, ring, garr, s["summed"])

            @block.sync
            def _(sp):
                def step(k, u):
                    i = UN * k + u
                    if live(k, u, 2, AG):
                        w = (u - 2) % UN
                        wait(sp, s["dve_v"], i - 2 - UN + 1)
                        sp.dma_start(x2[:, w], self.slots(self.x2, k, u, 2)).then_inc(arrived[w], 16)
                    if live(k, u, 8, AG):
                        sp.wait_ge(s["act_x3"], i - 7)
                        sp.dma_start(self.slots(self.x3, k, u, 8), x3[:, u]).then_inc(outx[u], 16)
                    if live(k, u, 9, AG):
                        w = (u - 9) % 2
                        sp.wait_ge(s["dve_h"], i - 8)
                        sp.dma_start(self.slots(self.th[0], k, u, 9), h0[:, w]).then_inc(outh[w], 16)

                steps(sp, AG, 9, step, 3)
                self.all_stored(sp, outx, AG)
                self.all_stored(sp, outh, AG)

            @block.tensor
            def _(pe):
                def step(k, u):
                    i = UN * k + u

                    def sums(j):
                        if live(k, u, 1, AG):
                            w = (u - 1) % 2
                            if j == 0:
                                pe.wait_ge(s["dve_m"], i)
                                pe.wait_ge(garr[(u - 1) % UN], 16 * G4 * (k + (0 if u < 1 else 1)))
                                wait(pe, s["dve_g"], i - 2)
                            self.sum_chunk(pe, i - 1, j, p_s[w][:, j * D:(j + 1) * D], m[:, w],
                                           ring[:, (u - 1) % UN, j, :], s["carried"], s["summed"])

                    sums(0)
                    if live(k, u, 3, AG):
                        pe.wait_ge(s["dve_g"], i - 2)
                        wait(pe, s["act_t"], i - 3)
                        for j in range(G4):
                            t = nc.tensor.transpose(p_t[:, j * D:(j + 1) * D], g[:, (u - 3) % 2, j, :], self.ident[:])
                        t.then_inc(s["pe_t"], 1)
                    sums(1)
                    if live(k, u, 7, AG):
                        pe.wait_ge(s["act_x3"], i - 6)
                        wait(pe, s["act_x"], i - 7)
                        for j in range(G4):
                            t = nc.tensor.transpose(p_x[:, j * D:(j + 1) * D], x3[:, (u - 7) % UN, j, :], self.ident[:])
                        t.then_inc(s["pe_x"], 1)
                    sums(2)
                    if live(k, u, 3, AG):
                        pe.wait_ge(s["act_t"], i - 2)
                        wait(pe, s["dve_v"], i - 3)
                        for j in range(G4):
                            t = nc.tensor.matmul(p_g[:, j * D:(j + 1) * D], gt[:, j * D:(j + 1) * D], self.wg[:],
                                                 start=True, stop=True)
                        t.then_inc(s["pe_g"], 1)
                    sums(3)
                    if live(k, u, 7, AG):
                        pe.wait_ge(s["act_x"], i - 6)
                        wait(pe, s["dve_h"], i - 7)
                        self.gat_rows(x3t, p_h, 0).then_inc(s["pe_h"], 1)

                steps(pe, AG, 7, step, 3)

            @block.scalar
            def _(act):
                def step(k, u):
                    i = UN * k + u

                    def carry(j):
                        if live(k, u, 1, AG):
                            if isinstance(i, int) and j == G4 and i == AG:
                                return
                            if j == G4:
                                act.wait_ge(garr[u], 16 * G4 * (k + 1))
                            if j == 1:
                                act.wait_ge(garr[(u - 1) % UN], 16 * G4 * (k + (0 if u < 1 else 1)))
                            self.carry_chunk(act, i - 1, j, ring[0:1, (u - 1 + j // G4) % UN, j % G4, :],
                                             p_s[(u - 1) % 2][0:1, (j - 1) * D:j * D], s["carried"], s["summed"])

                    def norm(tiles):
                        if live(k, u, 6, AG):
                            w = (u - 6) % UN
                            if tiles[0] == 0:
                                act.wait_ge(s["dve_nb"], i - 5)
                                self.stored(act, outx, k, u, 6)
                                wait(act, s["pe_x"], i - 6 - UN + 1)
                            last = self.norm_apply(x3[:, w], v[:, w], rs[:, w], nb[:, w], tiles)
                            if tiles[-1] == G4 - 1:
                                last.then_inc(s["act_x3"], 1)

                    if live(k, u, 5, AG):
                        w = (u - 5) % UN
                        act.wait_ge(s["dve_inv"], i - 4)
                        nc.scalar.activation(rs[:, w], inv[:, w], ACT.Sqrt).then_inc(s["act_rs"], 1)
                    carry(1)
                    norm((0, 1))
                    carry(2)
                    if live(k, u, 3, AG):
                        act.wait_ge(s["pe_t"], i - 2)
                        wait(act, s["pe_g"], i - 3)
                        nc.scalar.activation(gt[:], p_t[:], ACT.Copy).then_inc(s["act_t"], 1)
                    carry(3)
                    if live(k, u, 7, AG):
                        act.wait_ge(s["pe_x"], i - 6)
                        wait(act, s["pe_h"], i - 7)
                        nc.scalar.activation(x3t[:], p_x[:], ACT.Copy).then_inc(s["act_x"], 1)
                    carry(4)
                    norm((2, 3))

                steps(act, AG, 7, step, 3)

            @block.vector
            def _(dve):
                link = Chain(dve, s["link"], 4)

                def step(k, u):
                    i = UN * k + u
                    v_ = u % UN

                    def stats(n):
                        if live(k, u, 4, AG):
                            if n == 0:
                                link.last()
                            last = self.norm_part(n, lambda j: v[:, v_, j, :], st, mv[:, v_], inv[:, v_], link)
                            if n == 3:
                                last.then_inc(s["dve_inv"], 1)

                    def rows_out(half):
                        if live(k, u, 8, AG):
                            if half == 0:
                                dve.wait_ge(s["pe_h"], i - 7)
                                self.stored(dve, outh, k, u, 8)
                            last = self.gat_rows_out(h0[:, u % 2], p_h, 0, i - 8, (half,))
                            if half == 1:
                                last.then_inc(s["dve_h"], 1)

                    if live(k, u, 4, AG):
                        link.group(i - 4)
                        dve.wait_ge(s["pe_g"], i - 3)
                        dve.wait_ge(arrived[v_], 16 * k)
                        wait(dve, s["act_x3"], i - 4 - UN + 1)
                        nc.vector.tensor_tensor(v[:, v_].rearrange("p a b -> p (a b)"), p_g[:],
                                                x2[:, v_].rearrange("p a b -> p (a b)"), ALU.add).then_inc(s["dve_v"], 1)
                    rows_out(0)
                    if live(k, u, 4, AG):
                        dve.wait_ge(s["dve_v"], i - 3)
                        link.put(nc.vector.tensor_tensor(v[:, v_], v[:, v_], self.each(self.bg[:]), ALU.add))
                    rows_out(1)
                    stats(0)
                    if live(k, u, 2, AG):
                        self.wait_sums(dve, i - 2, s["carried"], s["summed"])
                        wait(dve, s["pe_t"], i - 3)
                        dis = self.dis[:, bass.ds((i - 2) * G4, G4)].rearrange("p (c o) -> p c o", o=1).to_broadcast([128, G4, D])
                        nc.vector.tensor_tensor(g[:, u % 2], p_s[u % 2][:].rearrange("p (a b) -> p a b", a=G4), dis,
                                                ALU.mult).then_inc(s["dve_g"], 1)
                    stats(1)
                    if live(k, u, 0, AG):
                        wait(dve, s["summed"], (i - 1) * G4)
                        self.select_group(m[:, u % 2], k, u, 0).then_inc(s["dve_m"], 1)
                    stats(2)
                    if live(k, u, 5, AG):
                        w = (u - 5) % UN
                        dve.wait_ge(s["act_rs"], i - 4)
                        self.norm_shift(mv[:, w], rs[:, w], nb[:, w]).then_inc(s["dve_nb"], 1)
                    stats(3)

                steps(dve, AG, 8, step, 3)

    def phase_gat_nodes(self, layer):
        nc = self.nc
        last_layer = layer == 2
        ctx, sb, ps, sem = self.scope(f"n{layer}")
        with ctx:
            h = sb("h", [128, UN, G4, XW]); n_ = sb("n", [128, 2, G4, D])
            st = sb("st", [128, G4, 6]); mv = sb("mv", [128, UN, G4, 2])
            inv = sb("inv", [128, UN, G4]); rs = sb("rs", [128, UN, G4]); nb = sb("nb", [128, UN, G4])
            arrived = [sem(f"arrived{u}") for u in range(UN)]
            outs = [sem(f"outs{u}") for u in range(UN)]
            got = sem("got")
            names = ["dve_inv", "act_rs", "dve_nb", "act_n", "link"]
            if last_layer:
                x3 = sb("x3", [128, UN, G4, D]); y = sb("y", [128, UN, G4, D]); res = sb("res", [128, UN, G4, D])
                st2 = sb("st2", [128, G4, 6]); mv2 = sb("mv2", [128, UN, G4, 2])
                inv2 = sb("inv2", [128, UN, G4]); rs2 = sb("rs2", [128, UN, G4]); nb2 = sb("nb2", [128, UN, G4])
                arrivedx = [sem(f"arrivedx{u}") for u in range(UN)]
                names += ["pool_z", "dve_y", "dve_inv2", "act_rs2", "dve_nb2", "act_res", "link2"]
            else:
                nt = sb("nt", [D, 2, GN]); hn = sb("hn", [128, UN, G4, XW])
                p_t = ps("p_t", (128, 2, 512)); p_h = ps("p_h", (128, 2, 2, 512))
                names += ["pe_t", "act_t", "pe_h", "dve_h"]
            s = {name: sem(name) for name in names}
            last_rows = (N - (DG - 1) * GN) // G4
            block = ctx.enter_context(nc.Block())

            @block.gpsimd
            def _(pool):
                if last_layer:
                    for n in range(DG):
                        self.resident_gather(self.row_i, self.th[layer], XW, got, range(2 * n, 2 * n + 2))
                        pool.wait_ge(arrivedx[n % UN], 16 * (n // UN + 1))
                        nc.gpsimd.tensor_tensor(x3[:, n % UN], x3[:, n % UN], self.each(self.bet[:]), ALU.add).then_inc(s["pool_z"], 1)
                self.resident_gather(self.row_i, self.th[layer], XW, got, range(2 * DG if last_layer else 0, CHUNKS))
                pool.wait_ge(got, 16 * CHUNKS)

            @block.sync
            def _(sp):
                def step(k, u):
                    i = UN * k + u
                    if live(k, u, 0, DG):
                        wait(sp, s["act_n"], i - UN + 1)
                        sp.dma_start(h[:, u], self.nodes(self.th[layer], k, u)).then_inc(arrived[u], 16)
                    if live(k, u, 1, DG) and last_layer:
                        w = (u - 1) % UN
                        wait(sp, s["dve_y"], i - 1 - UN + 1)
                        sp.dma_start(x3[:, w], self.nodes(self.x3, k, u, 1)).then_inc(arrivedx[w], 16)
                    if live(k, u, 7, DG):
                        w = (u - 7) % UN
                        if not last_layer:
                            sp.wait_ge(s["dve_h"], i - 6)
                            sp.dma_start(self.nodes(self.th[layer + 1], k, u, 7), hn[:, w]).then_inc(outs[w], 16)
                        else:
                            self.hold(sp, (s["act_res"], i - 6))
                            if isinstance(i, int) and i - 7 == DG - 1:
                                sp.dma_start(self.out[(DG - 1) * GN:N, :].rearrange("(p j) f -> p j f", j=G4),
                                             res[0:last_rows, w]).then_inc(outs[w], 16)
                            else:
                                t = self.out[0:(DG - 1) * GN, :].rearrange("(g p j) f -> g p j f", p=128, j=G4)
                                sp.dma_start(t[bass.ds(i - 7, 1)].rearrange("g p j f -> p (g j) f"), res[:, w]).then_inc(outs[w], 16)

                steps(sp, DG, 7, step, 2)
                self.all_stored(sp, outs, DG)

            if not last_layer:
                @block.tensor
                def _(pe):
                    def step(k, u):
                        i = UN * k + u
                        if live(k, u, 3, DG):
                            w = (u - 3) % 2
                            pe.wait_ge(s["act_n"], i - 2)
                            wait(pe, s["act_t"], i - 4)
                            for j in range(G4):
                                t = nc.tensor.transpose(p_t[:, w, j * D:(j + 1) * D], n_[:, w, j, :], self.ident[:])
                            t.then_inc(s["pe_t"], 1)
                        if live(k, u, 4, DG):
                            w = u % 2
                            pe.wait_ge(s["act_t"], i - 3)
                            wait(pe, s["dve_h"], i - 5)
                            self.gat_rows(nt[:, w], p_h[:, w], layer + 1).then_inc(s["pe_h"], 1)

                    steps(pe, DG, 4, step, 2)

            @block.scalar
            def _(act):
                def step(k, u):
                    i = UN * k + u
                    if live(k, u, 1, DG):
                        w = (u - 1) % UN
                        act.wait_ge(s["dve_inv"], i)
                        nc.scalar.activation(rs[:, w], inv[:, w], ACT.Sqrt).then_inc(s["act_rs"], 1)
                    if live(k, u, 4, DG) and last_layer:
                        act.wait_ge(s["dve_inv2"], i - 3)
                        nc.scalar.activation(rs2[:, u], inv2[:, u], ACT.Sqrt).then_inc(s["act_rs2"], 1)
                    if live(k, u, 2, DG):
                        w = (u - 2) % UN
                        act.wait_ge(s["dve_nb"], i - 1)
                        wait(act, s["dve_y"] if last_layer else s["pe_t"], i - 3)
                        self.norm_apply(n_[:, w % 2], h[:, w, :, 0:D], rs[:, w], nb[:, w]).then_inc(s["act_n"], 1)
                    if live(k, u, 3, DG) and not last_layer:
                        w = (u - 3) % 2
                        act.wait_ge(s["pe_t"], i - 2)
                        wait(act, s["pe_h"], i - 4)
                        nc.scalar.activation(nt[:, w], p_t[:, w], ACT.Copy).then_inc(s["act_t"], 1)
                    if live(k, u, 5, DG) and last_layer:
                        w = (u - 5) % UN
                        act.wait_ge(s["dve_nb2"], i - 4)
                        self.stored(act, outs, k, u, 5)
                        self.norm_apply(res[:, w], y[:, w], rs2[:, w], nb2[:, w]).then_inc(s["act_res"], 1)

                steps(act, DG, 5, step, 3)

            @block.vector
            def _(dve):
                link = Chain(dve, s["link"], 3)
                link2 = Chain(dve, s["link2"], 4) if last_layer else None

                def step(k, u):
                    i = UN * k + u

                    def rows_out(half):
                        if live(k, u, 5, DG) and not last_layer:
                            w = (u - 5) % UN
                            if half == 0:
                                dve.wait_ge(s["pe_h"], i - 4)
                                self.stored(dve, outs, k, u, 5)
                            last = self.gat_rows_out(hn[:, w], p_h[:, w % 2], layer + 1, half=(half,))
                            if half == 1:
                                last.then_inc(s["dve_h"], 1)

                    def shift():
                        if live(k, u, 1, DG):
                            w = (u - 1) % UN
                            dve.wait_ge(s["act_rs"], i)
                            self.norm_shift(mv[:, w], rs[:, w], nb[:, w]).then_inc(s["dve_nb"], 1)
                        if live(k, u, 4, DG) and last_layer:
                            dve.wait_ge(s["act_rs2"], i - 3)
                            self.norm_shift(mv2[:, u], rs2[:, u], nb2[:, u]).then_inc(s["dve_nb2"], 1)

                    def node(part):
                        if live(k, u, 0, DG):
                            if part == 0:
                                link.group(i)
                                dve.wait_ge(arrived[u], 16 * (k + 1))
                            last = self.norm_part(part, lambda j: h[:, u, j, 0:D], st, mv[:, u], inv[:, u], link)
                            if part == 3:
                                last.then_inc(s["dve_inv"], 1)

                    def result(part):
                        if not (last_layer and live(k, u, 3, DG)):
                            return
                        w = (u - 3) % UN
                        if part == 0:
                            link2.group(i - 3)
                            dve.wait_ge(s["act_n"], i - 2)
                            wait(dve, s["act_res"], i - 6)
                            link2.put(nc.vector.tensor_tensor(y[:, w], n_[:, w % 2], self.each(self.gam[:]), ALU.mult))
                        elif part == 1:
                            link2.last()
                            dve.wait_ge(s["pool_z"], i - 2)
                            nc.vector.tensor_tensor(y[:, w], y[:, w], x3[:, w], ALU.add).then_inc(s["dve_y"], 1)
                        elif part == 2:
                            dve.wait_ge(s["dve_y"], i - 2)
                        last = self.norm_part(part - 2, lambda j: y[:, w, j, :], st2, mv2[:, w], inv2[:, w], link2) if part > 1 else None
                        if part == 5:
                            last.then_inc(s["dve_inv2"], 1)

                    result(0)
                    rows_out(0)
                    node(0)
                    result(1)
                    rows_out(1)
                    node(1)
                    result(2)
                    node(2)
                    shift()
                    result(3)
                    node(3)
                    result(4)
                    result(5)

                steps(dve, DG, 5, step, 3)

    def phase_gat_weights(self, layer):
        nc = self.nc
        ctx, sb, ps, sem = self.scope(f"s{layer}")
        with ctx:
            own = sb("own", [128, CHUNKS]); col = sb("col", [ROWP, 3, 256])
            b = sb("b", [ROWP, 256]); mx = sb("mx", [ROWP, 256]); z = sb("z", [ROWP, 256])
            tmp = sb("tmp", [ROWP, 2, 256]); fill = sb("fill", [ROWP, 2, 256]); ex = sb("ex", [ROWP, 2, 256])
            edge1 = sb("edge1", [1, ROWP]); run1 = sb("run1", [1, ROWP + 1]); in1 = sb("in1", [ROWP, 1])
            edge2 = sb("edge2", [1, 2, ROWP]); run2 = sb("run2", [1, 2, ROWP + 1]); in2 = sb("in2", [ROWP, 2])
            one = sb("one", [1, 1])
            p_c = ps("p_c", (128, 3, 512)); p_1 = ps("p_1"); p_2 = ps("p_2"); p_w = ps("p_w", (128, 2, 512))
            v, own_done, cols_in, last1, row1, run1_done, first2, back2, exp_in, exp_out, wide = (
                sem(n) for n in ("v", "own_done", "cols_in", "last1", "row1", "run1_done", "first2", "back2",
                                 "exp_in", "exp_out", "wide"))
            pe_last, pe_in1, pe_first, pe_in2 = (sem(n) for n in ("pe_last", "pe_in1", "pe_first", "pe_in2"))
            idp = self.ident[0:ROWP, 0:ROWP]
            block = ctx.enter_context(nc.Block())

            @block.tensor
            def _(pe):
                pe.wait_ge(own_done, 1)
                for n, t in enumerate((self.msgs[:, :, D], self.att_s[:, :, 2], own[:])):
                    for j in range(2):
                        last = nc.tensor.transpose(p_c[0:ROWP, n, j * 128:(j + 1) * 128],
                                                   t.rearrange("q (p j) -> q j p", j=2)[:, j, :], self.ident[:])
                last.then_inc(cols_in, 1)
                pe.wait_ge(last1, 1)
                nc.tensor.transpose(p_1[0:1, 0:ROWP], mx[:, 255:256], idp).then_inc(pe_last, 1)
                pe.wait_ge(run1_done, 1)
                nc.tensor.matmul(p_2[0:ROWP, 0:1], run1[0:1, 0:ROWP], one[:], start=True, stop=True).then_inc(pe_in1, 1)
                pe.wait_ge(first2, 1)
                for n in range(2):
                    last = nc.tensor.transpose(p_1[0:1, n * 128:n * 128 + ROWP], fill[:, n, 0:1], idp)
                last.then_inc(pe_first, 1)
                pe.wait_ge(back2, 1)
                for n in range(2):
                    last = nc.tensor.matmul(p_2[0:ROWP, n:n + 1], run2[0:1, n, 1:ROWP + 1], one[:], start=True, stop=True)
                last.then_inc(pe_in2, 1)
                pe.wait_ge(exp_out, 1)
                for n in range(2):
                    for j in range(2):
                        last = nc.tensor.transpose(p_w[:, n, j * ROWP:(j + 1) * ROWP], ex[:, n, j * 128:(j + 1) * 128], idp)
                last.then_inc(wide, 1)

            @block.scalar
            def _(act):
                act.wait_ge(exp_in, 1)
                nc.scalar.activation(ex[:], tmp[:], ACT.Exp).then_inc(exp_out, 1)

            @block.vector
            def _(dve):
                count = [0]

                def after(ins):
                    count[0] += 1
                    ins.then_inc(v, 1)
                    dve.wait_ge(v, count[0])

                def leaky(out, x, t):
                    after(nc.vector.tensor_scalar(t, x, 0.2, None, ALU.mult))
                    after(nc.vector.tensor_tensor(out, x, t, ALU.max))

                nc.vector.memset(one[:], 1.0).then_inc(v, 1)
                nc.vector.memset(run1[:], -BIG).then_inc(v, 1)
                nc.vector.memset(run2[:], 0.0).then_inc(v, 1)
                count[0] += 3
                after(nc.vector.tensor_tensor(own[:], self.att_s[:, :, 0], self.att_s[:, :, 2], ALU.add))
                nc.vector.tensor_tensor(own[:], own[:], self.deg[:, :, 1 + layer], ALU.add).then_inc(own_done, 1)
                dve.wait_ge(cols_in, 1)
                after(nc.vector.tensor_copy(col[:], p_c[0:ROWP, :, 0:256]))
                after(nc.vector.tensor_tensor(b[:], col[:, 0], self.edge_t[:, layer], ALU.add))
                nc.vector.tensor_tensor_scan(mx[:], self.startneg[:], b[:], -BIG, ALU.add, ALU.max).then_inc(last1, 1)
                dve.wait_ge(pe_last, 1)
                after(nc.vector.tensor_copy(edge1[:], p_1[0:1, 0:ROWP]))
                nc.vector.tensor_tensor_scan(run1[:, 1:ROWP + 1], self.flag_rows[:, 0, :], edge1[:], -BIG,
                                             ALU.add, ALU.max).then_inc(run1_done, 1)
                dve.wait_ge(pe_in1, 1)
                after(nc.vector.tensor_copy(in1[:], p_2[0:ROWP, 0:1]))
                after(nc.vector.scalar_tensor_tensor(out=mx[:], in0=self.preneg[:], scalar=in1[:], in1=mx[:],
                                                     op0=ALU.add, op1=ALU.max))
                after(nc.vector.tensor_tensor(mx[:], mx[:], col[:, 1], ALU.add))
                after(nc.vector.tensor_tensor(mx[:], mx[:], col[:, 2], ALU.max))
                leaky(z[:], mx[:], tmp[:, 0])
                after(nc.vector.tensor_tensor(tmp[:, 0], z[:], self.end[:], ALU.mult))
                after(nc.vector.tensor_tensor(tmp[:, 1], col[:, 1], self.end[:], ALU.mult))
                for n in range(2):
                    last = nc.vector.tensor_tensor_scan(fill[:, n, ::-1], self.notend[:, ::-1], tmp[:, n, ::-1], 0.0,
                                                        ALU.mult, ALU.add)
                last.then_inc(first2, 1)
                dve.wait_ge(pe_first, 1)
                after(nc.vector.tensor_copy(edge2[:], p_1[0:1, 0:256].rearrange("o (n p) -> o n p", n=2)[:, :, 0:ROWP]))
                for n in range(2):
                    last = nc.vector.tensor_tensor_scan(run2[:, n, 0:ROWP][:, ::-1], self.flag_rows[:, 1, ::-1],
                                                        edge2[:, n, ::-1], 0.0, ALU.mult, ALU.add)
                last.then_inc(back2, 1)
                dve.wait_ge(pe_in2, 1)
                after(nc.vector.tensor_copy(in2[:], p_2[0:ROWP, 0:2]))
                for n in range(2):
                    last = nc.vector.scalar_tensor_tensor(out=fill[:, n], in0=self.open[:], scalar=in2[:, n:n + 1],
                                                          in1=fill[:, n], op0=ALU.mult, op1=ALU.add)
                after(last)
                after(nc.vector.tensor_tensor(b[:], b[:], fill[:, 1], ALU.add))
                leaky(b[:], b[:], tmp[:, 0])
                leaky(col[:, 2], col[:, 2], tmp[:, 1])
                after(nc.vector.tensor_tensor(tmp[:, 0], b[:], fill[:, 0], ALU.subtract))
                nc.vector.tensor_tensor(tmp[:, 1], col[:, 2], z[:], ALU.subtract).then_inc(exp_in, 1)
                dve.wait_ge(wide, 1)
                for n, t in enumerate((self.w_edge, self.w_self)):
                    last = nc.vector.tensor_copy(t[:].rearrange("q (p j) -> q j p", j=2),
                                                 p_w[:, n, 0:CHUNKS].rearrange("q (j p) -> q j p", j=2))
                after(last)
                after(nc.vector.memset(self.w_edge[0:1, :], 1.0))

    def phase_gat_sums(self, layer):
        nc = self.nc
        last_layer = layer == 2
        ctx, sb, ps, sem = self.scope(f"a{layer}")
        with ctx:
            h = sb("h", [128, UN, G4, XW]); m = sb("m", [128, 2, G4, 128])
            t_ = sb("t", [128, UN, G4, XW]); den = sb("den", [128, G4])
            n_ = sb("n", [128, 2, G4, D])
            st = sb("st", [128, G4, 6]); mv = sb("mv", [128, UN, G4, 2])
            inv = sb("inv", [128, UN, G4]); rs = sb("rs", [128, UN, G4]); nb = sb("nb", [128, UN, G4])
            p_s = ps("p_s", (128, 2, 2, 512))
            arrived = [sem(f"arrived{u}") for u in range(UN)]
            outs = [sem(f"outs{u}") for u in range(UN)]
            names = ["dve_m", "summed", "carried", "dve_t", "dve_inv", "act_rs", "dve_nb", "act_n", "link"]
            if last_layer:
                x3 = sb("x3", [128, UN, G4, D]); y = sb("y", [128, UN, G4, D]); res = sb("res", [128, UN, G4, D])
                st2 = sb("st2", [128, G4, 6]); mv2 = sb("mv2", [128, UN, G4, 2])
                inv2 = sb("inv2", [128, UN, G4]); rs2 = sb("rs2", [128, UN, G4]); nb2 = sb("nb2", [128, UN, G4])
                stage = sb("stage", [128, UN, G4], I32)
                arrivedx = [sem(f"arrivedx{u}") for u in range(UN)]
                names += ["pool_z", "dve_y", "dve_inv2", "act_rs2", "dve_nb2", "act_res", "link2", "staged"]
            else:
                nt = sb("nt", [D, 2, GN]); hn = sb("hn", [128, UN, G4, XW])
                p_t = ps("p_t"); p_h = ps("p_h", (128, 2, 512))
                names += ["pe_t", "act_t", "pe_h", "dve_h"]
            s = {name: sem(name) for name in names}
            place = lambda w, j: (w, j // 2, slice((j % 2) * XW, (j % 2 + 1) * XW))
            msg = lambda c: self.msgs[:, bass.ds(c, 1), :].rearrange("p o f -> p (o f)")
            block = ctx.enter_context(nc.Block())

            @block.sync
            def _(sp):
                def step(k, u):
                    i = UN * k + u
                    if live(k, u, 0, AG):
                        wait(sp, s["dve_t"], i - UN + 1)
                        sp.dma_start(h[:, u], self.slots(self.th[layer], k, u)).then_inc(arrived[u], 16)
                    if live(k, u, 2, AG) and last_layer:
                        wait(sp, s["dve_y"], i - 2 - UN + 1)
                        sp.dma_start(x3[:, (u - 2) % UN], self.slots(self.x3, k, u, 2)).then_inc(arrivedx[(u - 2) % UN], 16)
                    if live(k, u, 8, AG) and not last_layer:
                        sp.wait_ge(s["dve_h"], i - 7)
                        sp.dma_start(self.slots(self.th[layer + 1], k, u, 8), hn[:, u]).then_inc(outs[u], 16)

                steps(sp, AG, 8, step, 3)
                if not last_layer:
                    self.all_stored(sp, outs, AG)

            if last_layer:
                @block.gpsimd
                def _(pool):
                    def step(k, u):
                        i = UN * k + u
                        if live(k, u, 3, AG):
                            w = (u - 3) % UN
                            pool.wait_ge(arrivedx[w], 16 * (k + (u - 3) // UN + 1))
                            nc.gpsimd.tensor_tensor(x3[:, w], x3[:, w], self.each(self.bet[:]), ALU.add).then_inc(s["pool_z"], 1)
                        if live(k, u, 8, AG):
                            n = i - 8
                            self.stored_rows(pool, outs[u], k - 2)
                            nc.gpsimd.tensor_copy(stage[:, u, :], self.own_i[:, bass.ds(n * G4, G4)]).then_inc(s["staged"], 1)
                            self.hold(pool, (s["staged"], n + 1), (s["act_res"], n + 1))
                            for j in range(G4):
                                nc.gpsimd.indirect_dma_start(
                                    out=self.out, out_offset=bass.IndirectOffsetOnAxis(ap=stage[:, u, j:j + 1], axis=0),
                                    in_=res[:, u, j, :], in_offset=None, bounds_check=N - 1,
                                    oob_is_err=False).then_inc(outs[u], 16)

                    steps(pool, AG, 8, step, 3)
                    for w in range(UN):
                        pool.wait_ge(outs[w], 16 * G4 * ((AG - w + UN - 1) // UN))

            @block.tensor
            def _(pe):
                def step(k, u):
                    i = UN * k + u

                    def sums(j):
                        if live(k, u, 1, AG):
                            w = (u - 1) % 2
                            if j == 0:
                                pe.wait_ge(s["dve_m"], i)
                                wait(pe, s["dve_t"], i - 2)
                            a_, b_, c_ = place(w, j)
                            self.sum_chunk(pe, i - 1, j, p_s[:, a_, b_, c_], m[:, w], msg((i - 1) * G4 + j),
                                           s["carried"], s["summed"])

                    def turn(tiles):
                        if live(k, u, 5, AG) and not last_layer:
                            w = (u - 5) % 2
                            if tiles[0] == 0:
                                pe.wait_ge(s["act_n"], i - 4)
                                wait(pe, s["act_t"], i - 5)
                            for j in tiles:
                                t = nc.tensor.transpose(p_t[:, j * D:(j + 1) * D], n_[:, w, j, :], self.ident[:])
                            if tiles[-1] == G4 - 1:
                                t.then_inc(s["pe_t"], 1)

                    def product(tiles):
                        if live(k, u, 6, AG) and not last_layer:
                            if tiles[0] == 0:
                                pe.wait_ge(s["act_t"], i - 5)
                                wait(pe, s["dve_h"], i - 6)
                            last = self.gat_rows(nt[:, u % 2], p_h, layer + 1, tiles)
                            if tiles[-1] == G4 - 1:
                                last.then_inc(s["pe_h"], 1)

                    sums(0)
                    turn((0, 1))
                    sums(1)
                    turn((2, 3))
                    sums(2)
                    product((0,))
                    sums(3)
                    product((1, 2, 3))

                steps(pe, AG, 6, step, 3)

            @block.scalar
            def _(act):
                def step(k, u):
                    i = UN * k + u

                    def carry(j):
                        if live(k, u, 1, AG):
                            if isinstance(i, int) and j == G4 and i == AG:
                                return
                            a_, b_, c_ = place((u - 1) % 2, j - 1)
                            row0 = self.msgs[0:1, bass.ds((i - 1) * G4 + j, 1), :].rearrange("p o f -> p (o f)")
                            self.carry_chunk(act, i - 1, j, row0, p_s[0:1, a_, b_, c_], s["carried"], s["summed"])

                    def norm(j):
                        if live(k, u, 4, AG):
                            if j == 0:
                                act.wait_ge(s["dve_nb"], i - 3)
                                wait(act, s["dve_y"] if last_layer else s["pe_t"], i - 5)
                            last = self.norm_apply(n_[:, u % 2], t_[:, u, :, 0:D], rs[:, u], nb[:, u], (j,))
                            if j == G4 - 1:
                                last.then_inc(s["act_n"], 1)

                    def norm2(j):
                        if live(k, u, 7, AG) and last_layer:
                            w = (u - 7) % UN
                            if j == 0:
                                act.wait_ge(s["dve_nb2"], i - 6)
                                self.stored_rows(act, outs[w], k + (u - 7) // UN)
                            last = self.norm_apply(res[:, w], y[:, w], rs2[:, w], nb2[:, w], (j,))
                            if j == G4 - 1:
                                last.then_inc(s["act_res"], 1)

                    if live(k, u, 3, AG):
                        w = (u - 3) % UN
                        act.wait_ge(s["dve_inv"], i - 2)
                        nc.scalar.activation(rs[:, w], inv[:, w], ACT.Sqrt).then_inc(s["act_rs"], 1)
                    if live(k, u, 6, AG) and last_layer:
                        w = (u - 6) % UN
                        act.wait_ge(s["dve_inv2"], i - 5)
                        nc.scalar.activation(rs2[:, w], inv2[:, w], ACT.Sqrt).then_inc(s["act_rs2"], 1)
                    for j in range(G4):
                        carry(j + 1)
                        norm(j)
                        norm2(j)
                    if live(k, u, 5, AG) and not last_layer:
                        act.wait_ge(s["pe_t"], i - 4)
                        wait(act, s["pe_h"], i - 6)
                        nc.scalar.activation(nt[:, (u - 5) % 2], p_t[:], ACT.Copy).then_inc(s["act_t"], 1)

                steps(act, AG, 7, step, 3)

            @block.vector
            def _(dve):
                link = Chain(dve, s["link"], 5)
                link2 = Chain(dve, s["link2"], 4) if last_layer else None

                def step(k, u):
                    i = UN * k + u
                    v, y_ = (u - 2) % UN, (u - 5) % UN

                    def select(tiles):
                        if live(k, u, 0, AG):
                            if tiles[0] == 0:
                                wait(dve, s["summed"], (i - 1) * G4)
                            last = self.select_group(m[:, u % 2], k, u, 0, self.w_edge, tiles)
                            if tiles[-1] == G4 - 1:
                                last.then_inc(s["dve_m"], 1)

                    def node(part):
                        if not live(k, u, 2, AG):
                            return
                        if part == 0:
                            link.group(i - 2)
                            self.wait_sums(dve, i - 2, s["carried"], s["summed"])
                            dve.wait_ge(arrived[v], 16 * (k + (u - 2) // UN + 1))
                            wait(dve, s["act_n"], i - 2 - UN + 1)
                            for j in range(G4):
                                a_, b_, c_ = place(u % 2, j)
                                last = nc.vector.scalar_tensor_tensor(
                                    out=t_[:, v, j, :], in0=h[:, v, j, :], scalar=self.w_self[:, bass.ds((i - 2) * G4 + j, 1)],
                                    in1=p_s[:, a_, b_, c_], op0=ALU.mult, op1=ALU.add)
                            last.then_inc(s["dve_t"], 1)
                        elif part == 1:
                            dve.wait_ge(s["dve_t"], i - 1)
                            self.norm_part(0, lambda j: t_[:, v, j, 0:D], st, mv[:, v], inv[:, v], link)
                            link.put(nc.vector.tensor_tensor(den[:], t_[:, v, :, D + 1], t_[:, v, :, D + 1], ALU.mult))
                        elif part == 2:
                            link.last()
                            link.put(nc.vector.tensor_scalar(den[:], den[:], 1e-30, EPS, ALU.max, ALU.mult))
                        elif part == 3:
                            self.norm_part(1, None, st, mv[:, v], inv[:, v], link)
                        elif part == 4:
                            link.last()
                            link.put(nc.vector.tensor_tensor(inv[:, v], mv[:, v, :, 1], den[:], ALU.add))
                        else:
                            self.norm_part(3, None, st, mv[:, v], inv[:, v], link).then_inc(s["dve_inv"], 1)

                    def rest(part):
                        if last_layer and live(k, u, 5, AG):
                            if part == 0:
                                link2.group(i - 5)
                                dve.wait_ge(s["act_n"], i - 4)
                                wait(dve, s["act_res"], i - 8)
                                link2.put(nc.vector.tensor_tensor(y[:, y_], n_[:, y_ % 2], self.each(self.gam[:]), ALU.mult))
                            elif part == 1:
                                link2.last()
                                dve.wait_ge(s["pool_z"], i - 4)
                                nc.vector.tensor_tensor(y[:, y_], y[:, y_], x3[:, y_], ALU.add).then_inc(s["dve_y"], 1)
                            elif part == 2:
                                dve.wait_ge(s["dve_y"], i - 4)
                                self.norm_part(0, lambda j: y[:, y_, j, :], st2, mv2[:, y_], inv2[:, y_], link2)
                            elif part < 5:
                                self.norm_part(part - 2, None, st2, mv2[:, y_], inv2[:, y_], link2)
                            else:
                                self.norm_part(3, None, st2, mv2[:, y_], inv2[:, y_], link2).then_inc(s["dve_inv2"], 1)
                        if not last_layer and live(k, u, 7, AG) and part < 2:
                            w = (u - 7) % UN
                            if part == 0:
                                dve.wait_ge(s["pe_h"], i - 6)
                                self.stored(dve, outs, k, u, 7)
                            last = self.gat_rows_out(hn[:, w], p_h, layer + 1, i - 7, (part,))
                            if part == 1:
                                last.then_inc(s["dve_h"], 1)

                    def shift():
                        if live(k, u, 3, AG):
                            w = (u - 3) % UN
                            dve.wait_ge(s["act_rs"], i - 2)
                            self.norm_shift(mv[:, w], rs[:, w], nb[:, w]).then_inc(s["dve_nb"], 1)
                        if live(k, u, 6, AG) and last_layer:
                            w = (u - 6) % UN
                            dve.wait_ge(s["act_rs2"], i - 5)
                            self.norm_shift(mv2[:, w], rs2[:, w], nb2[:, w]).then_inc(s["dve_nb2"], 1)

                    rest(0)
                    if last_layer:
                        node(0)
                    rest(1)
                    if not last_layer:
                        node(0)
                    node(1)
                    select((0, 1))
                    node(2)
                    rest(2)
                    node(3)
                    select((2, 3))
                    node(4)
                    shift()
                    rest(3)
                    node(5)
                    rest(4)
                    rest(5)

                steps(dve, AG, 7, step, 3)


def resnorm_gnn(nc, args, out):
    net = Net(nc, args, out)
    with ExitStack() as ctx:
        net.allocate(ctx)
        net.phase_weights()
        net.phase_segments()
        net.phase_terms()
        net.phase_dense()
        net.phase_gin1()
        net.phase_gin2()
        net.phase_rgcn()
        net.phase_gcn()
        for layer in range(3):
            net.phase_gat_nodes(layer)
            net.phase_gat_weights(layer)
            net.phase_gat_sums(layer)


_INS = ["x", "src", "dst", "edge_attr_128", "edge_type_8", "edge_weight", "L0_gnn_w1a", "L0_gnn_b1a",
        "L0_gnn_w1b", "L0_gnn_b1b", "L0_gnn_w2a", "L0_gnn_b2a", "L0_gnn_w2b", "L0_gnn_b2b", "L0_gnn_wl",
        "L0_gnn_bl", "L1_gnn_bases", "L1_gnn_w_comp", "L2_gnn_W", "L2_gnn_bias", "L3_gnn_W",
        "L3_gnn_att_src", "L3_gnn_att_dst", "L3_gnn_W_e", "L3_gnn_att_edge", "L3_gnn_bias",
        "L3_gnn_ln_gamma", "L3_gnn_ln_beta"]


def kernel(**inputs):
    import concourse.bacc as bacc
    from concourse.bass_utils import run_bass_kernel_spmd

    nc = bacc.Bacc("TRN2", target_bir_lowering=False, num_devices=1)
    arrays, args = {}, {}
    for name in _INS:
        a = np.ascontiguousarray(inputs[name])
        arrays[f"in_{name}"] = a
        args[name] = nc.dram_tensor(f"in_{name}", a.shape, mybir.dt.from_np(a.dtype), kind="ExternalInput").ap()
    out = nc.dram_tensor("out_rows", (N, D), F32, kind="ExternalOutput").ap()
    resnorm_gnn(nc, args, out)
    r = run_bass_kernel_spmd(nc, [arrays], core_ids=[0])
    return r.results[0]["out_rows"]
```
